# Optimizing a Trainium2 kernel written in Bass

```python
import numpy as np
import jax
import jax.numpy as jnp

def _softmax(x, axis=-1):
    return jax.nn.softmax(x, axis=axis)

def _gelu(x):
    return jax.nn.gelu(x, approximate=True)

def _silu(x):
    return jax.nn.silu(x)

def _sigmoid(x):
    return jax.nn.sigmoid(x)

def _layernorm(x, axis=-1, eps=1e-05):
    m = jnp.mean(x, axis=axis, keepdims=True)
    v = jnp.var(x, axis=axis, keepdims=True)
    return (x - m) / jnp.sqrt(v + eps)

def _scatter_add(tgt, idx, src, axis=0):
    return tgt.at[idx].add(src)

def _segment_sum(src, seg, n):
    return jax.ops.segment_sum(src, seg, n)
kernel_name = 'mk_flamingo_gated_d2_seqx_r8_2f57c0'

def setup_inputs(seed: int=0):
    np.random.seed(seed)
    _w = jnp.asarray

    def _rec_inputs():
        import jax
        import jax.numpy as jnp
        _rk = jax.random.key(seed)
        x = -0.0003929 + 0.9999 * jax.random.normal(jax.random.fold_in(_rk, 1), (32, 64, 256), jnp.float32)
        _lenS = 64 - jax.random.randint(jax.random.fold_in(_rk, 7), (32,), 0, max(1, 64 // 4) + 1, jnp.int32)
        _lenS2 = 64 - jax.random.randint(jax.random.fold_in(_rk, 8), (32,), 0, max(1, 64 // 4) + 1, jnp.int32)
        _ctx_2048P = jax.random.normal(jax.random.fold_in(_rk, 11), (32, 16, 256), jnp.float32)
        _ctx_2048c = jax.random.dirichlet(jax.random.fold_in(_rk, 511), 0.3 * jnp.ones((16,), jnp.float32), (32, 64))
        _ctx_2048t = jnp.einsum('bsk,bkd->bsd', _ctx_2048c, _ctx_2048P)
        _ctx_2048t = _ctx_2048t * jax.lax.rsqrt(jnp.mean(jnp.square(_ctx_2048t)) + 1e-12) * 0.953939
        ctx_2048 = 2.81802e-05 + 1.00001 * (_ctx_2048t + 0.3 * jax.random.normal(jax.random.fold_in(_rk, 611), (32, 64, 256), jnp.float32))
        _g = jax.random.normal(jax.random.fold_in(_rk, 9001), (2, 2), jnp.float32)
        _g = jnp.sign(_g) * jnp.maximum(jnp.abs(_g), 1.0) + (_g == 0) * 1.0
        g_xattn = _g[0]
        g_ffn = _g[1]
        return (x, ctx_2048, g_xattn, g_ffn)
    x, ctx_2048, g_xattn, g_ffn = _rec_inputs()

    def _L0_xattn_setup():
        import jax, jax.numpy as jnp
        import numpy as np
        NUM_HEADS = 8

        def _proj(W, x):
            return jnp.einsum('oi,bin->bon', W, x)

        def _split_heads(x, h):
            B, D, N = x.shape
            return x.reshape(B, D, h, N // h).transpose(2, 0, 1, 3)

        def _mha(XQ, XK, XV, Wq, Wk, Wv, Wo):
            B, D, N = XQ.shape
            h = NUM_HEADS
            Nh = N // h
            q = _split_heads(_proj(Wq, XQ), h)
            k = _split_heads(_proj(Wk, XK), h)
            v = _split_heads(_proj(Wv, XV), h)
            scores = jnp.einsum('hbdn,hben->hbde', q, k) / jnp.sqrt(jnp.asarray(Nh, q.dtype))
            p = jax.nn.softmax(scores, axis=-1)
            out = jnp.einsum('hbde,hben->hbdn', p, v)
            attn_heads = out.transpose(1, 2, 0, 3).reshape(B, D, N)
            return _proj(Wo, XQ - attn_heads)
        key = jax.random.key(seed)
        ks = jax.random.split(key, 7)
        B, D, N = (16, 64, 256)
        sc = 1.0 / np.sqrt(D)
        return {'X_Query': jax.random.normal(ks[0], (B, D, N), jnp.float32), 'X_Key': jax.random.normal(ks[1], (B, D, N), jnp.float32), 'X_Value': jax.random.normal(ks[2], (B, D, N), jnp.float32), 'W_q': jax.random.normal(ks[3], (D, D), jnp.float32) * sc, 'W_k': jax.random.normal(ks[4], (D, D), jnp.float32) * sc, 'W_v': jax.random.normal(ks[5], (D, D), jnp.float32) * sc, 'W_o': jax.random.normal(ks[6], (D, D), jnp.float32) * sc}
    _L0_xattn_all = _L0_xattn_setup()
    _L0_xattn_in = {k: v for k, v in _L0_xattn_all.items() if k in ('W_q', 'W_k', 'W_v', 'W_o')}
    del _L0_xattn_all

    def _L0_ffn_setup():
        import jax, jax.numpy as jnp
        import numpy as np

        def _sparsify_2to4(h):
            B, S, I = h.shape
            g = h.reshape(B, S, I // 4, 4)
            a = jnp.abs(g)
            _, idx = jax.lax.top_k(a, 2)
            pos = jnp.arange(4)
            mask = (pos == idx[..., 0:1]) | (pos == idx[..., 1:2])
            return (g * mask.astype(g.dtype)).reshape(B, S, I)
        key = jax.random.key(seed)
        k1, k2, k3, k4 = jax.random.split(key, 4)
        B, S, H, I = (4, 256, 256, 1024)
        x = jax.random.normal(k1, (B, S, H), dtype=jnp.float32)
        w_gate = jax.random.normal(k2, (H, I), dtype=jnp.float32) / np.sqrt(H)
        w_up = jax.random.normal(k3, (H, I), dtype=jnp.float32) / np.sqrt(H)
        w_down = jax.random.normal(k4, (I, H), dtype=jnp.float32) / np.sqrt(I)
        return {'x': x, 'w_gate': w_gate, 'w_up': w_up, 'w_down': w_down}
    _L0_ffn_all = _L0_ffn_setup()
    _L0_ffn_in = {k: v for k, v in _L0_ffn_all.items() if k in ('w_gate', 'w_up', 'w_down')}
    del _L0_ffn_all

    def _L1_xattn_setup():
        import jax, jax.numpy as jnp
        import numpy as np
        N_HEAD = 8
        key = jax.random.key(seed)
        k1, k2, k3 = jax.random.split(key, 3)
        B, D, L = (4, 128, 256)
        q = jax.random.normal(k1, (B, D, L), dtype=jnp.float32)
        k = jax.random.normal(k2, (B, D, L), dtype=jnp.float32)
        v = jax.random.normal(k3, (B, D, L), dtype=jnp.float32)
        gamma = jnp.ones((), dtype=jnp.float32)
        return {'q': q, 'k': k, 'v': v, 'gamma': gamma}
    _L1_xattn_all = _L1_xattn_setup()
    _L1_xattn_in = {k: v for k, v in _L1_xattn_all.items() if k in ('gamma',)}
    del _L1_xattn_all

    def _L1_ffn_setup():
        import jax, jax.numpy as jnp
        import numpy as np
        E = 8
        TOP_K = 2
        D = 256
        DE = 176
        DS = 352
        B, S = (2, 256)
        key = jax.random.key(seed)
        ks = jax.random.split(key, 8)
        std = 0.02
        return {'x': jax.random.normal(ks[0], (B, S, D), jnp.float32), 'W_router': jax.random.normal(ks[1], (D, E), jnp.float32) * std, 'We_gate': jax.random.normal(ks[2], (E, D, DE), jnp.float32) * std, 'We_up': jax.random.normal(ks[3], (E, D, DE), jnp.float32) * std, 'We_down': jax.random.normal(ks[4], (E, DE, D), jnp.float32) * std, 'Ws_gate': jax.random.normal(ks[5], (D, DS), jnp.float32) * std, 'Ws_up': jax.random.normal(ks[6], (D, DS), jnp.float32) * std, 'Ws_down': jax.random.normal(ks[7], (DS, D), jnp.float32) * std}
    _L1_ffn_all = _L1_ffn_setup()
    _L1_ffn_in = {k: v for k, v in _L1_ffn_all.items() if k in ('W_router', 'We_gate', 'We_up', 'We_down', 'Ws_gate', 'Ws_up', 'Ws_down')}
    del _L1_ffn_all
    return {'x': x, 'ctx_2048': ctx_2048, 'g_xattn': g_xattn, 'g_ffn': g_ffn, 'L0_xattn_W_q': _L0_xattn_in['W_q'], 'L0_xattn_W_k': _L0_xattn_in['W_k'], 'L0_xattn_W_v': _L0_xattn_in['W_v'], 'L0_xattn_W_o': _L0_xattn_in['W_o'], 'L0_ffn_w_gate': _L0_ffn_in['w_gate'], 'L0_ffn_w_up': _L0_ffn_in['w_up'], 'L0_ffn_w_down': _L0_ffn_in['w_down'], 'L1_xattn_gamma': _L1_xattn_in['gamma'], 'L1_ffn_W_router': _L1_ffn_in['W_router'], 'L1_ffn_We_gate': _L1_ffn_in['We_gate'], 'L1_ffn_We_up': _L1_ffn_in['We_up'], 'L1_ffn_We_down': _L1_ffn_in['We_down'], 'L1_ffn_Ws_gate': _L1_ffn_in['Ws_gate'], 'L1_ffn_Ws_up': _L1_ffn_in['Ws_up'], 'L1_ffn_Ws_down': _L1_ffn_in['Ws_down']}

def reference(x, ctx_2048, g_xattn, g_ffn, L0_xattn_W_q, L0_xattn_W_k, L0_xattn_W_v, L0_xattn_W_o, L0_ffn_w_gate, L0_ffn_w_up, L0_ffn_w_down, L1_xattn_gamma, L1_ffn_W_router, L1_ffn_We_gate, L1_ffn_We_up, L1_ffn_We_down, L1_ffn_Ws_gate, L1_ffn_Ws_up, L1_ffn_Ws_down):
    import jax
    import jax.numpy as jnp

    def _L0_xattn_ref(X_Query, X_Key, X_Value, W_q, W_k, W_v, W_o):
        import jax, jax.numpy as jnp
        import numpy as np
        NUM_HEADS = 8

        def _proj(W, x):
            return jnp.einsum('oi,bin->bon', W, x)

        def _split_heads(x, h):
            B, D, N = x.shape
            return x.reshape(B, D, h, N // h).transpose(2, 0, 1, 3)

        def _mha(XQ, XK, XV, Wq, Wk, Wv, Wo):
            B, D, N = XQ.shape
            h = NUM_HEADS
            Nh = N // h
            q = _split_heads(_proj(Wq, XQ), h)
            k = _split_heads(_proj(Wk, XK), h)
            v = _split_heads(_proj(Wv, XV), h)
            scores = jnp.einsum('hbdn,hben->hbde', q, k) / jnp.sqrt(jnp.asarray(Nh, q.dtype))
            p = jax.nn.softmax(scores, axis=-1)
            out = jnp.einsum('hbde,hben->hbdn', p, v)
            attn_heads = out.transpose(1, 2, 0, 3).reshape(B, D, N)
            return _proj(Wo, XQ - attn_heads)
        return _mha(X_Query, X_Key, X_Value, W_q, W_k, W_v, W_o)

    def _L0_ffn_ref(x, w_gate, w_up, w_down):
        import jax, jax.numpy as jnp
        import numpy as np

        def _sparsify_2to4(h):
            B, S, I = h.shape
            g = h.reshape(B, S, I // 4, 4)
            a = jnp.abs(g)
            _, idx = jax.lax.top_k(a, 2)
            pos = jnp.arange(4)
            mask = (pos == idx[..., 0:1]) | (pos == idx[..., 1:2])
            return (g * mask.astype(g.dtype)).reshape(B, S, I)
        h = jax.nn.silu(jnp.einsum('bsh,hi->bsi', x, w_gate)) * jnp.einsum('bsh,hi->bsi', x, w_up)
        h_sparse = _sparsify_2to4(h)
        return jnp.einsum('bsi,ih->bsh', h_sparse, w_down)

    def _L1_xattn_ref(q, k, v, gamma):
        import jax, jax.numpy as jnp
        import numpy as np
        N_HEAD = 8
        B, Dq, Lq = q.shape
        Dv, Lk = (v.shape[-2], v.shape[-1])
        h = N_HEAD
        dq = Dq // h
        dv = Dv // h
        qh = q.reshape(B, h, dq, Lq)
        kh = k.reshape(B, h, dq, Lk)
        vh = v.reshape(B, h, dv, Lk)
        scale = 1.0 / jnp.sqrt(jnp.asarray(dq, dtype=q.dtype))
        qk = jnp.einsum('bhdq,bhdl->bhql', qh, kh) * scale
        sm = jax.nn.softmax(qk, axis=-1)
        ret = jnp.einsum('bhql,bhdl->bhdq', sm, vh)
        ret = ret.reshape(B, Dv, Lq)
        return gamma * ret

    def _L1_ffn_ref(x, W_router, We_gate, We_up, We_down, Ws_gate, Ws_up, Ws_down):
        import jax, jax.numpy as jnp
        import numpy as np
        E = 8
        TOP_K = 2
        D = 256
        DE = 176
        DS = 352
        B, S = (2, 256)
        b, s, d = x.shape
        shared = jax.nn.silu(x @ Ws_gate) * (x @ Ws_up) @ Ws_down
        scores = jax.nn.softmax(x @ W_router, axis=-1)
        topk_vals, topk_idx = jax.lax.top_k(scores, TOP_K)
        onehot = jax.nn.one_hot(topk_idx, E, dtype=x.dtype)
        combine = jnp.einsum('bsk,bske->bse', topk_vals, onehot)
        combine = combine.reshape(b * s, E)
        xf = x.reshape(b * s, d)
        h = jax.nn.silu(jnp.einsum('td,edh->eth', xf, We_gate)) * jnp.einsum('td,edh->eth', xf, We_up)
        y_all = jnp.einsum('eth,ehd->etd', h, We_down)
        routed = jnp.einsum('etd,te->td', y_all, combine)
        return routed.reshape(b, s, d) + shared
    x = x + jnp.tanh(g_xattn[0]) * _L0_xattn_ref(_layernorm(x, axis=-1), ctx_2048, ctx_2048, L0_xattn_W_q, L0_xattn_W_k, L0_xattn_W_v, L0_xattn_W_o)
    x = x + jnp.tanh(g_ffn[0]) * _L0_ffn_ref(_layernorm(x, axis=-1), L0_ffn_w_gate, L0_ffn_w_up, L0_ffn_w_down)
    x = x + jnp.tanh(g_xattn[1]) * _L1_xattn_ref(_layernorm(x, axis=-1), ctx_2048, ctx_2048, L1_xattn_gamma)
    x = x + jnp.tanh(g_ffn[1]) * _L1_ffn_ref(_layernorm(x, axis=-1), L1_ffn_W_router, L1_ffn_We_gate, L1_ffn_We_up, L1_ffn_We_down, L1_ffn_Ws_gate, L1_ffn_Ws_up, L1_ffn_Ws_down)
    return x

_drawn_inputs = setup_inputs


def setup_inputs(seed=0):
    import zlib

    import numpy as np

    out = dict(_drawn_inputs(seed))
    spreads = {'g_ffn': (-1.0, 0.6)}
    factors = {'L1_ffn_W_router': 8.0,
     'L1_ffn_We_gate': 8.0,
     'L1_ffn_We_up': 8.0,
     'L1_ffn_We_down': 8.0,
     'L1_ffn_Ws_gate': 3.687,
     'L1_ffn_Ws_up': 3.653,
     'L1_ffn_Ws_down': 3.652}
    for name, (base, spread) in spreads.items():
        noise = np.random.default_rng([zlib.crc32(name.encode()), seed]).standard_normal(out[name].shape)
        drawn = base * np.exp(spread * noise) if base else spread * noise
        out[name] = jnp.asarray(drawn.astype(out[name].dtype))
    for name, factor in factors.items():
        out[name] = (out[name] * factor).astype(out[name].dtype)
    return out
```

```python
from contextlib import ExitStack

import concourse.bass as bass
from concourse import mybir

F32 = mybir.dt.float32
F32R = mybir.dt.float32r
BF16 = mybir.dt.bfloat16
ACT = mybir.ActivationFunctionType
ALU = mybir.AluOpType
AX_X = mybir.AxisListType.X

P = 128
BATCH, SEQ, D = 32, 64, 256
TOK = BATCH * SEQ
TILES = TOK // P
DC = D // P
EPS = 1e-5

H0 = 8
N0 = D // H0
SCALE0 = float(N0) ** -0.5

H1 = 8
D1 = SEQ // H1
SCALE1 = float(D1) ** -0.5
UNITS = P // D1
QUADS = UNITS // 4
UROWS = 32
MROW = 3 * D1

GT = 4
GN = GT * P
GROUPS = TILES // GT
XT = TILES + GT

I0 = 1024
QUAD0 = I0 // (4 * P)
E, DE, DS = 8, 176, 352
I1 = E * DE + DS
CH1 = -(-I1 // P)
CHR = E * DE // P
LASTM = I1 - (CH1 - 1) * P


class Step:

    def __init__(self, rnd, slot, unroll):
        self.rnd, self.slot, self.unroll = rnd, slot, unroll
        self.known = isinstance(rnd, int)
        self.n = rnd * unroll + slot

    def plus(self, k):
        q, slot = divmod(self.slot + k, self.unroll)
        return Step(self.rnd + q, slot, self.unroll)

    def inside(self, count):
        return not self.known or 0 <= self.n < count


def run_steps(eng, body, count, lag, unroll):
    head = -(-lag // unroll)
    tail = count // unroll
    for n in range(head * unroll):
        body(Step(n // unroll, n % unroll, unroll))
    with eng.Fori(head, tail) as r:
        for slot in range(unroll):
            body(Step(r, slot, unroll))
    for n in range(tail * unroll, count + lag):
        body(Step(n // unroll, n % unroll, unroll))


def after(eng, sem, step, per=1, k=None):
    if step.known and step.n < 0:
        return
    eng.wait_ge(sem, step.n * per + (per if k is None else k))


def after_dma(eng, sems, step, transfers=1):
    if step.known and step.rnd < 0:
        return
    eng.wait_ge(sems[step.slot], (step.rnd + 1) * (16 * transfers))


def at(tensor, n):
    if isinstance(n, int):
        return tensor[:, n]
    v = tensor[:, bass.ds(n, 1)]
    return v.rearrange("p o n -> p (o n)")


def dram_at(ap, n):
    if isinstance(n, int):
        return ap[n]
    return ap[bass.ds(n, 1)].rearrange("o p n -> (o p) n")


def raw(ap):
    return ap.bitcast(F32)


def product3(pe, out, lhs, rhs, first, last, **kw):
    (lh, ll), (rh, rl) = lhs, rhs
    pe.matmul(out, lhsT=lh, rhs=rh, start=first, stop=False, **kw)
    pe.matmul(out, lhsT=lh, rhs=rl, start=False, stop=False, **kw)
    return pe.matmul(out, lhsT=ll, rhs=rh, start=False, stop=last, **kw)


class Norm:

    def __init__(self, sb, sem):
        self.stats = sb("stats", [P, XT, 6], F32)
        self.sum2, self.dif, self.m2, self.sq, self.var, self.std, self.rstd, self.shift = (
            sb(f"ln_{n}", [P, XT], F32) for n in ("sum2", "dif", "m2", "sq", "var", "std", "rstd", "shift"))
        self.eps = sb("eps", [P, 1], F32)
        self.steps = sem("ln_steps")
        self.used = 0

    def vector(self, dve, scalar_part=False):
        st, n = self.stats, self.used
        even, odd = st[:, :, 1], st[:, :, 4]
        dve.tensor_tensor(self.sum2[:], even, odd, ALU.add)
        dve.tensor_tensor(self.dif[:], even, odd, ALU.subtract)
        dve.tensor_tensor(self.m2[:], st[:, :, 2], st[:, :, 5], ALU.add).then_inc(self.steps, 1)
        dve.wait_ge(self.steps, n + 1)
        dve.scalar_tensor_tensor(self.sq[:], self.dif[:], 0.25, self.dif[:], ALU.mult, ALU.mult).then_inc(self.steps, 1)
        dve.wait_ge(self.steps, n + 2)
        dve.scalar_tensor_tensor(self.var[:], self.m2[:], 1.0 / D, self.sq[:], ALU.mult, ALU.add).then_inc(self.steps, 1)
        dve.wait_ge(self.steps, n + 4)
        dve.reciprocal(self.rstd[:], self.std[:]).then_inc(self.steps, 1)
        dve.wait_ge(self.steps, n + 5)
        dve.scalar_tensor_tensor(self.shift[:], self.sum2[:], -0.5, self.rstd[:], ALU.mult, ALU.mult).then_inc(self.steps, 1)
        dve.wait_ge(self.steps, n + 6)

    def scalar(self, act):
        act.wait_ge(self.steps, self.used + 3)
        act.activation(self.std[:], self.var[:], ACT.Sqrt, bias=self.eps[:, 0:1]).then_inc(self.steps, 1)

    def apply(self, dve, out, x_all, n):
        return dve.tensor_scalar(out, at(x_all, n), column(self.rstd, n), column(self.shift, n), ALU.mult, ALU.add)


def column(tensor, n):
    return tensor[:, n:n + 1] if isinstance(n, int) else tensor[:, bass.ds(n, 1)]


def attention0(nc, sem, keep, d):
    x_all, norm, ident, gates = keep["x_all"], keep["norm"], keep["ident"], keep["gates"]
    sel_out, sel_den = keep["sel_out"], keep["sel_den"]
    with ExitStack() as ctx:
        def sb(name, shape, dt):
            return ctx.enter_context(nc.sbuf_tensor(name, shape, dt))

        banks = [ctx.enter_context(nc.psum_tensor(f"a0_bank{i}", [P, 512], F32)) for i in range(8)]
        qk_ps, v_ps, s_ps = banks[0:2], banks[2], banks[3:5]
        pt_ps, o_ps, proj_ps = banks[5], banks[6], banks[7]

        w_raw = sb("w_raw", [P, 5, P], F32)
        w_t = sb("w_t", [P, 5, P], F32)
        gate_in = sb("gate_in", [P, 5], F32)
        ctx_t = sb("ctx_t", [P, 2, D], F32)
        xn = sb("xn", [P, 2, D], F32)
        q_t = sb("q_t", [P, 2, DC, P], F32)
        k_m = sb("k_m", [P, 2, DC, 2, 4, SEQ], F32)
        v_m = sb("v_m", [P, 2, 2, 4, 2, N0], F32)
        smax = sb("smax", [P, 2, H0], F32)
        shifted = sb("shifted", [P, 2, H0 * SEQ], F32)
        prob = sb("prob", [P, 2, H0 * SEQ], F32)
        den = sb("den", [P, 2, H0], F32)
        rden = sb("rden", [P, 2, H0], F32)
        p_t = sb("p_t", [P, 2, 4 * P], F32)
        head = sb("head", [P, 2, D], F32)
        mix = sb("mix", [P, 2, D], F32)
        k_hi = sb("k_hi", [P, 2, D], F32R)
        k_lo = sb("k_lo", [P, 2, D], F32R)
        pad = sb("pad", [P, UROWS - MROW, D], F32)

        zeroed, ident_steps, w_loaded, x_loaded, gate_loaded = (
            sem("zeroed"), sem("ident_steps"), sem("w_loaded"), sem("x_loaded"), sem("gate_loaded"))
        wt_done, wt_ready, gate_steps, stats0 = sem("wt_done"), sem("wt_ready"), sem("gate_steps"), sem("stats0")
        ctx_loaded = [sem("ctx_loaded0"), sem("ctx_loaded1")]
        kop_written = [sem("kop_written0"), sem("kop_written1")]
        pad_written, pad_ready = sem("pad_written"), sem("pad_ready")
        xn_ready, qk_done, v_done, q_ready, k_ready, v_ready = (
            sem(n) for n in ("xn_ready", "qk_done", "v_done", "q_ready", "k_ready", "v_ready"))
        score_done, smax_ready, shift_ready, prob_ready, den_ready, rden_ready = (
            sem(n) for n in ("score_done", "smax_ready", "shift_ready", "prob_ready", "den_ready", "rden_ready"))
        pt_done, pt_ready, o_done, head_ready, mix_ready, proj_done, x_ready, st_ready = (
            sem(n) for n in ("pt_done", "pt_ready", "o_done", "head_ready", "mix_ready", "proj_done", "x_ready", "st_ready"))
        khi_ready, klo_ready = sem("khi_ready"), sem("klo_ready")

        block = ctx.enter_context(nc.Block())

        @block.sync
        def _(sp):
            for c in range(4):
                n = TILES // 4
                sp.dma_start(x_all[:, c * n:(c + 1) * n], d["x"][c * n:(c + 1) * n].rearrange("t p n -> p t n")).then_inc(x_loaded, 16)
                if c == 0:
                    sp.wait_ge(zeroed, 1)
                    for m, w in ((0, "wq"), (1, "wk"), (2, "wo")):
                        for b in range(2):
                            r = slice(b * SEQ, (b + 1) * SEQ)
                            sp.dma_start(w_raw[r, m, r], d[w]).then_inc(w_loaded, 16)
                    for b in range(2):
                        for h in range(2):
                            sp.dma_start(w_raw[h * SEQ:(h + 1) * SEQ, 3 + b, b * SEQ:(b + 1) * SEQ], d["wv"]).then_inc(w_loaded, 16)

            def step(s):
                if s.inside(TILES):
                    after(sp, qk_done, s.plus(-2))
                    after(sp, v_done, s.plus(-2))
                    after(sp, klo_ready, s.plus(-2))
                    sp.dma_start(ctx_t[:, s.slot], dram_at(d["ctx"], s.n)).then_inc(ctx_loaded[s.slot], 16)
                t = s.plus(-1)
                if t.inside(TILES):
                    after(sp, khi_ready, t)
                    after(sp, klo_ready, t)
                    rows = d["kop"].rearrange("t u r n -> t r u n")
                    rows = rows[t.n] if t.known else rows[bass.ds(t.n, 1)].rearrange("o r u n -> (o r) u n")
                    for part, src in enumerate((k_hi, k_lo, k_hi)):
                        dst = rows[part * D1:(part + 1) * D1].rearrange("r u n -> u r n")
                        sp.dma_start(dst, raw(src[:, t.slot])).then_inc(kop_written[t.slot], 16)

            run_steps(sp, step, TILES, 2, 2)
            for m, w in enumerate(("L0_ffn_w_gate", "L0_ffn_w_up")):
                sp.dma_start(keep["w0_raw"][:, m], d["a"][w].rearrange("(c p) i -> p c i", p=P)).then_inc(keep["w0_loaded"], 16)
            sp.dma_start(keep["wd0_raw"][:], d["a"]["L0_ffn_w_down"].rearrange("(c p j) n -> p c j n", p=P, j=4)).then_inc(keep["w0_loaded"], 16)
            sp.wait_ge(pad_ready, 2)
            pads = d["kop"].rearrange("t u r n -> (t u) r n")
            for c in range(TILES * UNITS // P):
                sp.dma_start(pads[c * P:(c + 1) * P, MROW:UROWS], pad[:]).then_inc(pad_written, 16)
            sp.dma_start(d["qop"].rearrange("t u r n -> (t u) r n")[:, MROW:UROWS], pad[0:2 * UNITS]).then_inc(pad_written, 16)
            sp.wait_ge(pad_written, 16 * (TILES * UNITS // P + 1))
            for slot in range(2):
                sp.wait_ge(kop_written[slot], 16 * 3 * TILES // 2)

        @block.gpsimd
        def _(pool):
            pool.memset(w_raw[:], 0.0).then_inc(zeroed, 1)
            pool.memset(ident[:], 0.0)
            pool.memset(sel_out[:], 0.0)
            pool.memset(sel_den[:], 0.0).then_inc(ident_steps, 1)
            pool.wait_ge(ident_steps, 1)
            pool.affine_select(out=ident[:], in_=ident[:], compare_op=ALU.not_equal, fill=1.0, base=0,
                               pattern=[[-1, P]], channel_multiplier=1).then_inc(ident_steps, 1)
            pool.memset(k_m[:], 0.0)
            pool.memset(v_m[:], 0.0).then_inc(zeroed, 1)
            v = sel_out[:].rearrange("p (u r) -> p u r", u=4)
            pool.affine_select(out=v, in_=v, compare_op=ALU.not_equal, fill=1.0, base=0,
                               pattern=[[-UROWS, 4], [-1, D1]], channel_multiplier=1)
            v = sel_den[:].rearrange("p (u r) -> p u r", u=4)
            pool.affine_select(out=v, in_=v, compare_op=ALU.not_equal, fill=1.0, base=-D1,
                               pattern=[[-UROWS, 4], [0, D1]], channel_multiplier=1).then_inc(ident_steps, 1)
            pool.memset(x_all[:, TILES:XT], 0.0)
            pool.memset(norm.stats[:, TILES:XT], 0.0)
            pool.memset(norm.eps[:], EPS).then_inc(ident_steps, 1)

            def step(s):
                if s.inside(TILES):
                    after(pool, khi_ready, s)
                    after_dma(pool, kop_written, s.plus(-2), 3)
                    pool.tensor_tensor(k_lo[:, s.slot], ctx_t[:, s.slot], raw(k_hi[:, s.slot]), ALU.subtract).then_inc(klo_ready, 1)
                t = s.plus(-1)
                if t.inside(TILES):
                    after(pool, head_ready, t)
                    after(pool, proj_done, t.plus(-2))
                    pool.tensor_tensor(mix[:, t.slot], xn[:, t.slot], head[:, t.slot], ALU.subtract).then_inc(mix_ready, 1)

            run_steps(pool, step, TILES, 2, 2)
            pool.memset(pad[:], 0.0).then_inc(pad_ready, 1)
            pool.wait_ge(pad_ready, 1)
            pool.memset(pad[:, 0:2], 1.0).then_inc(pad_ready, 1)

        @block.scalar
        def _(act):
            for m, g in enumerate(("g_xattn", "g_ffn", "gamma")):
                w = 2 if m < 2 else 1
                act.dma_start(gate_in[:, 2 * m:2 * m + w], d[g]).then_inc(gate_loaded, 16)
            act.wait_ge(gate_loaded, 48)
            act.activation(gates[:], gate_in[:, 0:4], ACT.Tanh).then_inc(gate_steps, 1)
            act.wait_ge(ident_steps, 4)
            norm.scalar(act)
            act.wait_ge(zeroed, 2)
            act.wait_ge(wt_done, 1)
            act.activation(w_t[:, 0:4].rearrange("p m n -> p (m n)"), banks[0][:], ACT.Copy)
            act.activation(w_t[:, 4], banks[1][:, 0:P], ACT.Copy).then_inc(wt_ready, 1)

            def step(s):
                t = s.plus(-1)
                if t.inside(TILES):
                    after(act, pt_done, t)
                    after(act, o_done, t.plus(-2))
                    act.activation(p_t[:, t.slot], pt_ps[:], ACT.Copy).then_inc(pt_ready, 1)
                if s.inside(TILES):
                    after(act, qk_done, s)
                    after(act, score_done, s.plus(-2))
                    act.activation(q_t[:, s.slot].rearrange("p c n -> p (c n)"), qk_ps[s.slot][:, 0:D], ACT.Copy).then_inc(q_ready, 1)
                    for h in range(4):
                        r = slice(h * N0, (h + 1) * N0)
                        src = qk_ps[s.slot][r, D:2 * D].rearrange("p (c b e) -> p c b e", c=DC, b=2)
                        op = act.activation(k_m[r, s.slot, :, :, h], src, ACT.Copy)
                    op.then_inc(k_ready, 1)
                    after_dma(act, ctx_loaded, s)
                    after_dma(act, kop_written, s.plus(-2), 3)
                    act.activation(k_hi[:, s.slot], ctx_t[:, s.slot], ACT.Copy).then_inc(khi_ready, 1)
                    after(act, shift_ready, s)
                    after(act, pt_done, s.plus(-2))
                    after(act, den_ready, s.plus(-2))
                    act.activation(prob[:, s.slot], shifted[:, s.slot], ACT.Exp, scale=SCALE0).then_inc(prob_ready, 1)

            run_steps(act, step, TILES, 2, 2)

        @block.tensor
        def _(pe):
            pe.wait_ge(w_loaded, 160)
            pe.wait_ge(ident_steps, 2)
            for m in range(4):
                pe.transpose(banks[0][:, m * P:(m + 1) * P], w_raw[:, m], ident[:])
            pe.transpose(banks[1][:, 0:P], w_raw[:, 4], ident[:]).then_inc(wt_done, 1)
            pe.wait_ge(wt_ready, 1)

            def step(s):
                t, u = s.plus(-1), s.plus(-2)
                if t.inside(TILES):
                    after(pe, prob_ready, t)
                    after(pe, pt_ready, t.plus(-1))
                    for hp in range(4):
                        mm = pe.transpose(pt_ps[:, hp * P:(hp + 1) * P], prob[:, t.slot, hp * P:(hp + 1) * P], ident[:])
                    mm.then_inc(pt_done, 1)
                if s.inside(TILES):
                    after(pe, xn_ready, s)
                    after_dma(pe, ctx_loaded, s)
                    after(pe, q_ready, s.plus(-2))
                    after(pe, k_ready, s.plus(-2))
                    for m, src in ((0, xn), (1, ctx_t)):
                        for c in range(DC):
                            o = (2 * m + c) * P
                            mm = pe.matmul(qk_ps[s.slot][:, o:o + P], lhsT=src[:, s.slot, c * P:(c + 1) * P], rhs=w_t[:, m],
                                           start=True, stop=True)
                    mm.then_inc(qk_done, 1)
                    after(pe, v_ready, s.plus(-1))
                    for b in range(2):
                        mm = pe.matmul(v_ps[:, b * D:(b + 1) * D], lhsT=w_t[:, 3 + b], rhs=ctx_t[:, s.slot], start=True, stop=True)
                    mm.then_inc(v_done, 1)
                if u.inside(TILES):
                    after(pe, mix_ready, u)
                    after(pe, x_ready, u.plus(-1))
                    pe.matmul(proj_ps[:, 0:D], lhsT=w_t[:, 2], rhs=mix[:, u.slot], start=True, stop=True).then_inc(proj_done, 1)
                if t.inside(TILES):
                    after(pe, pt_ready, t)
                    after(pe, v_ready, t)
                    after(pe, head_ready, t.plus(-1))
                    for hp in range(4):
                        for b in range(2):
                            mm = pe.matmul(o_ps[b * SEQ:(b + 1) * SEQ, hp * SEQ:(hp + 1) * SEQ],
                                           lhsT=p_t[:, t.slot, hp * P + b * SEQ:hp * P + (b + 1) * SEQ],
                                           rhs=v_m[:, t.slot, b, hp].rearrange("p h n -> p (h n)"),
                                           start=True, stop=True, tile_position=(0, b * SEQ))
                    mm.then_inc(o_done, 1)
                if s.inside(TILES):
                    after(pe, q_ready, s)
                    after(pe, k_ready, s)
                    after(pe, shift_ready, s.plus(-2))
                    for c in range(DC):
                        for b in range(2):
                            mm = pe.matmul(s_ps[s.slot][b * SEQ:(b + 1) * SEQ, c * D:(c + 1) * D],
                                           lhsT=q_t[:, s.slot, c, b * SEQ:(b + 1) * SEQ],
                                           rhs=k_m[:, s.slot, c, b].rearrange("p h e -> p (h e)"),
                                           start=True, stop=True, tile_position=(0, b * SEQ))
                    mm.then_inc(score_done, 1)

            run_steps(pe, step, TILES, 2, 2)

        @block.vector
        def _(dve):
            dve.wait_ge(x_loaded, 64)
            with dve.Fori(0, TILES) as t:
                dve.bn_stats(at(norm.stats, t), at(x_all, t)).then_inc(stats0, 1)
            dve.wait_ge(stats0, TILES)
            dve.wait_ge(ident_steps, 4)
            norm.vector(dve)
            dve.wait_ge(gate_steps, 1)
            dve.tensor_tensor(gates[:, 1:2], gates[:, 1:2], gate_in[:, 4:5], ALU.mult).then_inc(gate_steps, 1)
            dve.wait_ge(gate_steps, 2)
            dve.wait_ge(zeroed, 2)

            def step(s):
                t, u = s.plus(-1), s.plus(-2)
                if t.inside(TILES):
                    after(dve, prob_ready, t)
                    dve.tensor_reduce(den[:, t.slot], prob[:, t.slot].rearrange("p (h e) -> p h e", h=H0), AX_X, ALU.add).then_inc(den_ready, 1)
                if s.inside(TILES):
                    after(dve, qk_done, s.plus(-2))
                    after(dve, mix_ready, s.plus(-2))
                    norm.apply(dve, xn[:, s.slot], x_all, s.n).then_inc(xn_ready, 1)
                if t.inside(TILES):
                    after(dve, den_ready, t)
                    dve.reciprocal(rden[:, t.slot], den[:, t.slot]).then_inc(rden_ready, 1)
                if s.inside(TILES):
                    after(dve, v_done, s)
                    after(dve, o_done, s.plus(-2))
                    for h in range(2):
                        r = slice(h * SEQ, (h + 1) * SEQ)
                        src = v_ps[r].rearrange("p (b g h n) -> p b g h n", b=2, g=4, h=2)
                        for b in range(2):
                            op = dve.tensor_copy(v_m[r, s.slot, b, :, h], src[:, b, :, h])
                    op.then_inc(v_ready, 1)
                if t.inside(TILES):
                    after(dve, o_done, t)
                    after(dve, rden_ready, t)
                    after(dve, mix_ready, t.plus(-2))
                    dve.tensor_tensor(head[:, t.slot].rearrange("p (h n) -> p h n", h=H0),
                                      o_ps[:, 0:D].rearrange("p (h n) -> p h n", h=H0),
                                      rden[:, t.slot].unsqueeze(2).to_broadcast([P, H0, N0]), ALU.mult).then_inc(head_ready, 1)
                if s.inside(TILES):
                    after(dve, score_done, s)
                    dve.tensor_reduce(smax[:, s.slot], s_ps[s.slot][:].rearrange("p (h e) -> p h e", h=H0), AX_X, ALU.max).then_inc(smax_ready, 1)
                    after(dve, smax_ready, s)
                    after(dve, prob_ready, s.plus(-2))
                    dve.tensor_tensor(shifted[:, s.slot].rearrange("p (h e) -> p h e", h=H0),
                                      s_ps[s.slot][:].rearrange("p (h e) -> p h e", h=H0),
                                      smax[:, s.slot].unsqueeze(2).to_broadcast([P, H0, SEQ]), ALU.subtract).then_inc(shift_ready, 1)
                if u.inside(TILES):
                    after(dve, proj_done, u)
                    dve.scalar_tensor_tensor(at(x_all, u.n), proj_ps[:, 0:D], gates[:, 0:1], at(x_all, u.n), ALU.mult, ALU.add).then_inc(x_ready, 1)
                    after(dve, x_ready, u)
                    dve.bn_stats(at(norm.stats, u.n), at(x_all, u.n)).then_inc(st_ready, 1)

            run_steps(dve, step, TILES, 2, 2)
            dve.wait_ge(st_ready, TILES)
    norm.used += 6


def normalised(dve, pe_xn_free, norm, xn, x_all, g, ready):
    for k in range(GT):
        op = norm.apply(dve, xn[:, k], x_all, g.n * GT + k)
    op.then_inc(ready, 1)


def feed_forward0(nc, sem, keep, d):
    x_all, norm, ident, gates = keep["x_all"], keep["norm"], keep["ident"], keep["gates"]
    w_raw, wd_raw, w_loaded = keep["w0_raw"], keep["wd0_raw"], keep["w0_loaded"]
    with ExitStack() as ctx:
        def sb(name, shape, dt):
            return ctx.enter_context(nc.sbuf_tensor(name, shape, dt))

        def pair(name, shape):
            return sb(name + "_hi", shape, F32R), sb(name + "_lo", shape, F32R)

        banks = [ctx.enter_context(nc.psum_tensor(f"f0_bank{i}", [P, 512], F32)) for i in range(8)]
        g_ps, u_ps, down_ps, xt_ps = banks[0:2], banks[2:4], banks[4:6], banks[6:8]

        w = pair("w0", [P, 2, DC, QUAD0, 4, P])
        wd = pair("wd0", [P, QUAD0, 4, D])
        xn = sb("f0_xn", [P, GT, D], F32)
        xt = pair("f0_xt", [P, DC, GN])
        sg = sb("f0_sg", [P, 2, GN], F32)
        hid = sb("f0_hid", [P, 2, 4, GN], F32)
        mag = sb("f0_mag", [P, 4, GN], F32)
        beat_a, beat_b, beat_c = (sb(f"f0_beat_{n}", [P, 2, GN], BF16) for n in "abc")
        wins = sb("f0_wins", [P, 4, GN], BF16)
        sums = sb("f0_sums", [P, 4, GN], BF16)
        kept = sb("f0_kept", [P, 4, GN], F32)
        hs = pair("f0_hs", [P, 4, GN])

        whi_ready, w_ready = sem("f0_whi_ready"), sem("f0_w_ready")
        xn_ready, xt_done, xhi_ready, xt_ready = sem("f0_xn_ready"), sem("f0_xt_done"), sem("f0_xhi_ready"), sem("f0_xt_ready")
        gate_done, up_done, silu_ready, hid_ready, mag_ready = (
            sem("f0_" + n) for n in ("gate_done", "up_done", "silu_ready", "hid_ready", "mag_ready"))
        beat_ready, wins_ready, sums_ready, kept_ready, hshi_ready, hs_ready = (
            sem("f0_" + n) for n in ("beat_ready", "wins_ready", "sums_ready", "kept_ready", "hshi_ready", "hs_ready"))
        down_done, x_ready, st_ready = sem("f0_down_done"), sem("f0_x_ready"), sem("f0_st_ready")

        block = ctx.enter_context(nc.Block())

        blocks = []
        for m in range(2):
            for dc in range(DC):
                for c in range(QUAD0):
                    src = w_raw[:, m, dc, c * GN:(c + 1) * GN].rearrange("p (m j) -> p j m", j=4)
                    blocks.append((src, w[0][:, m, dc, c], w[1][:, m, dc, c]))
        for c in range(QUAD0):
            for j in range(0, 4, 2):
                blocks.append((wd_raw[:, c, j:j + 2], wd[0][:, c, j:j + 2], wd[1][:, c, j:j + 2]))

        @block.tensor
        def _(pe):
            def transposes(g):
                after(pe, xn_ready, g)
                after(pe, xt_ready, g.plus(-1))
                for dc in range(DC):
                    for k in range(GT):
                        mm = pe.transpose(xt_ps[dc][:, k * P:(k + 1) * P], xn[:, k, dc * P:(dc + 1) * P], ident[:])
                mm.then_inc(xt_done, 1)

            def hidden(g, c):
                if c == 0:
                    after(pe, xt_ready, g)
                for j in range(4):
                    n = g.n * 8 + c * 4 + j
                    slot = j % 2
                    for m, ps, free, done in ((0, g_ps, silu_ready, gate_done), (1, u_ps, hid_ready, up_done)):
                        if not (g.known and n < 2):
                            pe.wait_ge(free, n - 1)
                        for dc in range(DC):
                            mm = product3(pe, ps[slot][:], (w[0][:, m, dc, c, j], w[1][:, m, dc, c, j]),
                                          (xt[0][:, dc], xt[1][:, dc]), dc == 0, dc == DC - 1)
                        mm.then_inc(done, 1)

            def down(g, c):
                if g.known and g.n < 0:
                    return
                if c == 0:
                    after(pe, x_ready, g.plus(-1), GT)
                for j in range(4):
                    pe.wait_ge(hs_ready, g.n * 8 + c * 4 + j + 1)
                    for k in range(GT):
                        cols = slice(k * P, (k + 1) * P)
                        mm = product3(pe, down_ps[k // 2][:, (k % 2) * D:(k % 2 + 1) * D],
                                      (hs[0][:, j, cols], hs[1][:, j, cols]), (wd[0][:, c, j], wd[1][:, c, j]),
                                      c == 0 and j == 0 and k % 2 == 0, c == QUAD0 - 1 and j == 3, skip_group_check=True)
                mm.then_inc(down_done, 1)

            def group(g):
                hidden(g, 0)
                down(g.plus(-1), 1)
                transposes(g.plus(1))
                hidden(g, 1)
                down(g, 0)

            pe.wait_ge(w_ready, len(blocks))
            transposes(Step(0, 0, 1))
            group(Step(0, 0, 1))
            with pe.Fori(1, GROUPS) as r:
                group(Step(r, 0, 1))
            down(Step(GROUPS - 1, 0, 1), 1)

        @block.scalar
        def _(act):
            norm.scalar(act)
            act.wait_ge(w_loaded, 48)
            for src, hi, _ in blocks:
                act.activation(hi, src, ACT.Copy).then_inc(whi_ready, 1)

            def xt_high(g):
                after(act, xt_done, g)
                after(act, up_done, g.plus(-1), 8)
                for dc in range(DC):
                    op = act.activation(xt[0][:, dc], xt_ps[dc][:], ACT.Copy)
                op.then_inc(xhi_ready, 1)

            def hidden_high(s, c, j):
                n = s * 4 + j
                act.wait_ge(kept_ready, n + 1)
                if not (isinstance(s, int) and s < 1):
                    act.wait_ge(down_done, s)
                act.activation(hs[0][:, j], kept[:, j], ACT.Copy).then_inc(hshi_ready, 1)

            def group(g):
                for c in range(2):
                    s = g.n * 2 + c
                    for j in range(4):
                        n = s * 4 + j
                        first = g.known and g.n == 0 and c == 0
                        if j == 3 and not first:
                            for jj in range(4):
                                hidden_high(s - 1, c, jj)
                        act.wait_ge(gate_done, n + 1)
                        if not (first and j < 2):
                            act.wait_ge(hid_ready, n - 1)
                        act.activation(sg[:, j % 2], g_ps[j % 2][:], ACT.Silu).then_inc(silu_ready, 1)
                        act.wait_ge(hid_ready, n + 1)
                        if not first:
                            act.wait_ge(beat_ready, s)
                        act.activation(mag[:, j], hid[:, c, j], ACT.Abs).then_inc(mag_ready, 1)
                xt_high(g.plus(1))

            xt_high(Step(0, 0, 1))
            group(Step(0, 0, 1))
            with act.Fori(1, GROUPS) as r:
                group(Step(r, 0, 1))
            for j in range(4):
                hidden_high(2 * GROUPS - 1, 1, j)

        @block.gpsimd
        def _(pool):
            with pool.Fori(0, 2 * GROUPS) as s:
                for j in range(4):
                    pool.wait_ge(hshi_ready, s * 4 + (j + 1))
                    pool.tensor_tensor(hs[1][:, j], kept[:, j], raw(hs[0][:, j]), ALU.subtract).then_inc(hs_ready, 1)

        @block.vector
        def _(dve):
            norm.vector(dve)

            def xt_low(g):
                after(dve, xhi_ready, g)
                for dc in range(DC):
                    op = dve.tensor_tensor(xt[1][:, dc], xt_ps[dc][:], raw(xt[0][:, dc]), ALU.subtract)
                op.then_inc(xt_ready, 1)

            def hidden(g, c, j):
                n = g.n * 8 + c * 4 + j
                dve.wait_ge(silu_ready, n + 1)
                dve.wait_ge(up_done, n + 1)
                if not (g.known and g.n == 0):
                    dve.wait_ge(mag_ready, n - 7)
                dve.tensor_tensor(hid[:, c, j], sg[:, j % 2], u_ps[j % 2][:], ALU.mult).then_inc(hid_ready, 1)

            def compare(s):
                dve.wait_ge(mag_ready, s * 4 + 4)
                if not (isinstance(s, int) and s < 1):
                    dve.wait_ge(sums_ready, s)
                dve.tensor_tensor(beat_a[:], mag[:, 0:2], mag[:, 2:4], ALU.is_ge)
                dve.tensor_tensor(beat_b[:, 0], mag[:, 0], mag[:, 3], ALU.is_ge)
                dve.tensor_tensor(beat_b[:, 1], mag[:, 1], mag[:, 2], ALU.is_ge)
                dve.tensor_tensor(beat_c[:], mag[:, 0:4:2], mag[:, 1:4:2], ALU.is_ge).then_inc(beat_ready, 1)

            def count(s):
                dve.wait_ge(beat_ready, s + 1)
                dve.tensor_tensor(wins[:, 0:2], beat_a[:], beat_b[:], ALU.add)
                dve.tensor_tensor(wins[:, 2], beat_a[:, 0], beat_b[:, 1], ALU.add)
                dve.tensor_tensor(wins[:, 3], beat_a[:, 1], beat_b[:, 0], ALU.add).then_inc(wins_ready, 1)
                dve.wait_ge(wins_ready, s + 1)
                if not (isinstance(s, int) and s < 1):
                    dve.wait_ge(kept_ready, s * 4)
                dve.tensor_tensor(sums[:, 0:4:3], wins[:, 0:4:3], beat_c[:], ALU.add)
                dve.tensor_tensor(sums[:, 1:3], wins[:, 1:3], beat_c[:], ALU.subtract).then_inc(sums_ready, 1)

            def keep_two(s, c):
                dve.wait_ge(sums_ready, s + 1)
                for j, (op, bound) in enumerate(((ALU.is_ge, 2.0), (ALU.is_ge, 1.0), (ALU.is_le, 0.0), (ALU.is_le, 1.0))):
                    if not (isinstance(s, int) and s < 1):
                        dve.wait_ge(hs_ready, s * 4 + (j - 3))
                    dve.scalar_tensor_tensor(kept[:, j], sums[:, j], bound, hid[:, c, j], op, ALU.mult).then_inc(kept_ready, 1)

            def residual(g):
                after(dve, down_done, g, 2)
                for k in range(GT):
                    t = g.n * GT + k
                    dve.scalar_tensor_tensor(at(x_all, t), down_ps[k // 2][:, (k % 2) * D:(k % 2 + 1) * D], gates[:, 2:3],
                                             at(x_all, t), ALU.mult, ALU.add).then_inc(x_ready, 1)
                for k in range(GT):
                    t = g.n * GT + k
                    dve.wait_ge(x_ready, t + 1)
                    dve.bn_stats(at(norm.stats, t), at(x_all, t)).then_inc(st_ready, 1)

            def group(g):
                first = g.known and g.n == 0
                for c in range(2):
                    s = g.n * 2 + c
                    lagged = not (first and c == 0)
                    if lagged:
                        compare(s - 1)
                    hidden(g, c, 0)
                    if lagged:
                        count(s - 1)
                    hidden(g, c, 1)
                    if lagged:
                        keep_two(s - 1, 1 - c)
                    hidden(g, c, 2)
                    hidden(g, c, 3)
                    if c == 0:
                        after(dve, xt_done, g)
                        normalised(dve, None, norm, xn, x_all, g.plus(1), xn_ready)
                        if not first:
                            residual(g.plus(-1))
                xt_low(g.plus(1))

            normalised(dve, None, norm, xn, x_all, Step(0, 0, 1), xn_ready)
            dve.wait_ge(whi_ready, len(blocks))
            for src, hi, lo in blocks:
                dve.tensor_tensor(lo, src, raw(hi), ALU.subtract).then_inc(w_ready, 1)
            xt_low(Step(0, 0, 1))
            group(Step(0, 0, 1))
            with dve.Fori(1, GROUPS) as r:
                group(Step(r, 0, 1))
            s = 2 * GROUPS - 1
            compare(s)
            count(s)
            keep_two(s, 1)
            residual(Step(GROUPS - 1, 0, 1))
            dve.wait_ge(st_ready, TILES)
    norm.used += 6


def attention1(nc, sem, keep, d):
    x_all, norm, ident, gates = keep["x_all"], keep["norm"], keep["ident"], keep["gates"]
    sel_out, sel_den = keep["sel_out"], keep["sel_den"]
    w_raw, wd_raw, w = keep["w1_raw"], keep["wd1_raw"], keep["w1"]
    PAIRS = UNITS // 2
    SPLIT = 4 * I1 // TILES
    with ExitStack() as ctx:
        def sb(name, shape, dt):
            return ctx.enter_context(nc.sbuf_tensor(name, shape, dt))

        s_ps = [ctx.enter_context(nc.psum_tensor(f"a1_s{i}", [P, 2, 512], F32)) for i in range(2)]
        st_ps = [ctx.enter_context(nc.psum_tensor(f"a1_st{i}", [P, 512], F32)) for i in range(2)]
        pv_ps = ctx.enter_context(nc.psum_tensor("a1_pv", [P, 512], F32))
        misc = ctx.enter_context(nc.psum_tensor("a1_misc", [P, 512], F32))

        xn = sb("a1_xn", [P, 2, D], F32)
        q_hi = sb("a1_q_hi", [P, 2, D], F32R)
        q_lo = sb("a1_q_lo", [P, 2, D], F32R)
        qop = sb("a1_qop", [P, 2, QUADS, D], F32R)
        kop = sb("a1_kop", [P, 2, QUADS, D], F32R)
        ctx_t = sb("a1_ctx", [P, 2, D], F32)
        vt = sb("a1_vt", [P, 2, DC, UNITS, 32], F32)
        smax = sb("a1_smax", [P, 2, UNITS, 2], F32)
        neg = sb("a1_neg", [P, 2, 2, 2, UNITS // 2], F32R)
        neg_t = sb("a1_neg_t", [UNITS, 2, D], F32)
        prob = sb("a1_prob", [P, 8, 2 * D], F32)
        pv = sb("a1_pv_sb", [P, 2, QUADS, D], F32)
        rden = sb("a1_rden", [P, D], F32)
        att = sb("a1_att", [P, D], F32)

        xn_ready, qhi_ready, qlo_ready, vt_cleared = (sem("a1_" + n) for n in ("xn_ready", "qhi_ready", "qlo_ready", "vt_cleared"))
        q_written = [sem(f"a1_q_written{i}") for i in range(2)]
        op_loaded = [[sem(f"a1_op_loaded{i}{h}") for i in range(2)] for h in range(2)]
        max_loaded = [[sem(f"a1_max_loaded{i}{h}") for i in range(2)] for h in range(2)]
        ctx_loaded = [sem(f"a1_ctx_loaded{i}") for i in range(2)]
        s_done, smax_ready, neg_hi, neg_ready, neg_done, neg_t_ready = (
            sem("a1_" + n) for n in ("s_done", "smax_ready", "neg_hi", "neg_ready", "neg_done", "neg_t_ready"))
        st_done, prob_ready, pv_done, pv_ready = (sem("a1_" + n) for n in ("st_done", "prob_ready", "pv_done", "pv_ready"))
        vt_done, vt_ready, sel_done, rden_ready, att_ready, x_ready, st_ready = (
            sem("a1_" + n) for n in ("vt_done", "vt_ready", "sel_done", "rden_ready", "att_ready", "x_ready", "st_ready"))
        split_hi, split_lo = sem("a1_split_hi"), sem("a1_split_lo")

        block = ctx.enter_context(nc.Block())
        LAG = 3

        @block.sync
        def _(sp):
            load_w1(sp, keep, d)

            def maxima(t, h):
                if not t.inside(TILES):
                    return
                after(sp, neg_t_ready, t, 2, h + 1)
                for part in range(2):
                    for q in range(2):
                        src = neg_t[part * 8 + q * 4:part * 8 + q * 4 + 4, h]
                        dst = qop[MROW + part:P:UROWS, t.slot, 2 * h + q]
                        sp.dma_start(raw(dst), src).then_inc(max_loaded[h][t.slot], 16)

            def operands(t, h):
                if not t.inside(TILES):
                    return
                after(sp, st_done, t.plus(-2), UNITS, 8 * (h + 1))
                quads = slice(2 * h, 2 * h + 2)
                rows = d["kop"].rearrange("t (g v) r n -> t (v r) g n", g=QUADS)
                rows = rows[t.n] if t.known else rows[bass.ds(t.n, 1)].rearrange("o p g n -> (o p) g n")
                sp.dma_start(raw(kop[:, t.slot, quads]), rows[:, quads]).then_inc(op_loaded[h][t.slot], 16)
                after_dma(sp, q_written, t, 3)
                rows = d["qop"][t.slot].rearrange("(g v) r n -> (v r) g n", g=QUADS)
                sp.dma_start(raw(qop[:, t.slot, quads]), rows[:, quads]).then_inc(op_loaded[h][t.slot], 16)

            def step(s):
                maxima(s.plus(-2), 1)
                v = s.plus(-1)
                if v.inside(TILES):
                    after(sp, vt_done, v.plus(-2))
                    sp.dma_start(ctx_t[:, v.slot], dram_at(d["ctx"], v.n)).then_inc(ctx_loaded[v.slot], 16)
                operands(s, 0)
                maxima(s.plus(-1), 0)
                operands(s, 1)

            run_steps(sp, step, TILES, LAG, 2)

        @block.gpsimd
        def _(pool):
            pool.memset(vt[:], 0.0).then_inc(vt_cleared, 1)
            pool.wait_ge(vt_cleared, 1)
            pool.memset(vt[:, :, :, :, D1:D1 + 1], 1.0).then_inc(vt_cleared, 1)
            pool.wait_ge(keep["w1_loaded"], 16 * W1_LOADS)

            def step(s):
                if s.inside(TILES):
                    after(pool, qhi_ready, s)
                    after_dma(pool, q_written, s.plus(-2), 3)
                    pool.tensor_tensor(q_lo[:, s.slot], xn[:, s.slot], raw(q_hi[:, s.slot]), ALU.subtract).then_inc(qlo_ready, 1)
                    cols = slice(s.n * SPLIT, (s.n + 1) * SPLIT) if s.known else bass.ds(s.n * SPLIT, SPLIT)
                    pool.tensor_copy(w[0][:, cols], w_raw[:, cols]).then_inc(split_hi, 1)
                    after(pool, qlo_ready, s)
                    for h in range(2):
                        after_dma(pool, op_loaded[h], s.plus(-2), 2)
                    after(pool, split_hi, s)
                    pool.tensor_tensor(w[1][:, cols], w_raw[:, cols], raw(w[0][:, cols]), ALU.subtract).then_inc(split_lo, 1)
                    rows = d["qop"][s.slot].rearrange("u r n -> r u n")
                    for part, src in enumerate((q_hi, q_hi, q_lo)):
                        dst = rows[part * D1:(part + 1) * D1].rearrange("r u n -> u r n")
                        pool.dma_start(dst, raw(src[:, s.slot])).then_inc(q_written[s.slot], 16)

            run_steps(pool, step, TILES, LAG, 2)
            pool.wait_ge(split_lo, TILES)

        @block.scalar
        def _(act):
            norm.scalar(act)

            def step(s):
                v, t, o = s.plus(-1), s.plus(-2), s.plus(-3)
                if s.inside(TILES):
                    after(act, xn_ready, s)
                    after_dma(act, q_written, s.plus(-2), 3)
                    act.activation(q_hi[:, s.slot], xn[:, s.slot], ACT.Copy).then_inc(qhi_ready, 1)

                def turned(w_, h):
                    if w_.inside(TILES):
                        after(act, neg_done, w_, 2, h + 1)
                        if not (w_.known and w_.rnd < 1):
                            pass
                        prev = w_.plus(-1)
                        after_dma(act, max_loaded[h], prev, 4)
                        act.activation(neg_t[:, h], misc[0:UNITS, 0:D], ACT.Copy).then_inc(neg_t_ready, 1)

                def weighted(w_, q):
                    if w_.inside(TILES):
                        after(act, pv_done, w_, QUADS, q + 1)
                        after(act, sel_done, w_.plus(-2))
                        act.activation(pv[:, w_.slot, q], pv_ps[:, 0:D], ACT.Copy).then_inc(pv_ready, 1)

                for u in range(UNITS):
                    j = u // 2
                    if t.inside(TILES):
                        after(act, st_done, t, UNITS, u + 1)
                        quad = (u - 8) // 4
                        if quad >= 0:
                            after(act, pv_done, t, QUADS, quad + 1)
                        else:
                            after(act, pv_done, t.plus(-1), QUADS, quad + QUADS + 1)
                        act.activation(prob[:, u % 8], st_ps[u % 2][:], ACT.Exp, scale=SCALE1).then_inc(prob_ready, 1)
                    if u == 1:
                        turned(t, 1)
                    if u == 3:
                        weighted(o, 3)
                    if u == 5 and v.inside(TILES):
                        after(act, vt_done, v)
                        act.activation(vt[:, v.slot, :, :, 0:D1], misc[:, 0:D].rearrange("p (c u r) -> p c u r", c=DC, r=D1),
                                       ACT.Copy).then_inc(vt_ready, 1)
                    if u == 11:
                        turned(v, 0)
                    if u in (7, 11, 15):
                        weighted(t, (u - 7) // 4)

            run_steps(act, step, TILES, LAG, 2)

        @block.tensor
        def _(pe):
            pe.wait_ge(vt_cleared, 2)

            def step(s):
                v, t, o = s.plus(-1), s.plus(-2), s.plus(-3)

                def turn(w_, h, before):
                    if w_.inside(TILES):
                        after(pe, neg_ready, w_, 2, h + 1)
                        before()
                        for q in range(2):
                            mm = pe.transpose(misc[0:UNITS, q * P:(q + 1) * P],
                                              raw(neg[:, h, q].rearrange("p a u -> p (a u)")), ident[:])
                        mm.then_inc(neg_done, 1)

                def products(w_, q):
                    if w_.inside(TILES):
                        after(pe, prob_ready, w_, UNITS, 4 * q + 4)
                        after(pe, vt_ready, w_)
                        if q:
                            after(pe, pv_ready, w_, QUADS, q)
                        else:
                            after(pe, pv_ready, w_.plus(-1), QUADS)
                        for c in range(DC):
                            for v4 in range(4):
                                u = 4 * q + v4
                                mm = pe.matmul(pv_ps[v4 * 32:(v4 + 1) * 32, 0:D], lhsT=vt[:, w_.slot, c, u],
                                               rhs=prob[:, u % 8, c * D:(c + 1) * D], start=(c == 0), stop=(c == DC - 1),
                                               tile_position=(0, v4 * 32))
                        mm.then_inc(pv_done, 1)

                for j in range(PAIRS):
                    if v.inside(TILES):
                        if j % 4 == 0:
                            after_dma(pe, op_loaded[j // 4], v, 2)
                        if j >= 2:
                            after(pe, smax_ready, v, PAIRS, j - 1)
                        else:
                            after(pe, smax_ready, v.plus(-1), PAIRS, PAIRS - 1 + j)
                        for k in range(2):
                            u = 2 * j + k
                            g, r = u // 4, slice((u % 4) * UROWS, (u % 4) * UROWS + MROW)
                            for q in range(2):
                                mm = pe.matmul(s_ps[j % 2][:, k, q * D:(q + 1) * D], lhsT=qop[r, v.slot, g, q * P:(q + 1) * P],
                                               rhs=kop[r, v.slot, g], start=True, stop=True, tile_position=((u % 4) * UROWS, 0))
                        mm.then_inc(s_done, 1)
                    if t.inside(TILES):
                        if j % 4 == 0:
                            after_dma(pe, max_loaded[j // 4], t, 4)
                        for k in range(2):
                            u = 2 * j + k
                            g, r = u // 4, slice((u % 4) * UROWS, (u % 4) * UROWS + MROW + 2)
                            if u >= 2:
                                after(pe, prob_ready, t, UNITS, u - 1)
                            else:
                                after(pe, prob_ready, t.plus(-1), UNITS, UNITS - 1 + u)
                            for c in range(DC):
                                mm = pe.matmul(st_ps[u % 2][:, c * D:(c + 1) * D], lhsT=kop[r, t.slot, g, c * P:(c + 1) * P],
                                               rhs=qop[r, t.slot, g], start=True, stop=True, tile_position=((u % 4) * UROWS, 0))
                            mm.then_inc(st_done, 1)
                    if j == 0:
                        turn(t, 1, lambda: after(pe, neg_t_ready, t, 2, 1))
                    if j == 1:
                        products(o, 3)
                    if j == 2 and v.inside(TILES):
                        after_dma(pe, ctx_loaded, v)
                        after(pe, neg_t_ready, t, 2)
                        for c in range(DC):
                            mm = pe.transpose(misc[:, c * P:(c + 1) * P], ctx_t[:, v.slot, c * P:(c + 1) * P], ident[:])
                        mm.then_inc(vt_done, 1)
                    if j == 3 and o.inside(TILES):
                        after(pe, pv_ready, o, QUADS)
                        if t.inside(TILES):
                            after(pe, neg_t_ready, t, 2)
                        if v.inside(TILES):
                            after(pe, vt_ready, v)
                        after(pe, att_ready, o.plus(-1))
                        for m, sel in enumerate((sel_out, sel_den)):
                            for q in range(QUADS):
                                mm = pe.matmul(misc[q * 32:(q + 1) * 32, m * D:(m + 1) * D], lhsT=sel[:], rhs=pv[:, o.slot, q],
                                               start=True, stop=True, tile_position=(0, q * 32))
                        mm.then_inc(sel_done, 1)
                    if j in (3, 5, 7):
                        products(t, (j - 3) // 2)
                    if j == 5:
                        def before():
                            after(pe, vt_ready, v)
                            after(pe, att_ready, o)
                        turn(v, 0, before)

            run_steps(pe, step, TILES, LAG, 2)

        @block.vector
        def _(dve):
            norm.vector(dve)

            def step(s):
                v, t, o = s.plus(-1), s.plus(-2), s.plus(-3)

                def negated(w_, h):
                    src = smax[:, w_.slot, 8 * h:8 * h + 8].rearrange("p u q -> p q u")
                    after(dve, smax_ready, w_, PAIRS, 4 * h + 4)
                    after(dve, neg_done, w_.plus(-1), 2, h + 1)
                    dve.tensor_scalar(neg[:, h, :, 0], src, -1.0, None, ALU.mult).then_inc(neg_hi, 1)
                    after(dve, neg_hi, w_, 2, h + 1)
                    dve.scalar_tensor_tensor(neg[:, h, :, 1], src, -1.0, raw(neg[:, h, :, 0]), ALU.mult, ALU.subtract).then_inc(neg_ready, 1)

                if s.inside(TILES):
                    after(dve, qlo_ready, s.plus(-2))
                    norm.apply(dve, xn[:, s.slot], x_all, s.n).then_inc(xn_ready, 1)
                for j in range(PAIRS):
                    if v.inside(TILES):
                        after(dve, s_done, v, PAIRS, j + 1)
                        dve.tensor_reduce(smax[:, v.slot, 2 * j:2 * j + 2].rearrange("p u q -> p (u q)"),
                                          s_ps[j % 2][:].rearrange("p u (q n) -> p (u q) n", q=2), AX_X, ALU.max).then_inc(smax_ready, 1)
                        if j == 3:
                            negated(v, 0)
                        if j == 7:
                            negated(v, 1)
                    if j == 4 and o.inside(TILES):
                        after(dve, sel_done, o)
                        dve.reciprocal(rden[:], misc[:, D:2 * D]).then_inc(rden_ready, 1)
                        after(dve, rden_ready, o)
                        dve.tensor_tensor(att[:], misc[:, 0:D], rden[:], ALU.mult).then_inc(att_ready, 1)
                        after(dve, att_ready, o)
                        dve.scalar_tensor_tensor(at(x_all, o.n), att[:], gates[:, 1:2], at(x_all, o.n), ALU.mult, ALU.add).then_inc(x_ready, 1)
                        after(dve, x_ready, o)
                        dve.bn_stats(at(norm.stats, o.n), at(x_all, o.n)).then_inc(st_ready, 1)

            run_steps(dve, step, TILES, LAG, 2)
            dve.wait_ge(st_ready, TILES)
    norm.used += 6


W1_LOADS = 2 * (DC + 1) + 3


def load_w1(sp, keep, d):
    a, loaded = d["a"], keep["w1_loaded"]
    raw_gu = keep["w1_raw"][:].rearrange("p (m c i) -> p m c i", m=2, c=DC)
    for m, (we, ws) in enumerate((("L1_ffn_We_gate", "L1_ffn_Ws_gate"), ("L1_ffn_We_up", "L1_ffn_Ws_up"))):
        for c in range(DC):
            dst = raw_gu[:, m, c, 0:E * DE].rearrange("p (e j) -> p e j", e=E)
            sp.dma_start(dst, a[we][:, c * P:(c + 1) * P].rearrange("e p j -> p e j")).then_inc(loaded, 16)
        sp.dma_start(raw_gu[:, m, :, E * DE:I1], a[ws].rearrange("(c p) j -> p c j", p=P)).then_inc(loaded, 16)
    raw_d = keep["wd1_raw"]
    sp.dma_start(raw_d[:, 0:CHR], a["L1_ffn_We_down"].rearrange("e j n -> (e j) n").rearrange("(c p) n -> p c n", p=P)).then_inc(loaded, 16)
    full = CH1 - 1 - CHR
    sp.dma_start(raw_d[:, CHR:CH1 - 1], a["L1_ffn_Ws_down"][0:full * P].rearrange("(c p) n -> p c n", p=P)).then_inc(loaded, 16)
    sp.dma_start(raw_d[0:LASTM, CH1 - 1], a["L1_ffn_Ws_down"][full * P:DS]).then_inc(loaded, 16)


def feed_forward1(nc, sem, keep, d):
    x_all, norm, ident, gates = keep["x_all"], keep["norm"], keep["ident"], keep["gates"]
    w, wd_raw = keep["w1"], keep["wd1_raw"]
    a = d["a"]
    with ExitStack() as ctx:
        def sb(name, shape, dt):
            return ctx.enter_context(nc.sbuf_tensor(name, shape, dt))

        def pair(name, shape):
            return sb(name + "_hi", shape, F32R), sb(name + "_lo", shape, F32R)

        banks = [ctx.enter_context(nc.psum_tensor(f"f1_bank{i}", [P, 512], F32)) for i in range(8)]
        g_ps, u_ps, down_ps, mix_ps, misc = banks[0:2], banks[2:4], banks[4:6], banks[6], banks[7]

        wgu = [t[:].rearrange("p (m c i) -> p m c i", m=2, c=DC) for t in w]
        wd = pair("wd1", [P, CH1, D])
        wr = sb("f1_wr", [P, DC, E], F32)
        xn = sb("f1_xn", [P, GT, D], F32)
        xt32 = sb("f1_xt32", [P, DC, GN], F32)
        xt = pair("f1_xt", [P, DC, GN])
        sg = sb("f1_sg", [P, 2, GN], F32)
        prod = sb("f1_prod", [P, 2, GN], F32)
        hid = sb("f1_hid", [P, 2, GN], F32)
        hs = pair("f1_hs", [P, 2, GN])
        logit = sb("f1_logit", [P, GT, E], F32)
        lmax = sb("f1_lmax", [P, GT], F32)
        expo = sb("f1_expo", [P, GT, E], F32)
        esum = sb("f1_esum", [P, GT], F32)
        score = sb("f1_score", [P, GT, E], F32)
        above = sb("f1_above", [P, GT, E, E], F32)
        same = sb("f1_same", [P, GT, E, E], F32)
        rank = sb("f1_rank", [P, GT, E], F32)
        weight = sb("f1_weight", [P, GT, E], F32)
        parts = sb("f1_parts", [P, GT, 2, E], F32R)
        parts_t = sb("f1_parts_t", [2 * E, GN], F32R)
        earlier = sb("f1_earlier", [P, E, E], F32)
        sel_e = sb("f1_sel_e", [2 * E, CHR, P], F32R)
        sel_a = sb("f1_sel_a", [2 * E, 2, CHR * P], F32)

        wr_loaded, consts, whi_ready, w_ready = (sem("f1_" + n) for n in ("wr_loaded", "consts", "whi_ready", "w_ready"))
        xn_ready, xt_done, xt32_ready, xhi_ready, xt_ready = (
            sem("f1_" + n) for n in ("xn_ready", "xt_done", "xt32_ready", "xhi_ready", "xt_ready"))
        gate_done, up_done, silu_ready, prod_ready, mix_done, hid_ready, hshi_ready, hs_ready, chunk_done = (
            sem("f1_" + n) for n in ("gate_done", "up_done", "silu_ready", "prod_ready", "mix_done", "hid_ready", "hshi_ready",
                                     "hs_ready", "chunk_done"))
        logit_done, r_steps, exp_ready, parts_ready, parts_done, parts_t_ready = (
            sem("f1_" + n) for n in ("logit_done", "r_steps", "exp_ready", "parts_ready", "parts_done", "parts_t_ready"))
        x_ready = sem("f1_x_ready")
        R_STEPS = 11

        def rows(c):
            return P if c < CH1 - 1 else LASTM

        def multiplied(eng, g, c):
            q, c = divmod(c, CH1)
            if g.known and g.n + q < 0:
                return
            if c < CHR:
                eng.wait_ge(prod_ready, (g.n + q) * CHR + (c + 1))
            else:
                eng.wait_ge(hid_ready, (g.n + q) * CH1 + (c + 1))

        block = ctx.enter_context(nc.Block())

        @block.sync
        def _(sp):
            sp.dma_start(wr[:], a["L1_ffn_W_router"].rearrange("(c p) e -> p c e", p=P)).then_inc(wr_loaded, 16)

        @block.tensor
        def _(pe):
            def transposes(g, dc):
                if dc == 0:
                    after(pe, xn_ready, g)
                    after(pe, parts_t_ready, g.plus(-1))
                else:
                    after(pe, xt32_ready, g, 2, 1)
                for k in range(GT):
                    mm = pe.transpose(misc[:, k * P:(k + 1) * P], xn[:, k, dc * P:(dc + 1) * P], ident[:])
                mm.then_inc(xt_done, 1)

            def router(g):
                after(pe, xt32_ready, g, 2)
                for k in range(GT):
                    for dc in range(DC):
                        mm = pe.matmul(misc[:, k * E:(k + 1) * E], lhsT=xt32[:, dc, k * P:(k + 1) * P], rhs=wr[:, dc],
                                       start=(dc == 0), stop=(dc == DC - 1))
                mm.then_inc(logit_done, 1)

            def weights(g):
                after(pe, parts_ready, g, 2)
                for k in range(GT):
                    mm = pe.transpose(misc[0:2 * E, k * P:(k + 1) * P], raw(parts[:, k].rearrange("p a e -> p (a e)")), ident[:])
                mm.then_inc(parts_done, 1)

            def hidden(g, c):
                n, slot = g.n * CH1 + c, c % 2
                if c == 0:
                    after(pe, xt_ready, g)
                r = rows(c)
                for m, ps, done in ((0, g_ps, gate_done), (1, u_ps, up_done)):
                    if m == 1:
                        multiplied(pe, g, c - 2)
                    elif not (g.known and n < 2):
                        pe.wait_ge(silu_ready, n - 1)
                    for dc in range(DC):
                        lhs = [t[:, m, dc, c * P:c * P + r] for t in wgu]
                        mm = product3(pe, ps[slot][0:r], lhs, (xt[0][:, dc], xt[1][:, dc]), dc == 0, dc == DC - 1)
                    mm.then_inc(done, 1)
                if c < CHR:
                    if c == 0:
                        after(pe, parts_t_ready, g)
                        after(pe, hid_ready, g.plus(-1), CH1)
                    else:
                        pe.wait_ge(hid_ready, n)
                    pe.matmul(mix_ps[:], lhsT=sel_e[:, c], rhs=parts_t[:], start=True, stop=True).then_inc(mix_done, 1)

            def down(g, c):
                if g.known and g.n < 0:
                    return
                n, r = g.n * CH1 + c, rows(c)
                if c == 0:
                    after(pe, x_ready, g.plus(-1), GT)
                pe.wait_ge(hs_ready, n + 1)
                for k in range(GT):
                    cols = slice(k * P, (k + 1) * P)
                    mm = product3(pe, down_ps[k // 2][:, (k % 2) * D:(k % 2 + 1) * D],
                                  [t[0:r, c % 2, cols] for t in hs], [t[0:r, c] for t in wd],
                                  c == 0 and k % 2 == 0, c == CH1 - 1, skip_group_check=True)
                mm.then_inc(chunk_done, 1)

            def group(g):
                for c in range(CH1):
                    hidden(g, c)
                    if c < 2:
                        down(g.plus(-1), CH1 - 2 + c)
                    else:
                        down(g, c - 2)
                    if c == 3:
                        transposes(g.plus(1), 0)
                    if c == 5:
                        transposes(g.plus(1), 1)
                    if c == 7:
                        router(g.plus(1))
                    if c == 11:
                        weights(g.plus(1))

            first = Step(0, 0, 1)
            pe.wait_ge(consts, 5)
            pe.wait_ge(wr_loaded, 16)
            transposes(first, 0)
            transposes(first, 1)
            router(first)
            weights(first)
            pe.wait_ge(w_ready, CH1)
            group(first)
            with pe.Fori(1, GROUPS) as r:
                group(Step(r, 0, 1))
            for c in range(2):
                down(Step(GROUPS - 1, 0, 1), CH1 - 2 + c)

        @block.scalar
        def _(act):
            norm.scalar(act)

            def transposed(g, dc):
                after(act, xt_done, g, 2, dc + 1)
                after(act, xt_ready, g.plus(-1))
                after(act, logit_done, g.plus(-1))
                act.activation(xt32[:, dc], misc[:], ACT.Copy).then_inc(xt32_ready, 1)

            def high(g):
                after(act, xt32_ready, g, 2)
                after(act, up_done, g.plus(-1), CH1)
                for dc in range(DC):
                    op = act.activation(xt[0][:, dc], xt32[:, dc], ACT.Copy)
                op.then_inc(xhi_ready, 1)

            def exponentials(g):
                after(act, r_steps, g, R_STEPS, 3)
                act.activation(expo[:], logit[:], ACT.Exp).then_inc(exp_ready, 1)

            def hidden_high(n, c, start):
                act.wait_ge(hid_ready, n + 1)
                if not start:
                    act.wait_ge(chunk_done, n - 1)
                act.activation(hs[0][0:rows(c), c % 2], hid[0:rows(c), c % 2], ACT.Copy).then_inc(hshi_ready, 1)

            def group(g):
                for c in range(CH1):
                    n, r = g.n * CH1 + c, rows(c)
                    zero = g.known and g.n == 0
                    act.wait_ge(gate_done, n + 1)
                    multiplied(act, g, c - 2)
                    act.activation(sg[0:r, c % 2], g_ps[c % 2][0:r], ACT.Silu).then_inc(silu_ready, 1)
                    if not (zero and c == 0):
                        hidden_high(n - 1, (c - 1) % CH1, zero and c < 3)
                    if c == 4:
                        transposed(g.plus(1), 0)
                    if c == 6:
                        transposed(g.plus(1), 1)
                    if c == 9:
                        exponentials(g.plus(1))
                high(g.plus(1))

            first = Step(0, 0, 1)
            transposed(first, 0)
            transposed(first, 1)
            high(first)
            act.wait_ge(keep["w1_loaded"], 16 * W1_LOADS)
            exponentials(first)
            for c in range(CH1):
                act.activation(wd[0][0:rows(c), c], wd_raw[0:rows(c), c], ACT.Copy).then_inc(whi_ready, 1)
            group(first)
            with act.Fori(1, GROUPS) as r:
                group(Step(r, 0, 1))
            hidden_high(GROUPS * CH1 - 1, CH1 - 1, False)

        @block.gpsimd
        def _(pool):
            pool.memset(earlier[:], 1.0)
            pool.memset(sel_a[:], 1.0).then_inc(consts, 1)
            pool.wait_ge(consts, 1)
            pool.affine_select(out=earlier[:], in_=earlier[:], compare_op=ALU.is_gt, fill=0.0, base=0,
                               pattern=[[1, E], [-1, E]], channel_multiplier=0)
            for m in range(2):
                v = sel_a[:, m]
                first = DE * E * m
                pool.affine_select(out=v, in_=v, compare_op=ALU.is_ge, fill=0.0, base=first,
                                   pattern=[[1, CHR * P]], channel_multiplier=-DE)
            pool.memset(lmax[:], 0.0).then_inc(consts, 1)
            pool.wait_ge(consts, 2)
            for m in range(2):
                v = sel_a[:, m]
                pool.affine_select(out=v, in_=v, compare_op=ALU.is_ge, fill=0.0, base=DE - 1 - DE * E * m,
                                   pattern=[[-1, CHR * P]], channel_multiplier=DE)
            pool.memset(esum[:], 0.0).then_inc(consts, 1)
            pool.wait_ge(consts, 3)
            pool.tensor_tensor(sel_a[:, 0], sel_a[:, 0], sel_a[:, 1], ALU.add).then_inc(consts, 1)
            pool.wait_ge(consts, 4)
            pool.tensor_copy(sel_e[:].rearrange("k c p -> k (c p)"), sel_a[:, 0]).then_inc(consts, 1)

            for c in range(CH1):
                pool.wait_ge(whi_ready, c + 1)
                r = rows(c)
                pool.tensor_tensor(wd[1][0:r, c], wd_raw[0:r, c], raw(wd[0][0:r, c]), ALU.subtract).then_inc(w_ready, 1)

            def group(g):
                for c in range(CH1):
                    r = rows(c)
                    pool.wait_ge(hshi_ready, g.n * CH1 + (c + 1))
                    pool.tensor_tensor(hs[1][0:r, c % 2], hid[0:r, c % 2], raw(hs[0][0:r, c % 2]), ALU.subtract).then_inc(hs_ready, 1)

            with pool.Fori(0, GROUPS) as r:
                group(Step(r, 0, 1))

        @block.vector
        def _(dve):
            norm.vector(dve)

            def low(g):
                after(dve, xhi_ready, g)
                for dc in range(DC):
                    op = dve.tensor_tensor(xt[1][:, dc], xt32[:, dc], raw(xt[0][:, dc]), ALU.subtract)
                op.then_inc(xt_ready, 1)

            def stage(g, k, op):
                op.then_inc(r_steps, 1)
                after(dve, r_steps, g, R_STEPS, k)

            def softmax_start(g):
                after(dve, logit_done, g)
                after(dve, exp_ready, g.plus(-1))
                stage(g, 1, dve.tensor_copy(logit[:].rearrange("p k e -> p (k e)"), misc[:, 0:GT * E]))
                stage(g, 2, dve.tensor_reduce(lmax[:], logit[:], AX_X, ALU.max))
                stage(g, 3, dve.tensor_tensor(logit[:], logit[:], lmax[:].unsqueeze(2).to_broadcast([P, GT, E]), ALU.subtract))

            def top2(g):
                after(dve, exp_ready, g)
                stage(g, 4, dve.tensor_reduce(esum[:], expo[:], AX_X, ALU.add))
                stage(g, 5, dve.reciprocal(lmax[:], esum[:]))
                stage(g, 6, dve.tensor_tensor(score[:], expo[:], lmax[:].unsqueeze(2).to_broadcast([P, GT, E]), ALU.mult))
                for k in range(GT):
                    other = score[:, k].unsqueeze(1).to_broadcast([P, E, E])
                    own = score[:, k].unsqueeze(2).to_broadcast([P, E, E])
                    dve.tensor_tensor(above[:, k], other, own, ALU.is_gt)
                    op = dve.tensor_tensor(same[:, k], other, own, ALU.is_equal)
                stage(g, 7, op)
                for k in range(GT):
                    op = dve.tensor_tensor(same[:, k], same[:, k], earlier[:], ALU.mult)
                stage(g, 8, op)
                flat = "p k a b -> p (k a b)"
                stage(g, 9, dve.tensor_tensor(above[:].rearrange(flat), above[:].rearrange(flat), same[:].rearrange(flat), ALU.add))
                stage(g, 10, dve.tensor_reduce(rank[:].rearrange("p k e -> p (k e)"), above[:].rearrange("p k a b -> p (k a) b"), AX_X, ALU.add))
                stage(g, 11, dve.scalar_tensor_tensor(weight[:], rank[:], 2.0, score[:], ALU.is_lt, ALU.mult))
                after(dve, parts_done, g.plus(-1))
                dve.tensor_copy(parts[:, :, 0], weight[:]).then_inc(parts_ready, 1)
                after(dve, parts_ready, g, 2, 1)
                dve.tensor_tensor(parts[:, :, 1], weight[:], raw(parts[:, :, 0]), ALU.subtract).then_inc(parts_ready, 1)

            def parts_turned(g):
                after(dve, parts_done, g)
                after(dve, mix_done, g.plus(-1), CHR)
                dve.tensor_copy(parts_t[:], misc[0:2 * E, :]).then_inc(parts_t_ready, 1)

            def chunk(g, c):
                n, r, slot = g.n * CH1 + c, rows(c), c % 2
                zero = g.known and g.n == 0 and c < 2
                routed = c < CHR
                dve.wait_ge(silu_ready, n + 1)
                dve.wait_ge(up_done, n + 1)
                if not zero:
                    dve.wait_ge(hs_ready, n - 1)
                out = prod if routed else hid
                done = prod_ready if routed else hid_ready
                dve.tensor_tensor(out[0:r, slot], sg[0:r, slot], u_ps[slot][0:r], ALU.mult).then_inc(done, 1)
                if routed:
                    multiplied(dve, g, c)
                    dve.wait_ge(mix_done, g.n * CHR + (c + 1))
                    dve.tensor_tensor(hid[:, slot], prod[:, slot], mix_ps[:], ALU.mult).then_inc(hid_ready, 1)

            def residual(g):
                after(dve, chunk_done, g, CH1)
                for k in range(GT):
                    t = g.n * GT + k
                    dve.scalar_tensor_tensor(at(x_all, t), down_ps[k // 2][:, (k % 2) * D:(k % 2 + 1) * D], gates[:, 3:4],
                                             at(x_all, t), ALU.mult, ALU.add).then_inc(x_ready, 1)

            def group(g):
                for c in range(CH1):
                    chunk(g, c)
                    if c == 1:
                        if not (g.known and g.n == 0):
                            residual(g.plus(-1))
                        after(dve, xt_done, g, 2)
                        normalised(dve, None, norm, xn, x_all, g.plus(1), xn_ready)
                    if c == 8:
                        softmax_start(g.plus(1))
                    if c == 10:
                        top2(g.plus(1))
                    if c == 12:
                        parts_turned(g.plus(1))
                low(g.plus(1))

            first = Step(0, 0, 1)
            normalised(dve, None, norm, xn, x_all, first, xn_ready)
            low(first)
            softmax_start(first)
            dve.wait_ge(consts, 4)
            top2(first)
            parts_turned(first)
            group(first)
            with dve.Fori(1, GROUPS) as r:
                group(Step(r, 0, 1))
            residual(Step(GROUPS - 1, 0, 1))
            dve.wait_ge(x_ready, TILES)
    norm.used += 6


def finish(nc, sem, keep, d):
    x_all = keep["x_all"]
    stored = sem("stored")
    with nc.Block() as block:
        @block.sync
        def _(sp):
            sp.dma_start(d["out"].rearrange("t p n -> p t n"), x_all[:, 0:TILES]).then_inc(stored, 16)
            sp.wait_ge(stored, 16)


def flamingo(nc, a, out, stages=4):
    d = {
        "x": a["x"].rearrange("(t b) s n -> t (b s) n", b=2),
        "ctx": a["ctx_2048"].rearrange("(t b) s n -> t (b s) n", b=2),
        "wq": a["L0_xattn_W_q"], "wk": a["L0_xattn_W_k"], "wv": a["L0_xattn_W_v"], "wo": a["L0_xattn_W_o"],
        "g_xattn": a["g_xattn"].partition_broadcast(P), "g_ffn": a["g_ffn"].partition_broadcast(P),
        "gamma": a["L1_xattn_gamma"].partition_broadcast(P),
        "kop": nc.dram_tensor("kop_rows", (TILES, UNITS, UROWS, D), F32).ap(),
        "qop": nc.dram_tensor("qop_rows", (2, UNITS, UROWS, D), F32).ap(),
        "out": out.rearrange("(t b) s n -> t (b s) n", b=2),
        "a": a,
    }
    with ExitStack() as ctx:
        def sb(name, shape, dt):
            return ctx.enter_context(nc.sbuf_tensor(name, shape, dt))

        def sem(name):
            return ctx.enter_context(nc.semaphore(name))

        keep = {
            "x_all": sb("x_all", [P, XT, D], F32),
            "norm": Norm(sb, sem),
            "ident": sb("ident", [P, P], F32),
            "gates": sb("gates", [P, 4], F32),
            "sel_out": sb("sel_out", [P, 32], F32),
            "sel_den": sb("sel_den", [P, 32], F32),
        }
        with ExitStack() as early:
            keep["w0_raw"] = early.enter_context(nc.sbuf_tensor("w0_raw", [P, 2, DC, I0], F32))
            keep["wd0_raw"] = early.enter_context(nc.sbuf_tensor("wd0_raw", [P, QUAD0, 4, D], F32))
            keep["w0_loaded"] = sem("w0_loaded")
            attention0(nc, sem, keep, d)
            if stages > 1:
                feed_forward0(nc, sem, keep, d)
        keep["w1_raw"] = sb("w1_raw", [P, 4 * I1], F32)
        keep["wd1_raw"] = sb("wd1_raw", [P, CH1, D], F32)
        keep["w1"] = sb("w1_hi", [P, 4 * I1], F32R), sb("w1_lo", [P, 4 * I1], F32R)
        keep["w1_loaded"] = sem("w1_loaded")
        if stages > 2:
            attention1(nc, sem, keep, d)
        if stages > 3:
            feed_forward1(nc, sem, keep, d)
        finish(nc, sem, keep, d)


_INS = ['x', 'ctx_2048', 'g_xattn', 'g_ffn', 'L0_xattn_W_q', 'L0_xattn_W_k', 'L0_xattn_W_v', 'L0_xattn_W_o',
        'L0_ffn_w_gate', 'L0_ffn_w_up', 'L0_ffn_w_down', 'L1_xattn_gamma', 'L1_ffn_W_router', 'L1_ffn_We_gate',
        'L1_ffn_We_up', 'L1_ffn_We_down', 'L1_ffn_Ws_gate', 'L1_ffn_Ws_up', 'L1_ffn_Ws_down']


def kernel(**inputs):
    import numpy as _np
    import concourse.bacc as _bacc
    from concourse import mybir as _mybir
    from concourse.bass_utils import run_bass_kernel_spmd as _run

    nc = _bacc.Bacc("TRN2", target_bir_lowering=False, num_devices=1)
    arrays, args = {}, {}
    for name in _INS:
        a = _np.ascontiguousarray(inputs[name])
        if a.ndim == 0:
            a = a.reshape(1)
        arrays[f"in_{name}"] = a
        args[name] = nc.dram_tensor(f"in_{name}", a.shape, _mybir.dt.from_np(a.dtype), kind="ExternalInput").ap()
    out = nc.dram_tensor("out_x", (BATCH, SEQ, D), F32, kind="ExternalOutput").ap()
    flamingo(nc, args, out)
    r = _run(nc, [arrays], core_ids=[0])
    return r.results[0]["out_x"]
```

```python
from contextlib import ExitStack

import concourse.bass as bass
from concourse import mybir

F32 = mybir.dt.float32
F32R = mybir.dt.float32r
BF16 = mybir.dt.bfloat16
ACT = mybir.ActivationFunctionType
ALU = mybir.AluOpType
AX_X = mybir.AxisListType.X

P = 128
BATCH, SEQ, D = 32, 64, 256
TOK = BATCH * SEQ
TILES = TOK // P
DC = D // P
EPS = 1e-5

H0 = 8
N0 = D // H0
SCALE0 = float(N0) ** -0.5

H1 = 8
D1 = SEQ // H1
SCALE1 = float(D1) ** -0.5
UNITS = P // D1
QUADS = UNITS // 4
QROWS = 3 * D1
UROWS = 32
MROW = P - 1
HALF = UNITS // 2

GT = 4
GN = GT * P
GROUPS = TILES // GT
XT = TILES + GT

I0 = 1024
W0_COLS = 2 * I0 // TILES
QUAD0 = I0 // (4 * P)
E, DE, DS = 8, 176, 352
I1 = E * DE + DS
CH1 = -(-I1 // P)
CHR = E * DE // P
LASTM = I1 - (CH1 - 1) * P


class Step:

    def __init__(self, rnd, slot, unroll):
        self.rnd, self.slot, self.unroll = rnd, slot, unroll
        self.known = isinstance(rnd, int)
        self.n = rnd * unroll + slot

    def plus(self, k):
        q, slot = divmod(self.slot + k, self.unroll)
        return Step(self.rnd + q, slot, self.unroll)

    def inside(self, count):
        return not self.known or 0 <= self.n < count


def run_steps(eng, body, count, lag, unroll):
    head = -(-lag // unroll)
    tail = count // unroll
    for n in range(head * unroll):
        body(Step(n // unroll, n % unroll, unroll))
    with eng.Fori(head, tail) as r:
        for slot in range(unroll):
            body(Step(r, slot, unroll))
    for n in range(tail * unroll, count + lag):
        body(Step(n // unroll, n % unroll, unroll))


def after(eng, sem, step, per=1, k=None):
    if step.known and step.n < 0:
        return
    eng.wait_ge(sem, step.n * per + (per if k is None else k))


def after_dma(eng, sems, step, transfers=1):
    if step.known and step.rnd < 0:
        return
    eng.wait_ge(sems[step.slot], (step.rnd + 1) * (16 * transfers))


def at(tensor, n):
    if isinstance(n, int):
        return tensor[:, n]
    v = tensor[:, bass.ds(n, 1)]
    return v.rearrange("p o n -> p (o n)")


def dram_at(ap, n):
    if isinstance(n, int):
        return ap[n]
    return ap[bass.ds(n, 1)].rearrange("o p n -> (o p) n")


def raw(ap):
    return ap.bitcast(F32)


def product3(pe, out, lhs, rhs, first, last, **kw):
    (lh, ll), (rh, rl) = lhs, rhs
    pe.matmul(out, lhsT=lh, rhs=rh, start=first, stop=False, **kw)
    pe.matmul(out, lhsT=lh, rhs=rl, start=False, stop=False, **kw)
    return pe.matmul(out, lhsT=ll, rhs=rh, start=False, stop=last, **kw)


class Norm:

    def __init__(self, sb, sem):
        self.stats = sb("stats", [P, XT, 6], F32)
        self.sum2, self.dif, self.m2, self.sq, self.var, self.std, self.rstd, self.shift = (
            sb(f"ln_{n}", [P, XT], F32) for n in ("sum2", "dif", "m2", "sq", "var", "std", "rstd", "shift"))
        self.eps = sb("eps", [P, 1], F32)
        self.steps = sem("ln_steps")
        self.used = self.rooted = 0

    def vector(self, dve, tiles=slice(0, XT)):
        st, n = self.stats, self.used
        self.used += 6
        even, odd = st[:, tiles, 1], st[:, tiles, 4]
        sum2, dif, m2, sq, var, std, rstd, shift = (
            t[:, tiles] for t in (self.sum2, self.dif, self.m2, self.sq, self.var, self.std, self.rstd, self.shift))
        dve.tensor_tensor(sum2, even, odd, ALU.add)
        dve.tensor_tensor(dif, even, odd, ALU.subtract)
        dve.tensor_tensor(m2, st[:, tiles, 2], st[:, tiles, 5], ALU.add).then_inc(self.steps, 1)
        dve.wait_ge(self.steps, n + 1)
        dve.scalar_tensor_tensor(sq, dif, 0.25, dif, ALU.mult, ALU.mult).then_inc(self.steps, 1)
        dve.wait_ge(self.steps, n + 2)
        dve.scalar_tensor_tensor(var, m2, 1.0 / D, sq, ALU.mult, ALU.add).then_inc(self.steps, 1)
        dve.wait_ge(self.steps, n + 4)
        dve.reciprocal(rstd, std).then_inc(self.steps, 1)
        dve.wait_ge(self.steps, n + 5)
        dve.scalar_tensor_tensor(shift, sum2, -0.5, rstd, ALU.mult, ALU.mult).then_inc(self.steps, 1)
        dve.wait_ge(self.steps, n + 6)

    def scalar(self, act, tiles=slice(0, XT)):
        act.wait_ge(self.steps, self.rooted + 3)
        self.rooted += 6
        act.activation(self.std[:, tiles], self.var[:, tiles], ACT.Sqrt, bias=self.eps[:, 0:1]).then_inc(self.steps, 1)

    def apply(self, dve, out, x_all, n):
        return dve.tensor_scalar(out, at(x_all, n), column(self.rstd, n), column(self.shift, n), ALU.mult, ALU.add)


def columns(n, width):
    return slice(n * width, (n + 1) * width) if isinstance(n, int) else bass.ds(n * width, width)


def column(tensor, n):
    return tensor[:, n:n + 1] if isinstance(n, int) else tensor[:, bass.ds(n, 1)]


def attention0(nc, sem, keep, d):
    x_all, norm, ident, gates = keep["x_all"], keep["norm"], keep["ident"], keep["gates"]
    sel_out, sel_den = keep["sel_out"], keep["sel_den"]
    with ExitStack() as ctx:
        def sb(name, shape, dt):
            return ctx.enter_context(nc.sbuf_tensor(name, shape, dt))

        banks = [ctx.enter_context(nc.psum_tensor(f"a0_bank{i}", [P, 512], F32)) for i in range(8)]
        qk_ps, v_ps, s_ps = banks[0:2], banks[2], banks[3:5]
        pt_ps, o_ps, proj_ps = banks[5], banks[6], banks[7]

        w_raw = sb("w_raw", [P, 5, P], F32)
        w_t = sb("w_t", [P, 5, P], F32)
        gate_in = sb("gate_in", [P, 5], F32)
        ctx_t = sb("ctx_t", [P, 2, D], F32)
        xn = sb("xn", [P, 2, D], F32)
        xn_late = sb("xn_late", [P, 2, D], F32)
        q_t = sb("q_t", [P, 2, DC, P], F32)
        k_m = sb("k_m", [P, 2, DC, 2, 4, SEQ], F32)
        v_m = sb("v_m", [P, 2, 2, 4, 2, N0], F32)
        smax = sb("smax", [P, 2, H0], F32)
        shifted = sb("shifted", [P, 2, H0 * SEQ], F32)
        prob = sb("prob", [P, 2, H0 * SEQ], F32)
        den = sb("den", [P, 2, H0], F32)
        rden = sb("rden", [P, 2, H0], F32)
        p_t = sb("p_t", [P, 2, 4 * P], F32)
        head = sb("head", [P, 2, D], F32)
        mix = sb("mix", [P, 2, D], F32)
        k_hi = sb("k_hi", [P, 2, D], F32R)
        k_lo = sb("k_lo", [P, 2, D], F32R)

        zeroed, ident_steps, w_loaded, x_loaded, gate_loaded = (
            sem("zeroed"), sem("ident_steps"), sem("w_loaded"), [sem("x_loaded0"), sem("x_loaded1")], sem("gate_loaded"))
        wt_done, wt_ready, gate_steps, stats0 = sem("wt_done"), sem("wt_ready"), sem("gate_steps"), sem("stats0")
        ctx_loaded = [sem("ctx_loaded0"), sem("ctx_loaded1")]
        kop_written = [sem("kop_written0"), sem("kop_written1")]
        w0_raw, w0, w0_loaded, w0_hi, w0_lo = keep["w0_raw"], keep["w0"], keep["w0_loaded"], sem("w0_hi_ready"), sem("w0_lo_ready")
        xn_ready, qk_done, v_done, q_ready, k_ready, v_ready = (
            sem(n) for n in ("xn_ready", "qk_done", "v_done", "q_ready", "k_ready", "v_ready"))
        score_done, smax_ready, shift_ready, prob_ready, den_ready, rden_ready = (
            sem(n) for n in ("score_done", "smax_ready", "shift_ready", "prob_ready", "den_ready", "rden_ready"))
        pt_done, pt_ready, o_done, head_ready, mix_ready, proj_done, x_ready, st_ready = (
            sem(n) for n in ("pt_done", "pt_ready", "o_done", "head_ready", "mix_ready", "proj_done", "x_ready", "st_ready"))
        khi_ready, klo_ready = sem("khi_ready"), sem("klo_ready")

        block = ctx.enter_context(nc.Block())

        @block.sync
        def _(sp):
            def load_x(part, tiles):
                sp.dma_start(x_all[:, tiles], d["x"][tiles].rearrange("t p n -> p t n")).then_inc(x_loaded[part], 16)

            load_x(0, slice(0, GT))
            sp.wait_ge(zeroed, 1)
            for m, w in ((0, "wq"), (1, "wk"), (2, "wo")):
                for b in range(2):
                    r = slice(b * SEQ, (b + 1) * SEQ)
                    sp.dma_start(w_raw[r, m, r], d[w]).then_inc(w_loaded, 16)
            for b in range(2):
                for h in range(2):
                    sp.dma_start(w_raw[h * SEQ:(h + 1) * SEQ, 3 + b, b * SEQ:(b + 1) * SEQ], d["wv"]).then_inc(w_loaded, 16)

            def step(s):
                if s.inside(TILES):
                    after(sp, qk_done, s.plus(-2))
                    after(sp, v_done, s.plus(-2))
                    after(sp, klo_ready, s.plus(-2))
                    sp.dma_start(ctx_t[:, s.slot], dram_at(d["ctx"], s.n)).then_inc(ctx_loaded[s.slot], 16)
                    if s.known and s.n == 0:
                        load_x(1, slice(GT, TILES))
                t = s.plus(-1)
                if t.inside(TILES):
                    after(sp, khi_ready, t)
                    after(sp, klo_ready, t)
                    rows = d["kop"].rearrange("t u r n -> t r u n")
                    rows = rows[t.n] if t.known else rows[bass.ds(t.n, 1)].rearrange("o r u n -> (o r) u n")
                    for part, src in enumerate((k_hi, k_lo, k_hi)):
                        dst = rows[part * D1:(part + 1) * D1].rearrange("r u n -> u r n")
                        sp.dma_start(dst, raw(src[:, t.slot])).then_inc(kop_written[t.slot], 16)
                if s.inside(TILES):
                    a = d["a"][("L0_ffn_w_gate", "L0_ffn_w_up")[s.slot]].rearrange("(c p) i -> p c i", p=P)
                    cols = columns(s.rnd, W0_COLS)
                    sp.dma_start(w0_raw[:, s.slot, :, cols], a[:, :, cols]).then_inc(w0_loaded[s.slot], 16)

            run_steps(sp, step, TILES, 2, 2)
            sp.dma_start(keep["wd0_raw"][:], d["a"]["L0_ffn_w_down"].rearrange("(c p j) n -> p c j n", p=P, j=4)).then_inc(keep["wd0_loaded"], 16)
            for slot in range(2):
                sp.wait_ge(kop_written[slot], 16 * 3 * TILES // 2)

        @block.gpsimd
        def _(pool):
            pool.memset(w_raw[:], 0.0).then_inc(zeroed, 1)
            pool.memset(ident[:], 0.0)
            pool.memset(sel_out[:], 0.0)
            pool.memset(sel_den[:], 0.0).then_inc(ident_steps, 1)
            pool.wait_ge(ident_steps, 1)
            pool.affine_select(out=ident[:], in_=ident[:], compare_op=ALU.not_equal, fill=1.0, base=0,
                               pattern=[[-1, P]], channel_multiplier=1).then_inc(ident_steps, 1)
            pool.memset(k_m[:], 0.0)
            pool.memset(v_m[:], 0.0).then_inc(zeroed, 1)
            v = sel_out[:].rearrange("p (u r) -> p u r", u=4)
            pool.affine_select(out=v, in_=v, compare_op=ALU.not_equal, fill=1.0, base=0,
                               pattern=[[-UROWS, 4], [-1, D1]], channel_multiplier=1)
            v = sel_den[:].rearrange("p (u r) -> p u r", u=4)
            pool.affine_select(out=v, in_=v, compare_op=ALU.not_equal, fill=1.0, base=-D1,
                               pattern=[[-UROWS, 4], [0, D1]], channel_multiplier=1).then_inc(ident_steps, 1)
            pool.memset(x_all[:, TILES:XT], 0.0)
            pool.memset(norm.stats[:, TILES:XT], 0.0)
            pool.memset(norm.eps[:], EPS).then_inc(ident_steps, 1)

            def step(s):
                if s.plus(-1).inside(TILES):
                    after_dma(pool, w0_loaded, s.plus(-1))
                if s.inside(TILES):
                    after(pool, khi_ready, s)
                    after_dma(pool, kop_written, s.plus(-2), 3)
                    pool.tensor_tensor(k_lo[:, s.slot], ctx_t[:, s.slot], raw(k_hi[:, s.slot]), ALU.subtract).then_inc(klo_ready, 1)
                t = s.plus(-1)
                if t.inside(TILES):
                    m, r, n = t.slot, columns(t.rnd, W0_COLS), columns(t.rnd, W0_COLS // 4)
                    src = w0_raw[:, m, :, r].rearrange("p c (g j) -> p c j g", j=4)
                    pool.tensor_copy(w0[0][:, m, :, :, n], src).then_inc(w0_hi, 1)
                    after(pool, w0_hi, t)
                    pool.tensor_tensor(w0[1][:, m, :, :, n], src, raw(w0[0][:, m, :, :, n]), ALU.subtract).then_inc(w0_lo, 1)
                    after(pool, head_ready, t)
                    after(pool, proj_done, t.plus(-2))
                    pool.tensor_tensor(mix[:, t.slot], xn_late[:, t.slot], head[:, t.slot], ALU.subtract).then_inc(mix_ready, 1)

            run_steps(pool, step, TILES, 2, 2)
            pool.wait_ge(w0_lo, TILES)

        @block.scalar
        def _(act):
            for m, g in enumerate(("g_xattn", "g_ffn", "gamma")):
                w = 2 if m < 2 else 1
                act.dma_start(gate_in[:, 2 * m:2 * m + w], d[g]).then_inc(gate_loaded, 16)
            act.wait_ge(gate_loaded, 48)
            act.activation(gates[:], gate_in[:, 0:4], ACT.Tanh).then_inc(gate_steps, 1)
            act.wait_ge(ident_steps, 4)
            norm.scalar(act, slice(0, GT))
            act.wait_ge(zeroed, 2)
            act.wait_ge(wt_done, 1)
            act.activation(w_t[:, 0:4].rearrange("p m n -> p (m n)"), banks[0][:], ACT.Copy)
            act.activation(w_t[:, 4], banks[1][:, 0:P], ACT.Copy).then_inc(wt_ready, 1)

            def step(s):
                t = s.plus(-1)
                if s.inside(TILES):
                    after(act, qk_done, s)
                    after(act, score_done, s.plus(-2))
                    act.activation(q_t[:, s.slot].rearrange("p c n -> p (c n)"), qk_ps[s.slot][:, 0:D], ACT.Copy).then_inc(q_ready, 1)
                    for h in range(4):
                        r = slice(h * N0, (h + 1) * N0)
                        src = qk_ps[s.slot][r, D:2 * D].rearrange("p (c b e) -> p c b e", c=DC, b=2)
                        op = act.activation(k_m[r, s.slot, :, :, h], src, ACT.Copy)
                    op.then_inc(k_ready, 1)
                if t.inside(TILES):
                    after(act, pt_done, t)
                    after(act, o_done, t.plus(-2))
                    act.activation(p_t[:, t.slot], pt_ps[:], ACT.Copy).then_inc(pt_ready, 1)
                if s.inside(TILES):
                    after_dma(act, ctx_loaded, s)
                    after_dma(act, kop_written, s.plus(-2), 3)
                    act.activation(k_hi[:, s.slot], ctx_t[:, s.slot], ACT.Copy).then_inc(khi_ready, 1)
                    if s.known and s.n == 1:
                        norm.scalar(act, slice(GT, XT))
                    after(act, shift_ready, s)
                    after(act, pt_done, s.plus(-2))
                    after(act, den_ready, s.plus(-2))
                    act.activation(prob[:, s.slot], shifted[:, s.slot], ACT.Exp, scale=SCALE0).then_inc(prob_ready, 1)

            run_steps(act, step, TILES, 2, 2)

        @block.tensor
        def _(pe):
            pe.wait_ge(w_loaded, 160)
            pe.wait_ge(ident_steps, 2)
            for m in range(4):
                pe.transpose(banks[0][:, m * P:(m + 1) * P], w_raw[:, m], ident[:])
            pe.transpose(banks[1][:, 0:P], w_raw[:, 4], ident[:]).then_inc(wt_done, 1)
            pe.wait_ge(wt_ready, 1)

            def step(s):
                t, u = s.plus(-1), s.plus(-2)
                if s.inside(TILES):
                    after(pe, xn_ready, s)
                    after_dma(pe, ctx_loaded, s)
                    after(pe, q_ready, s.plus(-2))
                    after(pe, k_ready, s.plus(-2))
                    for m, src in ((0, xn), (1, ctx_t)):
                        for c in range(DC):
                            o = (2 * m + c) * P
                            mm = pe.matmul(qk_ps[s.slot][:, o:o + P], lhsT=src[:, s.slot, c * P:(c + 1) * P], rhs=w_t[:, m],
                                           start=True, stop=True)
                    mm.then_inc(qk_done, 1)
                    after(pe, v_ready, s.plus(-1))
                    for b in range(2):
                        mm = pe.matmul(v_ps[:, b * D:(b + 1) * D], lhsT=w_t[:, 3 + b], rhs=ctx_t[:, s.slot], start=True, stop=True)
                    mm.then_inc(v_done, 1)
                if t.inside(TILES):
                    after(pe, prob_ready, t)
                    after(pe, pt_ready, t.plus(-1))
                    for hp in range(4):
                        mm = pe.transpose(pt_ps[:, hp * P:(hp + 1) * P], prob[:, t.slot, hp * P:(hp + 1) * P], ident[:])
                    mm.then_inc(pt_done, 1)
                if s.inside(TILES):
                    after(pe, q_ready, s)
                    after(pe, k_ready, s)
                    after(pe, shift_ready, s.plus(-2))
                    for c in range(DC):
                        for b in range(2):
                            mm = pe.matmul(s_ps[s.slot][b * SEQ:(b + 1) * SEQ, c * D:(c + 1) * D],
                                           lhsT=q_t[:, s.slot, c, b * SEQ:(b + 1) * SEQ],
                                           rhs=k_m[:, s.slot, c, b].rearrange("p h e -> p (h e)"),
                                           start=True, stop=True, tile_position=(0, b * SEQ))
                    mm.then_inc(score_done, 1)
                if t.inside(TILES):
                    after(pe, pt_ready, t)
                    after(pe, v_ready, t)
                    after(pe, head_ready, t.plus(-1))
                    for hp in range(4):
                        for b in range(2):
                            mm = pe.matmul(o_ps[b * SEQ:(b + 1) * SEQ, hp * SEQ:(hp + 1) * SEQ],
                                           lhsT=p_t[:, t.slot, hp * P + b * SEQ:hp * P + (b + 1) * SEQ],
                                           rhs=v_m[:, t.slot, b, hp].rearrange("p h n -> p (h n)"),
                                           start=True, stop=True, tile_position=(0, b * SEQ))
                    mm.then_inc(o_done, 1)
                if u.inside(TILES):
                    after(pe, mix_ready, u)
                    after(pe, x_ready, u.plus(-1))
                    pe.matmul(proj_ps[:, 0:D], lhsT=w_t[:, 2], rhs=mix[:, u.slot], start=True, stop=True).then_inc(proj_done, 1)

            run_steps(pe, step, TILES, 2, 2)

        @block.vector
        def _(dve):
            def statistics(part, tiles):
                dve.wait_ge(x_loaded[part], 16)
                with dve.Fori(tiles.start // GT, tiles.stop // GT) as r:
                    for k in range(GT):
                        t = r * GT + k
                        dve.bn_stats(at(norm.stats, t), at(x_all, t)).then_inc(stats0, 1)
                dve.wait_ge(stats0, tiles.stop)
                norm.vector(dve, slice(tiles.start, XT) if part else tiles)

            dve.wait_ge(ident_steps, 4)
            statistics(0, slice(0, GT))
            dve.wait_ge(gate_steps, 1)
            dve.tensor_tensor(gates[:, 1:2], gates[:, 1:2], gate_in[:, 4:5], ALU.mult).then_inc(gate_steps, 1)
            dve.wait_ge(gate_steps, 2)
            dve.wait_ge(zeroed, 2)

            def normalise(n):
                after(dve, qk_done, n.plus(-2))
                norm.apply(dve, xn[:, n.slot], x_all, n.n).then_inc(xn_ready, 1)

            def step(s):
                t, u, n = s.plus(-1), s.plus(-2), s.plus(1)
                if t.inside(TILES):
                    after(dve, prob_ready, t)
                    dve.tensor_reduce(den[:, t.slot], prob[:, t.slot].rearrange("p (h e) -> p h e", h=H0), AX_X, ALU.add).then_inc(den_ready, 1)
                    after(dve, den_ready, t)
                    dve.reciprocal(rden[:, t.slot], den[:, t.slot]).then_inc(rden_ready, 1)
                if s.inside(TILES):
                    after(dve, v_done, s)
                    after(dve, o_done, s.plus(-2))
                    for h in range(2):
                        r = slice(h * SEQ, (h + 1) * SEQ)
                        src = v_ps[r].rearrange("p (b g h n) -> p b g h n", b=2, g=4, h=2)
                        for b in range(2):
                            op = dve.tensor_copy(v_m[r, s.slot, b, :, h], src[:, b, :, h])
                    op.then_inc(v_ready, 1)
                if s.inside(TILES):
                    normalise(n)
                    after(dve, score_done, s)
                    dve.tensor_reduce(smax[:, s.slot], s_ps[s.slot][:].rearrange("p (h e) -> p h e", h=H0), AX_X, ALU.max).then_inc(smax_ready, 1)
                    after(dve, smax_ready, s)
                    after(dve, prob_ready, s.plus(-2))
                    dve.tensor_tensor(shifted[:, s.slot].rearrange("p (h e) -> p h e", h=H0),
                                      s_ps[s.slot][:].rearrange("p (h e) -> p h e", h=H0),
                                      smax[:, s.slot].unsqueeze(2).to_broadcast([P, H0, SEQ]), ALU.subtract).then_inc(shift_ready, 1)
                if t.inside(TILES):
                    after(dve, mix_ready, t.plus(-2))
                    norm.apply(dve, xn_late[:, t.slot], x_all, t.n)
                    after(dve, o_done, t)
                    after(dve, rden_ready, t)
                    dve.tensor_tensor(head[:, t.slot].rearrange("p (h n) -> p h n", h=H0),
                                      o_ps[:, 0:D].rearrange("p (h n) -> p h n", h=H0),
                                      rden[:, t.slot].unsqueeze(2).to_broadcast([P, H0, N0]), ALU.mult).then_inc(head_ready, 1)
                if u.inside(TILES):
                    after(dve, proj_done, u)
                    dve.scalar_tensor_tensor(at(x_all, u.n), proj_ps[:, 0:D], gates[:, 0:1], at(x_all, u.n), ALU.mult, ALU.add).then_inc(x_ready, 1)
                    after(dve, x_ready, u)
                    dve.bn_stats(at(norm.stats, u.n), at(x_all, u.n)).then_inc(st_ready, 1)
                if s.known and s.n == 1:
                    statistics(1, slice(GT, TILES))

            normalise(Step(0, 0, 2))
            run_steps(dve, step, TILES, 2, 2)
            dve.wait_ge(st_ready, TILES)


def normalised(dve, pe_xn_free, norm, xn, x_all, g, ready):
    for k in range(GT):
        op = norm.apply(dve, xn[:, k], x_all, g.n * GT + k)
    op.then_inc(ready, 1)


def feed_forward0(nc, sem, keep, d):
    x_all, norm, ident, gates = keep["x_all"], keep["norm"], keep["ident"], keep["gates"]
    w, wd_raw = keep["w0"], keep["wd0_raw"]
    with ExitStack() as ctx:
        def sb(name, shape, dt):
            return ctx.enter_context(nc.sbuf_tensor(name, shape, dt))

        def pair(name, shape):
            return sb(name + "_hi", shape, F32R), sb(name + "_lo", shape, F32R)

        banks = [ctx.enter_context(nc.psum_tensor(f"f0_bank{i}", [P, 512], F32)) for i in range(8)]
        g_ps, u_ps, down_ps, xt_ps = banks[0:2], banks[2:4], banks[4:6], banks[6:8]

        wd = pair("wd0", [P, QUAD0, 4, D])
        xn = sb("f0_xn", [P, GT, D], F32)
        xt = pair("f0_xt", [P, DC, GN])
        sg = sb("f0_sg", [P, 2, GN], F32)
        hid = sb("f0_hid", [P, 2, 4, GN], F32)
        mag = sb("f0_mag", [P, 4, GN], F32)
        beat_a, beat_b, beat_c = (sb(f"f0_beat_{n}", [P, 2, GN], BF16) for n in "abc")
        wins = sb("f0_wins", [P, 4, GN], BF16)
        sums = sb("f0_sums", [P, 4, GN], BF16)
        kept = sb("f0_kept", [P, 4, GN], F32)
        hs = pair("f0_hs", [P, 4, GN])

        whi_ready, w_ready = sem("f0_whi_ready"), sem("f0_w_ready")
        xn_ready, xt_done, xhi_ready, xt_ready = sem("f0_xn_ready"), sem("f0_xt_done"), sem("f0_xhi_ready"), sem("f0_xt_ready")
        gate_done, up_done, silu_ready, hid_ready, mag_ready = (
            sem("f0_" + n) for n in ("gate_done", "up_done", "silu_ready", "hid_ready", "mag_ready"))
        beat_ready, wins_ready, sums_ready, kept_ready, hshi_ready, hs_ready = (
            sem("f0_" + n) for n in ("beat_ready", "wins_ready", "sums_ready", "kept_ready", "hshi_ready", "hs_ready"))
        down_done, x_ready, st_ready = sem("f0_down_done"), sem("f0_x_ready"), sem("f0_st_ready")

        block = ctx.enter_context(nc.Block())

        @block.tensor
        def _(pe):
            def transposes(g):
                after(pe, xn_ready, g)
                after(pe, xt_ready, g.plus(-1))
                for dc in range(DC):
                    for k in range(GT):
                        mm = pe.transpose(xt_ps[dc][:, k * P:(k + 1) * P], xn[:, k, dc * P:(dc + 1) * P], ident[:])
                mm.then_inc(xt_done, 1)

            def hidden(g, c):
                if c == 0:
                    after(pe, xt_ready, g)
                for j in range(4):
                    n = g.n * 8 + c * 4 + j
                    slot = j % 2
                    for m, ps, free, done in ((0, g_ps, silu_ready, gate_done), (1, u_ps, hid_ready, up_done)):
                        if not (g.known and n < 2):
                            pe.wait_ge(free, n - 1)
                        for dc in range(DC):
                            mm = product3(pe, ps[slot][:], [part[:, m, dc, j, c * P:(c + 1) * P] for part in w],
                                          (xt[0][:, dc], xt[1][:, dc]), dc == 0, dc == DC - 1)
                        mm.then_inc(done, 1)

            def down(g, c):
                if g.known and g.n < 0:
                    return
                if c == 0:
                    after(pe, x_ready, g.plus(-1), GT)
                if g.known and g.n == 0:
                    pe.wait_ge(w_ready, 4 * (c + 1))
                for j in range(4):
                    pe.wait_ge(hs_ready, g.n * 8 + c * 4 + j + 1)
                    for k in range(GT):
                        cols = slice(k * P, (k + 1) * P)
                        mm = product3(pe, down_ps[k // 2][:, (k % 2) * D:(k % 2 + 1) * D],
                                      (hs[0][:, j, cols], hs[1][:, j, cols]), (wd[0][:, c, j], wd[1][:, c, j]),
                                      c == 0 and j == 0 and k % 2 == 0, c == QUAD0 - 1 and j == 3, skip_group_check=True)
                mm.then_inc(down_done, 1)

            def group(g):
                hidden(g, 0)
                down(g.plus(-1), 1)
                transposes(g.plus(1))
                hidden(g, 1)
                down(g, 0)

            transposes(Step(0, 0, 1))
            group(Step(0, 0, 1))
            with pe.Fori(1, GROUPS) as r:
                group(Step(r, 0, 1))
            down(Step(GROUPS - 1, 0, 1), 1)

        @block.scalar
        def _(act):
            norm.scalar(act)
            def xt_high(g):
                after(act, xt_done, g)
                after(act, up_done, g.plus(-1), 8)
                for dc in range(DC):
                    op = act.activation(xt[0][:, dc], xt_ps[dc][:], ACT.Copy)
                op.then_inc(xhi_ready, 1)

            def hidden_high(s, c, j):
                n = s * 4 + j
                act.wait_ge(kept_ready, n + 1)
                if not (isinstance(s, int) and s < 1):
                    act.wait_ge(down_done, s)
                act.activation(hs[0][:, j], kept[:, j], ACT.Copy).then_inc(hshi_ready, 1)

            def group(g):
                for c in range(2):
                    s = g.n * 2 + c
                    for j in range(4):
                        n = s * 4 + j
                        first = g.known and g.n == 0 and c == 0
                        if j == 3 and not first:
                            for jj in range(4):
                                hidden_high(s - 1, c, jj)
                        act.wait_ge(gate_done, n + 1)
                        if not (first and j < 2):
                            act.wait_ge(hid_ready, n - 1)
                        act.activation(sg[:, j % 2], g_ps[j % 2][:], ACT.Silu).then_inc(silu_ready, 1)
                        act.wait_ge(hid_ready, n + 1)
                        if not first:
                            act.wait_ge(beat_ready, s)
                        act.activation(mag[:, j], hid[:, c, j], ACT.Abs).then_inc(mag_ready, 1)
                xt_high(g.plus(1))

            xt_high(Step(0, 0, 1))
            group(Step(0, 0, 1))
            with act.Fori(1, GROUPS) as r:
                group(Step(r, 0, 1))
            for j in range(4):
                hidden_high(2 * GROUPS - 1, 1, j)

        @block.gpsimd
        def _(pool):
            pool.wait_ge(keep["wd0_loaded"], 16)
            for c in range(QUAD0):
                for j in range(4):
                    pool.tensor_copy(wd[0][:, c, j], wd_raw[:, c, j]).then_inc(whi_ready, 1)
                for j in range(4):
                    pool.wait_ge(whi_ready, 4 * c + j + 1)
                    pool.tensor_tensor(wd[1][:, c, j], wd_raw[:, c, j], raw(wd[0][:, c, j]), ALU.subtract).then_inc(w_ready, 1)
            with pool.Fori(0, 2 * GROUPS) as s:
                for j in range(4):
                    pool.wait_ge(hshi_ready, s * 4 + (j + 1))
                    pool.tensor_tensor(hs[1][:, j], kept[:, j], raw(hs[0][:, j]), ALU.subtract).then_inc(hs_ready, 1)

        @block.vector
        def _(dve):
            norm.vector(dve)

            def xt_low(g):
                after(dve, xhi_ready, g)
                for dc in range(DC):
                    op = dve.tensor_tensor(xt[1][:, dc], xt_ps[dc][:], raw(xt[0][:, dc]), ALU.subtract)
                op.then_inc(xt_ready, 1)

            def hidden(g, c, j):
                n = g.n * 8 + c * 4 + j
                dve.wait_ge(silu_ready, n + 1)
                dve.wait_ge(up_done, n + 1)
                if not (g.known and g.n == 0):
                    dve.wait_ge(mag_ready, n - 7)
                dve.tensor_tensor(hid[:, c, j], sg[:, j % 2], u_ps[j % 2][:], ALU.mult).then_inc(hid_ready, 1)

            def compare(s):
                dve.wait_ge(mag_ready, s * 4 + 4)
                if not (isinstance(s, int) and s < 1):
                    dve.wait_ge(sums_ready, s)
                dve.tensor_tensor(beat_a[:], mag[:, 0:2], mag[:, 2:4], ALU.is_ge)
                dve.tensor_tensor(beat_b[:, 0], mag[:, 0], mag[:, 3], ALU.is_ge)
                dve.tensor_tensor(beat_b[:, 1], mag[:, 1], mag[:, 2], ALU.is_ge)
                dve.tensor_tensor(beat_c[:], mag[:, 0:4:2], mag[:, 1:4:2], ALU.is_ge).then_inc(beat_ready, 1)

            def count(s):
                dve.wait_ge(beat_ready, s + 1)
                dve.tensor_tensor(wins[:, 0:2], beat_a[:], beat_b[:], ALU.add)
                dve.tensor_tensor(wins[:, 2], beat_a[:, 0], beat_b[:, 1], ALU.add)
                dve.tensor_tensor(wins[:, 3], beat_a[:, 1], beat_b[:, 0], ALU.add).then_inc(wins_ready, 1)
                dve.wait_ge(wins_ready, s + 1)
                if not (isinstance(s, int) and s < 1):
                    dve.wait_ge(kept_ready, s * 4)
                dve.tensor_tensor(sums[:, 0:4:3], wins[:, 0:4:3], beat_c[:], ALU.add)
                dve.tensor_tensor(sums[:, 1:3], wins[:, 1:3], beat_c[:], ALU.subtract).then_inc(sums_ready, 1)

            def keep_two(s, c):
                dve.wait_ge(sums_ready, s + 1)
                for j, (op, bound) in enumerate(((ALU.is_ge, 2.0), (ALU.is_ge, 1.0), (ALU.is_le, 0.0), (ALU.is_le, 1.0))):
                    if not (isinstance(s, int) and s < 1):
                        dve.wait_ge(hs_ready, s * 4 + (j - 3))
                    dve.scalar_tensor_tensor(kept[:, j], sums[:, j], bound, hid[:, c, j], op, ALU.mult).then_inc(kept_ready, 1)

            def residual(g):
                after(dve, down_done, g, 2)
                for k in range(GT):
                    t = g.n * GT + k
                    dve.scalar_tensor_tensor(at(x_all, t), down_ps[k // 2][:, (k % 2) * D:(k % 2 + 1) * D], gates[:, 2:3],
                                             at(x_all, t), ALU.mult, ALU.add).then_inc(x_ready, 1)
                for k in range(GT):
                    t = g.n * GT + k
                    dve.wait_ge(x_ready, t + 1)
                    dve.bn_stats(at(norm.stats, t), at(x_all, t)).then_inc(st_ready, 1)

            def group(g):
                first = g.known and g.n == 0
                for c in range(2):
                    s = g.n * 2 + c
                    lagged = not (first and c == 0)
                    if lagged:
                        compare(s - 1)
                    hidden(g, c, 0)
                    if lagged:
                        count(s - 1)
                    hidden(g, c, 1)
                    if lagged:
                        keep_two(s - 1, 1 - c)
                    hidden(g, c, 2)
                    hidden(g, c, 3)
                    if c == 0:
                        after(dve, xt_done, g)
                        normalised(dve, None, norm, xn, x_all, g.plus(1), xn_ready)
                        if not first:
                            residual(g.plus(-1))
                xt_low(g.plus(1))

            normalised(dve, None, norm, xn, x_all, Step(0, 0, 1), xn_ready)
            xt_low(Step(0, 0, 1))
            group(Step(0, 0, 1))
            with dve.Fori(1, GROUPS) as r:
                group(Step(r, 0, 1))
            s = 2 * GROUPS - 1
            compare(s)
            count(s)
            keep_two(s, 1)
            residual(Step(GROUPS - 1, 0, 1))
            dve.wait_ge(st_ready, TILES)


def attention1(nc, sem, keep, d):
    x_all, norm, ident, gates = keep["x_all"], keep["norm"], keep["ident"], keep["gates"]
    sel_out, sel_den = keep["sel_out"], keep["sel_den"]
    w_raw, wd_raw, w = keep["w1_raw"], keep["wd1_raw"], keep["w1"]
    PAIRS = UNITS // 2
    SPLIT = 4 * I1 // TILES
    with ExitStack() as ctx:
        def sb(name, shape, dt):
            return ctx.enter_context(nc.sbuf_tensor(name, shape, dt))

        s_ps = [ctx.enter_context(nc.psum_tensor(f"a1_s{i}", [P, 2, 512], F32)) for i in range(2)]
        st_ps = [ctx.enter_context(nc.psum_tensor(f"a1_st{i}", [P, 512], F32)) for i in range(2)]
        pv_ps = ctx.enter_context(nc.psum_tensor("a1_pv", [P, 512], F32))
        misc = ctx.enter_context(nc.psum_tensor("a1_misc", [P, 512], F32))

        xn = sb("a1_xn", [P, 2, D], F32)
        q_hi = sb("a1_q_hi", [P, 2, D], F32R)
        q_lo = sb("a1_q_lo", [P, 2, D], F32R)
        qop = sb("a1_qop", [P, 2, QUADS, 4, D], F32R)
        kop = sb("a1_kop", [P, 2, QUADS, D], F32R)
        ctx_t = sb("a1_ctx", [P, 2, D], F32)
        vt = sb("a1_vt", [P, 2, DC, UNITS, 32], F32)
        smax = sb("a1_smax", [P, 2, UNITS, 2], F32)
        neg = sb("a1_neg", [P, 2, 2, HALF], F32R)
        neg_t = sb("a1_neg_t", [HALF, 2, D], F32)
        prob = sb("a1_prob", [P, 8, 2 * D], F32)
        pv = sb("a1_pv_sb", [P, 2, QUADS, D], F32)
        back = sb("a1_back", [P, 2, D], F32)
        rden = sb("a1_rden", [P, D], F32)
        att = sb("a1_att", [P, D], F32)

        xn_ready, qhi_ready, qlo_ready, vt_cleared = (sem("a1_" + n) for n in ("xn_ready", "qhi_ready", "qlo_ready", "vt_cleared"))
        q_written = [sem(f"a1_q_written{i}") for i in range(2)]
        op_loaded = [[sem(f"a1_op_loaded{i}{h}") for i in range(2)] for h in range(2)]
        max_loaded = [[sem(f"a1_max_loaded{i}{h}") for i in range(2)] for h in range(2)]
        ctx_loaded = [sem(f"a1_ctx_loaded{i}") for i in range(2)]
        s_done, smax_ready, neg_ready, neg_done, neg_t_ready = (
            sem("a1_" + n) for n in ("s_done", "smax_ready", "neg_ready", "neg_done", "neg_t_ready"))
        st_done, prob_ready, pv_done, pv_ready = (sem("a1_" + n) for n in ("st_done", "prob_ready", "pv_done", "pv_ready"))
        vt_done, vt_ready, sel_done, back_ready, rden_ready, att_ready, x_ready, st_ready = (
            sem("a1_" + n) for n in ("vt_done", "vt_ready", "sel_done", "back_ready", "rden_ready", "att_ready", "x_ready", "st_ready"))
        split_hi, split_lo = sem("a1_split_hi"), sem("a1_split_lo")
        kop_cleared, qop_cleared = sem("a1_kop_cleared"), sem("a1_qop_cleared")

        block = ctx.enter_context(nc.Block())
        LAG = 3

        @block.sync
        def _(sp):
            def maxima(t, h):
                if not t.inside(TILES):
                    return
                after(sp, neg_t_ready, t, 2, h + 1)
                sp.dma_start(raw(qop[MROW:P, t.slot, 2 * h:2 * h + 2]), neg_t[:, h]).then_inc(max_loaded[h][t.slot], 16)

            def operands(t, h):
                if not t.inside(TILES):
                    return
                after(sp, st_done, t.plus(-2), UNITS, 8 * (h + 1))
                if h == 0 and t.known and t.n < 2:
                    sp.wait_ge(kop_cleared, 1)
                    sp.wait_ge(qop_cleared, 1)
                quads = slice(2 * h, 2 * h + 2)
                rows = d["kop"].rearrange("t (g v) r n -> t v r g n", g=QUADS)
                for v in range(4):
                    src = rows[t.n, v] if t.known else rows[bass.ds(t.n, 1), v].rearrange("o r g n -> (o r) g n")
                    dst = kop[v * UROWS:v * UROWS + QROWS, t.slot, quads]
                    sp.dma_start(raw(dst), src[:, quads]).then_inc(op_loaded[h][t.slot], 16)
                after_dma(sp, q_written, t, 3)
                rows = d["qop"][t.slot].rearrange("(g v) r n -> v r g n", g=QUADS)
                for v in range(4):
                    dst = qop[v * UROWS:v * UROWS + QROWS, t.slot, quads, v]
                    sp.dma_start(raw(dst), rows[v, :, quads]).then_inc(op_loaded[h][t.slot], 16)

            def step(s):
                maxima(s.plus(-2), 1)
                v = s.plus(-1)
                if v.inside(TILES):
                    after(sp, vt_done, v.plus(-2))
                    sp.dma_start(ctx_t[:, v.slot], dram_at(d["ctx"], v.n)).then_inc(ctx_loaded[v.slot], 16)
                operands(s, 0)
                maxima(s.plus(-1), 0)
                operands(s, 1)
                if s.known and 1 <= s.n <= 3:
                    load_w1(sp, keep, d, s.n - 1)

            run_steps(sp, step, TILES, LAG, 2)

        def weight_columns(s):
            return slice(s.n * SPLIT, (s.n + 1) * SPLIT) if s.known else bass.ds(s.n * SPLIT, SPLIT)

        @block.gpsimd
        def _(pool):
            pool.memset(raw(kop[:]), 1.0).then_inc(kop_cleared, 1)
            pool.memset(vt[:], 0.0).then_inc(vt_cleared, 1)
            pool.wait_ge(vt_cleared, 1)
            pool.memset(vt[:, :, :, :, D1:D1 + 1], 1.0).then_inc(vt_cleared, 1)

            def step(s):
                w_, l, o = s.plus(-3), s.plus(-4), s.plus(-3)
                if s.inside(TILES):
                    after(pool, qhi_ready, s)
                    after_dma(pool, q_written, s.plus(-2), 3)
                    pool.tensor_tensor(q_lo[:, s.slot], xn[:, s.slot], raw(q_hi[:, s.slot]), ALU.subtract).then_inc(qlo_ready, 1)
                    after(pool, qlo_ready, s)
                    for h in range(2):
                        after_dma(pool, op_loaded[h], s.plus(-2), 8)
                if l.inside(TILES):
                    after(pool, split_hi, l)
                    cols = weight_columns(l)
                    pool.tensor_tensor(w[1][:, cols], w_raw[:, cols], raw(w[0][:, cols]), ALU.subtract).then_inc(split_lo, 1)
                if s.inside(TILES):
                    rows = d["qop"][s.slot].rearrange("u r n -> r u n")
                    for part, src in enumerate((q_hi, q_hi, q_lo)):
                        dst = rows[part * D1:(part + 1) * D1].rearrange("r u n -> u r n")
                        pool.dma_start(dst, raw(src[:, s.slot])).then_inc(q_written[s.slot], 16)
                if w_.inside(TILES):
                    if w_.known and w_.n == 0:
                        pool.wait_ge(keep["w1_loaded"], 16 * W1_LOADS)
                    cols = weight_columns(w_)
                    pool.tensor_copy(w[0][:, cols], w_raw[:, cols]).then_inc(split_hi, 1)
                if o.inside(TILES):
                    after(pool, rden_ready, o, 2)
                    after(pool, x_ready, o.plus(-1))
                    pool.tensor_tensor(att[:], back[:, 0], rden[:], ALU.mult).then_inc(att_ready, 1)

            run_steps(pool, step, TILES, LAG + 1, 2)
            pool.wait_ge(split_lo, TILES)

        @block.scalar
        def _(act):
            norm.scalar(act)

            def step(s):
                v, t, o = s.plus(-1), s.plus(-2), s.plus(-3)
                def turned(w_, h):
                    if w_.inside(TILES):
                        after(act, neg_done, w_, 2, h + 1)
                        after_dma(act, max_loaded[h], w_.plus(-1))
                        act.activation(neg_t[:, h], misc[0:HALF, 0:D], ACT.Copy).then_inc(neg_t_ready, 1)

                def weighted(w_, q):
                    if w_.inside(TILES):
                        after(act, pv_done, w_, QUADS, q + 1)
                        after(act, sel_done, w_.plus(-2))
                        act.activation(pv[:, w_.slot, q], pv_ps[:, 0:D], ACT.Copy).then_inc(pv_ready, 1)

                for u in range(UNITS):
                    j = u // 2
                    if t.inside(TILES):
                        after(act, st_done, t, UNITS, u + 1)
                        quad = (u - 8) // 4
                        if quad >= 0:
                            after(act, pv_done, t, QUADS, quad + 1)
                        else:
                            after(act, pv_done, t.plus(-1), QUADS, quad + QUADS + 1)
                        act.activation(prob[:, u % 8], st_ps[u % 2][:], ACT.Exp, scale=SCALE1).then_inc(prob_ready, 1)
                    if u == 2:
                        turned(t, 1)
                    if u == 1 and s.inside(TILES):
                        after(act, xn_ready, s)
                        after_dma(act, q_written, s.plus(-2), 3)
                        act.activation(q_hi[:, s.slot], xn[:, s.slot], ACT.Copy).then_inc(qhi_ready, 1)
                    if u == 3:
                        weighted(o, 3)
                    if u == 9 and o.inside(TILES):
                        after(act, sel_done, o)
                        after(act, att_ready, o.plus(-1))
                        act.activation(back[:].rearrange("p m n -> p (m n)"), misc[:], ACT.Copy).then_inc(back_ready, 1)
                    if u == 11:
                        turned(v, 0)
                    if u == 14 and v.inside(TILES):
                        after(act, vt_done, v)
                        act.activation(vt[:, v.slot, :, :, 0:D1], misc[:, 0:D].rearrange("p (c u r) -> p c u r", c=DC, r=D1),
                                       ACT.Copy).then_inc(vt_ready, 1)
                    if u in (7, 11, 15):
                        weighted(t, (u - 7) // 4)

            run_steps(act, step, TILES, LAG, 2)

        @block.tensor
        def _(pe):
            pe.wait_ge(vt_cleared, 2)

            def step(s):
                v, t, o = s.plus(-1), s.plus(-2), s.plus(-3)

                def turn(w_, h, before):
                    if w_.inside(TILES):
                        after(pe, neg_ready, w_, 2, h + 1)
                        before()
                        for q in range(2):
                            mm = pe.transpose(misc[0:HALF, q * P:(q + 1) * P], raw(neg[:, h, q]), ident[:])
                        mm.then_inc(neg_done, 1)

                def products(w_, q, c):
                    if not w_.inside(TILES):
                        return
                    if c == 0:
                        after(pe, prob_ready, w_, UNITS, 4 * q + 4)
                        after(pe, vt_ready, w_)
                        if q:
                            after(pe, pv_ready, w_, QUADS, q)
                        else:
                            after(pe, pv_ready, w_.plus(-1), QUADS)
                    for v4 in range(4):
                        u = 4 * q + v4
                        mm = pe.matmul(pv_ps[v4 * 32:(v4 + 1) * 32, 0:D], lhsT=vt[:, w_.slot, c, u],
                                       rhs=prob[:, u % 8, c * D:(c + 1) * D], start=(c == 0), stop=(c == DC - 1),
                                       tile_position=(0, v4 * 32))
                    if c == DC - 1:
                        mm.then_inc(pv_done, 1)

                def selected(w_, m):
                    if not w_.inside(TILES):
                        return
                    if m == 0:
                        after(pe, pv_ready, w_, QUADS)
                        if t.inside(TILES):
                            after(pe, neg_t_ready, t, 2)
                    for q in range(QUADS):
                        mm = pe.matmul(misc[q * 32:(q + 1) * 32, m * D:(m + 1) * D], lhsT=(sel_out, sel_den)[m][:],
                                       rhs=pv[:, w_.slot, q], start=True, stop=True, tile_position=(0, q * 32))
                    if m == 1:
                        mm.then_inc(sel_done, 1)

                for u in range(UNITS):
                    j, k = divmod(u, 2)
                    if t.inside(TILES):
                        if u % HALF == 0:
                            after_dma(pe, max_loaded[u // HALF], t)
                        if u >= 2:
                            after(pe, prob_ready, t, UNITS, u - 1)
                        else:
                            after(pe, prob_ready, t.plus(-1), UNITS, UNITS - 1 + u)
                        for c in range(DC):
                            mm = pe.matmul(st_ps[u % 2][:, c * D:(c + 1) * D], lhsT=kop[:, t.slot, u // 4, c * P:(c + 1) * P],
                                           rhs=qop[:, t.slot, u // 4, u % 4], start=True, stop=True)
                        mm.then_inc(st_done, 1)
                    if v.inside(TILES):
                        if u % HALF == 0:
                            after_dma(pe, op_loaded[u // HALF], v, 8)
                        if k == 0 and j >= 2:
                            after(pe, smax_ready, v, PAIRS, j - 1)
                        elif k == 0:
                            after(pe, smax_ready, v.plus(-1), PAIRS, PAIRS - 1 + j)
                        for q in range(2):
                            mm = pe.matmul(s_ps[j % 2][:, k, q * D:(q + 1) * D], lhsT=qop[0:MROW, v.slot, u // 4, u % 4, q * P:(q + 1) * P],
                                           rhs=kop[0:MROW, v.slot, u // 4], start=True, stop=True)
                        if k == 1:
                            mm.then_inc(s_done, 1)
                    if u == 2:
                        turn(t, 1, lambda: after(pe, vt_ready, t))
                    if u in (1, 3):
                        products(o, 3, u // 2)
                    if u % 2 and u > 3:
                        products(t, u // 4 - 1, u % 4 // 2)
                    if u in (6, 8):
                        selected(o, u // 2 - 3)
                    if u == 11:
                        def before():
                            after(pe, neg_t_ready, t, 2)
                            after(pe, back_ready, o)
                        turn(v, 0, before)
                    if u == 14 and v.inside(TILES):
                        after_dma(pe, ctx_loaded, v)
                        after(pe, neg_t_ready, v, 2, 1)
                        for c in range(DC):
                            mm = pe.transpose(misc[:, c * P:(c + 1) * P], ctx_t[:, v.slot, c * P:(c + 1) * P], ident[:])
                        mm.then_inc(vt_done, 1)

            run_steps(pe, step, TILES, LAG, 2)

        @block.vector
        def _(dve):
            norm.vector(dve)
            norm.apply(dve, xn[:, 0], x_all, 0).then_inc(xn_ready, 1)
            dve.memset(raw(qop[:]), 0.0).then_inc(qop_cleared, 1)

            def step(s):
                v, t, o, p = s.plus(-1), s.plus(-2), s.plus(-3), s.plus(-4)

                def negated(w_, h):
                    if not w_.inside(TILES):
                        return
                    src = smax[:, w_.slot, 8 * h:8 * h + 8].rearrange("p u q -> p q u")
                    after(dve, smax_ready, w_, PAIRS, 4 * h + 4)
                    after(dve, neg_done, w_.plus(-1), 2, h + 1)
                    dve.tensor_scalar(neg[:, h], src, -1.0, None, ALU.mult).then_inc(neg_ready, 1)

                if s.inside(TILES) and not (s.known and s.n == 0):
                    after(dve, qlo_ready, s.plus(-2))
                    norm.apply(dve, xn[:, s.slot], x_all, s.n).then_inc(xn_ready, 1)
                negated(t, 1)
                for j in range(PAIRS):
                    if j == 4:
                        negated(v, 0)
                    if v.inside(TILES):
                        after(dve, s_done, v, PAIRS, j + 1)
                        dve.tensor_reduce(smax[:, v.slot, 2 * j:2 * j + 2].rearrange("p u q -> p (u q)"),
                                          s_ps[j % 2][:].rearrange("p u (q n) -> p (u q) n", q=2), AX_X, ALU.max).then_inc(smax_ready, 1)
                    if j in (5, 6) and o.inside(TILES):
                        cols = slice((j - 5) * P, (j - 4) * P)
                        after(dve, back_ready, o)
                        after(dve, att_ready, o.plus(-1))
                        dve.reciprocal(rden[:, cols], back[:, 1, cols]).then_inc(rden_ready, 1)
                    if j == 0 and p.inside(TILES):
                        after(dve, att_ready, p)
                        dve.scalar_tensor_tensor(at(x_all, p.n), att[:], gates[:, 1:2], at(x_all, p.n), ALU.mult, ALU.add).then_inc(x_ready, 1)
                    if j == 1 and p.inside(TILES):
                        after(dve, x_ready, p)
                        dve.bn_stats(at(norm.stats, p.n), at(x_all, p.n)).then_inc(st_ready, 1)

            run_steps(dve, step, TILES, LAG + 1, 2)
            dve.wait_ge(st_ready, TILES)


W1_LOADS = 2 * (DC + 1) + 3


def load_w1(sp, keep, d, part):
    a, loaded = d["a"], keep["w1_loaded"]
    if part < 2:
        we, ws = ("L1_ffn_We_gate", "L1_ffn_Ws_gate") if part == 0 else ("L1_ffn_We_up", "L1_ffn_Ws_up")
        dst = keep["w1_raw"][:].rearrange("p (m c i) -> p m c i", m=2, c=DC)[:, part]
        for c in range(DC):
            experts = dst[:, c, 0:E * DE].rearrange("p (e j) -> p e j", e=E)
            sp.dma_start(experts, a[we][:, c * P:(c + 1) * P].rearrange("e p j -> p e j")).then_inc(loaded, 16)
        sp.dma_start(dst[:, :, E * DE:I1], a[ws].rearrange("(c p) j -> p c j", p=P)).then_inc(loaded, 16)
        return
    dst, full = keep["wd1_raw"], CH1 - 1 - CHR
    sp.dma_start(dst[:, 0:CHR], a["L1_ffn_We_down"].rearrange("e j n -> (e j) n").rearrange("(c p) n -> p c n", p=P)).then_inc(loaded, 16)
    sp.dma_start(dst[:, CHR:CH1 - 1], a["L1_ffn_Ws_down"][0:full * P].rearrange("(c p) n -> p c n", p=P)).then_inc(loaded, 16)
    sp.dma_start(dst[0:LASTM, CH1 - 1], a["L1_ffn_Ws_down"][full * P:DS]).then_inc(loaded, 16)


def feed_forward1(nc, sem, keep, d):
    x_all, norm, ident, gates = keep["x_all"], keep["norm"], keep["ident"], keep["gates"]
    w, wd_raw = keep["w1"], keep["wd1_raw"]
    a = d["a"]
    with ExitStack() as ctx:
        def sb(name, shape, dt):
            return ctx.enter_context(nc.sbuf_tensor(name, shape, dt))

        def pair(name, shape):
            return sb(name + "_hi", shape, F32R), sb(name + "_lo", shape, F32R)

        banks = [ctx.enter_context(nc.psum_tensor(f"f1_bank{i}", [P, 512], F32)) for i in range(8)]
        g_ps, u_ps, down_ps, mix_ps, misc = banks[0:2], banks[2:4], banks[4:6], banks[6], banks[7]

        wgu = [t[:].rearrange("p (m c i) -> p m c i", m=2, c=DC) for t in w]
        wd = pair("wd1", [P, CH1, D])
        wr = sb("f1_wr", [P, DC, E], F32)
        xn = sb("f1_xn", [P, GT, D], F32)
        xt32 = sb("f1_xt32", [P, DC, GN], F32)
        xt = pair("f1_xt", [P, DC, GN])
        sg = sb("f1_sg", [P, 2, GN], F32)
        prod = sb("f1_prod", [P, 2, GN], F32)
        hid = sb("f1_hid", [P, 2, GN], F32)
        hs = pair("f1_hs", [P, 2, GN])
        logit = sb("f1_logit", [P, GT, E], F32)
        lmax = sb("f1_lmax", [P, GT], F32)
        expo = sb("f1_expo", [P, GT, E], F32)
        esum = sb("f1_esum", [P, GT], F32)
        score = sb("f1_score", [P, GT, E], F32)
        above = sb("f1_above", [P, GT, E, E], F32)
        same = sb("f1_same", [P, GT, E, E], F32)
        rank = sb("f1_rank", [P, GT, E], F32)
        weight = sb("f1_weight", [P, GT, E], F32)
        parts = sb("f1_parts", [P, GT, 2, E], F32R)
        parts_t = sb("f1_parts_t", [2 * E, GN], F32R)
        earlier = sb("f1_earlier", [P, E, E], F32)
        sel_e = sb("f1_sel_e", [2 * E, CHR, P], F32R)
        sel_a = sb("f1_sel_a", [2 * E, 2, CHR * P], F32)

        wr_loaded, consts, whi_ready, w_ready = (sem("f1_" + n) for n in ("wr_loaded", "consts", "whi_ready", "w_ready"))
        xn_ready, xt_done, xt32_ready, xhi_ready, xt_ready = (
            sem("f1_" + n) for n in ("xn_ready", "xt_done", "xt32_ready", "xhi_ready", "xt_ready"))
        gate_done, up_done, silu_ready, prod_ready, mix_done, hid_ready, hshi_ready, hs_ready, chunk_done = (
            sem("f1_" + n) for n in ("gate_done", "up_done", "silu_ready", "prod_ready", "mix_done", "hid_ready", "hshi_ready",
                                     "hs_ready", "chunk_done"))
        logit_done, r_steps, exp_ready, parts_ready, parts_done, parts_t_ready = (
            sem("f1_" + n) for n in ("logit_done", "r_steps", "exp_ready", "parts_ready", "parts_done", "parts_t_ready"))
        x_ready = sem("f1_x_ready")
        R_STEPS = 11

        def rows(c):
            return P if c < CH1 - 1 else LASTM

        def multiplied(eng, g, c):
            q, c = divmod(c, CH1)
            if g.known and g.n + q < 0:
                return
            if c < CHR:
                eng.wait_ge(prod_ready, (g.n + q) * CHR + (c + 1))
            else:
                eng.wait_ge(hid_ready, (g.n + q) * CH1 + (c + 1))

        block = ctx.enter_context(nc.Block())

        @block.sync
        def _(sp):
            sp.dma_start(wr[:], a["L1_ffn_W_router"].rearrange("(c p) e -> p c e", p=P)).then_inc(wr_loaded, 16)

        @block.tensor
        def _(pe):
            def transposes(g, dc):
                if dc == 0:
                    after(pe, xn_ready, g)
                    after(pe, parts_t_ready, g.plus(-1))
                else:
                    after(pe, xt32_ready, g, 2, 1)
                for k in range(GT):
                    mm = pe.transpose(misc[:, k * P:(k + 1) * P], xn[:, k, dc * P:(dc + 1) * P], ident[:])
                mm.then_inc(xt_done, 1)

            def router(g):
                after(pe, xt32_ready, g, 2)
                for k in range(GT):
                    for dc in range(DC):
                        mm = pe.matmul(misc[:, k * E:(k + 1) * E], lhsT=xt32[:, dc, k * P:(k + 1) * P], rhs=wr[:, dc],
                                       start=(dc == 0), stop=(dc == DC - 1))
                mm.then_inc(logit_done, 1)

            def weights(g):
                after(pe, parts_ready, g, 2)
                for k in range(GT):
                    mm = pe.transpose(misc[0:2 * E, k * P:(k + 1) * P], raw(parts[:, k].rearrange("p a e -> p (a e)")), ident[:])
                mm.then_inc(parts_done, 1)

            def hidden(g, c):
                n, slot = g.n * CH1 + c, c % 2
                if c == 0:
                    after(pe, xt_ready, g)
                r = rows(c)
                for m, ps, done in ((0, g_ps, gate_done), (1, u_ps, up_done)):
                    if m == 1:
                        multiplied(pe, g, c - 2)
                    elif not (g.known and n < 2):
                        pe.wait_ge(silu_ready, n - 1)
                    for dc in range(DC):
                        lhs = [t[:, m, dc, c * P:c * P + r] for t in wgu]
                        mm = product3(pe, ps[slot][0:r], lhs, (xt[0][:, dc], xt[1][:, dc]), dc == 0, dc == DC - 1)
                    mm.then_inc(done, 1)
                if c < CHR:
                    if c == 0:
                        after(pe, parts_t_ready, g)
                        after(pe, hid_ready, g.plus(-1), CH1)
                    else:
                        pe.wait_ge(hid_ready, n)
                    pe.matmul(mix_ps[:], lhsT=sel_e[:, c], rhs=parts_t[:], start=True, stop=True).then_inc(mix_done, 1)

            def down(g, c):
                if g.known and g.n < 0:
                    return
                n, r = g.n * CH1 + c, rows(c)
                if c == 0:
                    after(pe, x_ready, g.plus(-1), GT)
                pe.wait_ge(hs_ready, n + 1)
                for k in range(GT):
                    cols = slice(k * P, (k + 1) * P)
                    mm = product3(pe, down_ps[k // 2][:, (k % 2) * D:(k % 2 + 1) * D],
                                  [t[0:r, c % 2, cols] for t in hs], [t[0:r, c] for t in wd],
                                  c == 0 and k % 2 == 0, c == CH1 - 1, skip_group_check=True)
                mm.then_inc(chunk_done, 1)

            def group(g):
                for c in range(CH1):
                    hidden(g, c)
                    if c < 2:
                        down(g.plus(-1), CH1 - 2 + c)
                    else:
                        down(g, c - 2)
                    if c == 3:
                        transposes(g.plus(1), 0)
                    if c == 5:
                        transposes(g.plus(1), 1)
                    if c == 7:
                        router(g.plus(1))
                    if c == 11:
                        weights(g.plus(1))

            first = Step(0, 0, 1)
            pe.wait_ge(consts, 5)
            pe.wait_ge(wr_loaded, 16)
            transposes(first, 0)
            transposes(first, 1)
            router(first)
            weights(first)
            pe.wait_ge(w_ready, CH1)
            group(first)
            with pe.Fori(1, GROUPS) as r:
                group(Step(r, 0, 1))
            for c in range(2):
                down(Step(GROUPS - 1, 0, 1), CH1 - 2 + c)

        @block.scalar
        def _(act):
            norm.scalar(act)

            def transposed(g, dc):
                after(act, xt_done, g, 2, dc + 1)
                after(act, xt_ready, g.plus(-1))
                after(act, logit_done, g.plus(-1))
                act.activation(xt32[:, dc], misc[:], ACT.Copy).then_inc(xt32_ready, 1)

            def high(g):
                after(act, xt32_ready, g, 2)
                after(act, up_done, g.plus(-1), CH1)
                for dc in range(DC):
                    op = act.activation(xt[0][:, dc], xt32[:, dc], ACT.Copy)
                op.then_inc(xhi_ready, 1)

            def exponentials(g):
                after(act, r_steps, g, R_STEPS, 3)
                act.activation(expo[:], logit[:], ACT.Exp).then_inc(exp_ready, 1)

            def hidden_high(n, c, start):
                act.wait_ge(hid_ready, n + 1)
                if not start:
                    act.wait_ge(chunk_done, n - 1)
                act.activation(hs[0][0:rows(c), c % 2], hid[0:rows(c), c % 2], ACT.Copy).then_inc(hshi_ready, 1)

            def group(g):
                for c in range(CH1):
                    n, r = g.n * CH1 + c, rows(c)
                    zero = g.known and g.n == 0
                    act.wait_ge(gate_done, n + 1)
                    multiplied(act, g, c - 2)
                    act.activation(sg[0:r, c % 2], g_ps[c % 2][0:r], ACT.Silu).then_inc(silu_ready, 1)
                    if not (zero and c == 0):
                        hidden_high(n - 1, (c - 1) % CH1, zero and c < 3)
                    if c == 4:
                        transposed(g.plus(1), 0)
                    if c == 6:
                        transposed(g.plus(1), 1)
                    if c == 9:
                        exponentials(g.plus(1))
                high(g.plus(1))

            first = Step(0, 0, 1)
            transposed(first, 0)
            transposed(first, 1)
            high(first)
            act.wait_ge(keep["w1_loaded"], 16 * W1_LOADS)
            exponentials(first)
            for c in range(CH1):
                act.activation(wd[0][0:rows(c), c], wd_raw[0:rows(c), c], ACT.Copy).then_inc(whi_ready, 1)
            group(first)
            with act.Fori(1, GROUPS) as r:
                group(Step(r, 0, 1))
            hidden_high(GROUPS * CH1 - 1, CH1 - 1, False)

        @block.gpsimd
        def _(pool):
            pool.memset(earlier[:], 1.0)
            pool.memset(sel_a[:], 1.0).then_inc(consts, 1)
            pool.wait_ge(consts, 1)
            pool.affine_select(out=earlier[:], in_=earlier[:], compare_op=ALU.is_gt, fill=0.0, base=0,
                               pattern=[[1, E], [-1, E]], channel_multiplier=0)
            for m in range(2):
                v = sel_a[:, m]
                first = DE * E * m
                pool.affine_select(out=v, in_=v, compare_op=ALU.is_ge, fill=0.0, base=first,
                                   pattern=[[1, CHR * P]], channel_multiplier=-DE)
            pool.memset(lmax[:], 0.0).then_inc(consts, 1)
            pool.wait_ge(consts, 2)
            for m in range(2):
                v = sel_a[:, m]
                pool.affine_select(out=v, in_=v, compare_op=ALU.is_ge, fill=0.0, base=DE - 1 - DE * E * m,
                                   pattern=[[-1, CHR * P]], channel_multiplier=DE)
            pool.memset(esum[:], 0.0).then_inc(consts, 1)
            pool.wait_ge(consts, 3)
            pool.tensor_tensor(sel_a[:, 0], sel_a[:, 0], sel_a[:, 1], ALU.add).then_inc(consts, 1)
            pool.wait_ge(consts, 4)
            pool.tensor_copy(sel_e[:].rearrange("k c p -> k (c p)"), sel_a[:, 0]).then_inc(consts, 1)

            for c in range(CH1):
                pool.wait_ge(whi_ready, c + 1)
                r = rows(c)
                pool.tensor_tensor(wd[1][0:r, c], wd_raw[0:r, c], raw(wd[0][0:r, c]), ALU.subtract).then_inc(w_ready, 1)

            def group(g):
                for c in range(CH1):
                    r = rows(c)
                    pool.wait_ge(hshi_ready, g.n * CH1 + (c + 1))
                    pool.tensor_tensor(hs[1][0:r, c % 2], hid[0:r, c % 2], raw(hs[0][0:r, c % 2]), ALU.subtract).then_inc(hs_ready, 1)

            with pool.Fori(0, GROUPS) as r:
                group(Step(r, 0, 1))

        @block.vector
        def _(dve):
            norm.vector(dve)

            def low(g):
                after(dve, xhi_ready, g)
                for dc in range(DC):
                    op = dve.tensor_tensor(xt[1][:, dc], xt32[:, dc], raw(xt[0][:, dc]), ALU.subtract)
                op.then_inc(xt_ready, 1)

            def stage(g, k, op):
                op.then_inc(r_steps, 1)
                after(dve, r_steps, g, R_STEPS, k)

            def softmax_start(g):
                after(dve, logit_done, g)
                after(dve, exp_ready, g.plus(-1))
                stage(g, 1, dve.tensor_copy(logit[:].rearrange("p k e -> p (k e)"), misc[:, 0:GT * E]))
                stage(g, 2, dve.tensor_reduce(lmax[:], logit[:], AX_X, ALU.max))
                stage(g, 3, dve.tensor_tensor(logit[:], logit[:], lmax[:].unsqueeze(2).to_broadcast([P, GT, E]), ALU.subtract))

            def top2(g):
                after(dve, exp_ready, g)
                stage(g, 4, dve.tensor_reduce(esum[:], expo[:], AX_X, ALU.add))
                stage(g, 5, dve.reciprocal(lmax[:], esum[:]))
                stage(g, 6, dve.tensor_tensor(score[:], expo[:], lmax[:].unsqueeze(2).to_broadcast([P, GT, E]), ALU.mult))
                for k in range(GT):
                    other = score[:, k].unsqueeze(1).to_broadcast([P, E, E])
                    own = score[:, k].unsqueeze(2).to_broadcast([P, E, E])
                    dve.tensor_tensor(above[:, k], other, own, ALU.is_gt)
                    op = dve.tensor_tensor(same[:, k], other, own, ALU.is_equal)
                stage(g, 7, op)
                for k in range(GT):
                    op = dve.tensor_tensor(same[:, k], same[:, k], earlier[:], ALU.mult)
                stage(g, 8, op)
                flat = "p k a b -> p (k a b)"
                stage(g, 9, dve.tensor_tensor(above[:].rearrange(flat), above[:].rearrange(flat), same[:].rearrange(flat), ALU.add))
                stage(g, 10, dve.tensor_reduce(rank[:].rearrange("p k e -> p (k e)"), above[:].rearrange("p k a b -> p (k a) b"), AX_X, ALU.add))
                stage(g, 11, dve.scalar_tensor_tensor(weight[:], rank[:], 2.0, score[:], ALU.is_lt, ALU.mult))
                after(dve, parts_done, g.plus(-1))
                dve.tensor_copy(parts[:, :, 0], weight[:]).then_inc(parts_ready, 1)
                after(dve, parts_ready, g, 2, 1)
                dve.tensor_tensor(parts[:, :, 1], weight[:], raw(parts[:, :, 0]), ALU.subtract).then_inc(parts_ready, 1)

            def parts_turned(g):
                after(dve, parts_done, g)
                after(dve, mix_done, g.plus(-1), CHR)
                dve.tensor_copy(parts_t[:], misc[0:2 * E, :]).then_inc(parts_t_ready, 1)

            def chunk(g, c):
                n, r, slot = g.n * CH1 + c, rows(c), c % 2
                zero = g.known and g.n == 0 and c < 2
                routed = c < CHR
                dve.wait_ge(silu_ready, n + 1)
                dve.wait_ge(up_done, n + 1)
                if not zero:
                    dve.wait_ge(hs_ready, n - 1)
                out = prod if routed else hid
                done = prod_ready if routed else hid_ready
                dve.tensor_tensor(out[0:r, slot], sg[0:r, slot], u_ps[slot][0:r], ALU.mult).then_inc(done, 1)
                if routed:
                    multiplied(dve, g, c)
                    dve.wait_ge(mix_done, g.n * CHR + (c + 1))
                    dve.tensor_tensor(hid[:, slot], prod[:, slot], mix_ps[:], ALU.mult).then_inc(hid_ready, 1)

            def residual(g):
                after(dve, chunk_done, g, CH1)
                for k in range(GT):
                    t = g.n * GT + k
                    dve.scalar_tensor_tensor(at(x_all, t), down_ps[k // 2][:, (k % 2) * D:(k % 2 + 1) * D], gates[:, 3:4],
                                             at(x_all, t), ALU.mult, ALU.add).then_inc(x_ready, 1)

            def group(g):
                for c in range(CH1):
                    chunk(g, c)
                    if c == 1:
                        if not (g.known and g.n == 0):
                            residual(g.plus(-1))
                        after(dve, xt_done, g, 2)
                        normalised(dve, None, norm, xn, x_all, g.plus(1), xn_ready)
                    if c == 8:
                        softmax_start(g.plus(1))
                    if c == 10:
                        top2(g.plus(1))
                    if c == 12:
                        parts_turned(g.plus(1))
                low(g.plus(1))

            first = Step(0, 0, 1)
            normalised(dve, None, norm, xn, x_all, first, xn_ready)
            low(first)
            softmax_start(first)
            dve.wait_ge(consts, 4)
            top2(first)
            parts_turned(first)
            group(first)
            with dve.Fori(1, GROUPS) as r:
                group(Step(r, 0, 1))
            residual(Step(GROUPS - 1, 0, 1))
            dve.wait_ge(x_ready, TILES)


def finish(nc, sem, keep, d):
    x_all = keep["x_all"]
    stored = sem("stored")
    with nc.Block() as block:
        @block.sync
        def _(sp):
            sp.dma_start(d["out"].rearrange("t p n -> p t n"), x_all[:, 0:TILES]).then_inc(stored, 16)
            sp.wait_ge(stored, 16)


def flamingo(nc, a, out, stages=4):
    d = {
        "x": a["x"].rearrange("(t b) s n -> t (b s) n", b=2),
        "ctx": a["ctx_2048"].rearrange("(t b) s n -> t (b s) n", b=2),
        "wq": a["L0_xattn_W_q"], "wk": a["L0_xattn_W_k"], "wv": a["L0_xattn_W_v"], "wo": a["L0_xattn_W_o"],
        "g_xattn": a["g_xattn"].partition_broadcast(P), "g_ffn": a["g_ffn"].partition_broadcast(P),
        "gamma": a["L1_xattn_gamma"].partition_broadcast(P),
        "kop": nc.dram_tensor("kop_rows", (TILES, UNITS, QROWS, D), F32).ap(),
        "qop": nc.dram_tensor("qop_rows", (2, UNITS, QROWS, D), F32).ap(),
        "out": out.rearrange("(t b) s n -> t (b s) n", b=2),
        "a": a,
    }
    with ExitStack() as ctx:
        def sb(name, shape, dt):
            return ctx.enter_context(nc.sbuf_tensor(name, shape, dt))

        def sem(name):
            return ctx.enter_context(nc.semaphore(name))

        keep = {
            "x_all": sb("x_all", [P, XT, D], F32),
            "norm": Norm(sb, sem),
            "ident": sb("ident", [P, P], F32),
            "gates": sb("gates", [P, 4], F32),
            "sel_out": sb("sel_out", [P, 32], F32),
            "sel_den": sb("sel_den", [P, 32], F32),
        }
        with ExitStack() as early:
            keep["w0_raw"] = early.enter_context(nc.sbuf_tensor("w0_raw", [P, 2, DC, I0], F32))
            keep["wd0_raw"] = early.enter_context(nc.sbuf_tensor("wd0_raw", [P, QUAD0, 4, D], F32))
            keep["w0"] = [early.enter_context(nc.sbuf_tensor(n, [P, 2, DC, 4, I0 // 4], F32R)) for n in ("w0_hi", "w0_lo")]
            keep["w0_loaded"] = [sem("w0_loaded0"), sem("w0_loaded1")]
            keep["wd0_loaded"] = sem("wd0_loaded")
            attention0(nc, sem, keep, d)
            if stages > 1:
                feed_forward0(nc, sem, keep, d)
        keep["w1_raw"] = sb("w1_raw", [P, 4 * I1], F32)
        keep["wd1_raw"] = sb("wd1_raw", [P, CH1, D], F32)
        keep["w1"] = sb("w1_hi", [P, 4 * I1], F32R), sb("w1_lo", [P, 4 * I1], F32R)
        keep["w1_loaded"] = sem("w1_loaded")
        if stages > 2:
            attention1(nc, sem, keep, d)
        if stages > 3:
            feed_forward1(nc, sem, keep, d)
        finish(nc, sem, keep, d)


_INS = ['x', 'ctx_2048', 'g_xattn', 'g_ffn', 'L0_xattn_W_q', 'L0_xattn_W_k', 'L0_xattn_W_v', 'L0_xattn_W_o',
        'L0_ffn_w_gate', 'L0_ffn_w_up', 'L0_ffn_w_down', 'L1_xattn_gamma', 'L1_ffn_W_router', 'L1_ffn_We_gate',
        'L1_ffn_We_up', 'L1_ffn_We_down', 'L1_ffn_Ws_gate', 'L1_ffn_Ws_up', 'L1_ffn_Ws_down']


def kernel(**inputs):
    import numpy as _np
    import concourse.bacc as _bacc
    from concourse import mybir as _mybir
    from concourse.bass_utils import run_bass_kernel_spmd as _run

    nc = _bacc.Bacc("TRN2", target_bir_lowering=False, num_devices=1)
    arrays, args = {}, {}
    for name in _INS:
        a = _np.ascontiguousarray(inputs[name])
        if a.ndim == 0:
            a = a.reshape(1)
        arrays[f"in_{name}"] = a
        args[name] = nc.dram_tensor(f"in_{name}", a.shape, _mybir.dt.from_np(a.dtype), kind="ExternalInput").ap()
    out = nc.dram_tensor("out_x", (BATCH, SEQ, D), F32, kind="ExternalOutput").ap()
    flamingo(nc, args, out)
    r = _run(nc, [arrays], core_ids=[0])
    return r.results[0]["out_x"]
```

```python
from contextlib import ExitStack

import concourse.bass as bass
from concourse import mybir

F32 = mybir.dt.float32
F32R = mybir.dt.float32r
BF16 = mybir.dt.bfloat16
ACT = mybir.ActivationFunctionType
ALU = mybir.AluOpType
AX_X = mybir.AxisListType.X

P = 128
BATCH, SEQ, D = 32, 64, 256
TOK = BATCH * SEQ
TILES = TOK // P
DC = D // P
EPS = 1e-5

H0 = 8
N0 = D // H0
SCALE0 = float(N0) ** -0.5

H1 = 8
D1 = SEQ // H1
SCALE1 = float(D1) ** -0.5
UNITS = P // D1
QUADS = UNITS // 4
QROWS = 3 * D1
UROWS = 32
MROW = P - 1
HALF = UNITS // 2

GT = 4
GN = GT * P
GROUPS = TILES // GT
XT = TILES + 1
EARLY, LATE = slice(0, TILES - GT), slice(TILES - GT, XT)

I0 = 1024
W0_COLS = 2 * I0 // TILES
QUAD0 = I0 // (4 * P)
E, DE, DS = 8, 176, 352
I1 = E * DE + DS
CH1 = -(-I1 // P)
CHR = E * DE // P
LASTM = I1 - (CH1 - 1) * P


class Step:

    def __init__(self, rnd, slot, unroll):
        self.rnd, self.slot, self.unroll = rnd, slot, unroll
        self.known = isinstance(rnd, int)
        self.n = rnd * unroll + slot

    def plus(self, k):
        q, slot = divmod(self.slot + k, self.unroll)
        return Step(self.rnd + q, slot, self.unroll)

    def inside(self, count):
        return not self.known or 0 <= self.n < count


def run_steps(eng, body, count, lag, unroll, head=0):
    head = max(head, -(-lag // unroll))
    tail = count // unroll
    for n in range(head * unroll):
        body(Step(n // unroll, n % unroll, unroll))
    with eng.Fori(head, tail) as r:
        for slot in range(unroll):
            body(Step(r, slot, unroll))
    for n in range(tail * unroll, count + lag):
        body(Step(n // unroll, n % unroll, unroll))


def after(eng, sem, step, per=1, k=None):
    if step.known and step.n < 0:
        return
    eng.wait_ge(sem, step.n * per + (per if k is None else k))


def after_dma(eng, sems, step, transfers=1):
    if step.known and step.rnd < 0:
        return
    eng.wait_ge(sems[step.slot], (step.rnd + 1) * (16 * transfers))


def at(tensor, n):
    if isinstance(n, int):
        return tensor[:, n]
    v = tensor[:, bass.ds(n, 1)]
    return v.rearrange("p o n -> p (o n)")


def dram_at(ap, n):
    if isinstance(n, int):
        return ap[n]
    return ap[bass.ds(n, 1)].rearrange("o p n -> (o p) n")


def raw(ap):
    return ap.bitcast(F32)


def product3(pe, out, lhs, rhs, first, last, **kw):
    (lh, ll), (rh, rl) = lhs, rhs
    pe.matmul(out, lhsT=lh, rhs=rh, start=first, stop=False, **kw)
    pe.matmul(out, lhsT=lh, rhs=rl, start=False, stop=False, **kw)
    return pe.matmul(out, lhsT=ll, rhs=rh, start=False, stop=last, **kw)


MEMBERS = (0, 3, 1, 2)
LAST = Step(GROUPS - 1, 0, 1)


class Norm:

    def __init__(self, sb, sem):
        self.stats = sb("stats", [P, XT, 6], F32)
        self.sum2, self.dif, self.m2, self.sq, self.var, self.std, self.rstd, self.shift = (
            sb(f"ln_{n}", [P, XT], F32) for n in ("sum2", "dif", "m2", "sq", "var", "std", "rstd", "shift"))
        self.eps = sb("eps", [P, 1], F32)
        self.steps = sem("ln_steps")
        self.used = self.rooted = 0

    def vector(self, dve, tiles=slice(0, XT), meanwhile=lambda: None):
        st, n = self.stats, self.used
        self.used += 6
        even, odd = st[:, tiles, 1], st[:, tiles, 4]
        sum2, dif, m2, sq, var, std, rstd, shift = (
            t[:, tiles] for t in (self.sum2, self.dif, self.m2, self.sq, self.var, self.std, self.rstd, self.shift))
        dve.tensor_tensor(sum2, even, odd, ALU.add)
        dve.tensor_tensor(dif, even, odd, ALU.subtract)
        dve.tensor_tensor(m2, st[:, tiles, 2], st[:, tiles, 5], ALU.add).then_inc(self.steps, 1)
        dve.wait_ge(self.steps, n + 1)
        dve.scalar_tensor_tensor(sq, dif, 0.25, dif, ALU.mult, ALU.mult).then_inc(self.steps, 1)
        dve.wait_ge(self.steps, n + 2)
        dve.scalar_tensor_tensor(var, m2, 1.0 / D, sq, ALU.mult, ALU.add).then_inc(self.steps, 1)
        meanwhile()
        dve.wait_ge(self.steps, n + 4)
        dve.reciprocal(rstd, std).then_inc(self.steps, 1)
        dve.wait_ge(self.steps, n + 5)
        dve.scalar_tensor_tensor(shift, sum2, -0.5, rstd, ALU.mult, ALU.mult).then_inc(self.steps, 1)
        dve.wait_ge(self.steps, n + 6)

    def scalar(self, act, tiles=slice(0, XT)):
        act.wait_ge(self.steps, self.rooted + 3)
        self.rooted += 6
        act.activation(self.std[:, tiles], self.var[:, tiles], ACT.Sqrt, bias=self.eps[:, 0:1]).then_inc(self.steps, 1)

    def apply(self, dve, out, x_all, n):
        return dve.tensor_scalar(out, at(x_all, n), column(self.rstd, n), column(self.shift, n), ALU.mult, ALU.add)


class QueryParts:

    def __init__(self, sb, sem):
        self.xn = sb("q_xn", [P, 2, D], F32)
        self.hi, self.lo = sb("q_hi", [P, 2, D], F32R), sb("q_lo", [P, 2, D], F32R)
        self.hi_ready, self.lo_ready = sem("q_hi_ready"), sem("q_lo_ready")
        self.first_written = [sem("q_first_written0"), sem("q_first_written1")]
        self.written = [sem("q_written0"), sem("q_written1")]

    def high(self, act, norm, x_all, s):
        after(act, self.lo_ready, s.plus(-2))
        self.after_store(act, s.plus(-2))
        for out in (self.xn, self.hi):
            op = act.activation(out[:, s.slot], at(x_all, s.n), ACT.Identity, bias=column(norm.shift, s.n), scale=column(norm.rstd, s.n))
        op.then_inc(self.hi_ready, 1)

    def low(self, pool, s):
        after(pool, self.hi_ready, s)
        self.after_store(pool, s.plus(-2))
        pool.tensor_tensor(self.lo[:, s.slot], self.xn[:, s.slot], raw(self.hi[:, s.slot]), ALU.subtract).then_inc(self.lo_ready, 1)

    def store(self, eng, d, s):
        rows = d["qop"][s.slot].rearrange("u r n -> r u n")
        for part, src in enumerate((self.hi, self.hi, self.lo)):
            dst = rows[part * D1:(part + 1) * D1].rearrange("r u n -> u r n")
            first = s.known and s.rnd == 0
            eng.dma_start(dst, raw(src[:, s.slot])).then_inc((self.first_written if first else self.written)[s.slot], 16)

    def after_store(self, eng, t):
        if t.known and t.rnd == 0:
            eng.wait_ge(self.first_written[t.slot], 16 * 3)
        elif not t.known or t.rnd > 0:
            eng.wait_ge(self.written[t.slot], t.rnd * (16 * 3))


class Operands:

    def __init__(self, sb, sem):
        self.q, self.k = [], []
        self.add_slot(sb)
        self.cleared = sem("op_cleared")
        self.loaded = [[sem(f"op_loaded{i}{h}") for i in range(2)] for h in range(2)]

    def add_slot(self, sb):
        n = len(self.q)
        self.q.append(sb(f"qop{n}", [P, QUADS, 4, D], F32R))
        self.k.append(sb(f"kop{n}", [P, QUADS, D], F32R))

    def clear(self, pool, slot):
        pool.memset(raw(self.k[slot][:]), 1.0)
        pool.memset(raw(self.q[slot][:]), 0.0).then_inc(self.cleared, 1)

    def load_k(self, sp, d, t, h):
        quads = slice(2 * h, 2 * h + 2)
        rows = d["kop"].rearrange("t (g v) r n -> t v r g n", g=QUADS)
        for v in range(4):
            src = rows[t.n, v] if t.known else rows[bass.ds(t.n, 1), v].rearrange("o r g n -> (o r) g n")
            dst = self.k[t.slot][v * UROWS:v * UROWS + QROWS, quads]
            sp.dma_start(raw(dst), src[:, quads]).then_inc(self.loaded[h][t.slot], 16)

    def load_q(self, sp, d, t, h):
        quads = slice(2 * h, 2 * h + 2)
        rows = d["qop"][t.slot].rearrange("(g v) r n -> v r g n", g=QUADS)
        for v in range(4):
            dst = self.q[t.slot][v * UROWS:v * UROWS + QROWS, quads, v]
            sp.dma_start(raw(dst), rows[v, :, quads]).then_inc(self.loaded[h][t.slot], 16)


class Turned:

    def __init__(self, sb, sem):
        self.parts = sb("turned_hi", [P, DC, GN], F32R), sb("turned_lo", [P, DC, GN], F32R)
        self.plain = sb("turned", [P, DC, GN], F32)
        self.xn_ready, self.done, self.plain_ready, self.hi_ready, self.ready = (
            sem("turned_" + n) for n in ("xn_ready", "done", "plain_ready", "hi_ready", "ready"))

    def transpose(self, pe, xn, dc, bank, ident):
        for k in range(GT):
            mm = pe.transpose(bank[:, k * P:(k + 1) * P], xn[:, k, dc * P:(dc + 1) * P], ident[:])
        mm.then_inc(self.done, 1)

    def copy(self, act, g, dc, bank):
        after(act, self.done, g, DC, dc + 1)
        act.activation(self.plain[:, dc], bank, ACT.Copy).then_inc(self.plain_ready, 1)

    def high(self, act, g):
        after(act, self.plain_ready, g, DC)
        for dc in range(DC):
            act.activation(self.parts[0][:, dc], self.plain[:, dc], ACT.Copy).then_inc(self.hi_ready, 1)

    def low(self, dve, g):
        for dc in range(DC):
            after(dve, self.hi_ready, g, DC, dc + 1)
            dve.tensor_tensor(self.parts[1][:, dc], self.plain[:, dc], raw(self.parts[0][:, dc]), ALU.subtract).then_inc(self.ready, 1)


def columns(n, width):
    return slice(n * width, (n + 1) * width) if isinstance(n, int) else bass.ds(n * width, width)


def column(tensor, n):
    return tensor[:, n:n + 1] if isinstance(n, int) else tensor[:, bass.ds(n, 1)]


def attention0(nc, sem, keep, d):
    x_all, norm, ident, gates = keep["x_all"], keep["norm"], keep["ident"], keep["gates"]
    sel_out, sel_den = keep["sel_out"], keep["sel_den"]
    with ExitStack() as ctx:
        def sb(name, shape, dt):
            return ctx.enter_context(nc.sbuf_tensor(name, shape, dt))

        banks = [ctx.enter_context(nc.psum_tensor(f"a0_bank{i}", [P, 512], F32)) for i in range(8)]
        qk_ps, v_ps, s_ps = banks[0:2], banks[2], banks[3:5]
        pt_ps, o_ps, proj_ps = banks[5], banks[6], banks[7]

        w_raw = sb("w_raw", [P, 5, P], F32)
        w_t = sb("w_t", [P, 5, P], F32)
        gate_in = sb("gate_in", [P, 5], F32)
        ctx_t = sb("ctx_t", [P, 2, D], F32)
        xn = sb("xn", [P, 2, D], F32)
        xn_late = sb("xn_late", [P, 2, D], F32)
        q_t = sb("q_t", [P, 2, DC, P], F32)
        k_m = sb("k_m", [P, 2, DC, 2, 4, SEQ], F32)
        v_m = sb("v_m", [P, 2, 2, 4, 2, N0], F32)
        smax = sb("smax", [P, 2, H0], F32)
        shifted = sb("shifted", [P, 2, H0 * SEQ], F32)
        prob = sb("prob", [P, 2, H0 * SEQ], F32)
        den = sb("den", [P, 2, H0], F32)
        rden = sb("rden", [P, 2, H0], F32)
        p_t = sb("p_t", [P, 2, 4 * P], F32)
        head = sb("head", [P, 2, D], F32)
        mix = sb("mix", [P, 2, D], F32)
        k_hi = sb("k_hi", [P, 2, D], F32R)
        k_lo = sb("k_lo", [P, 2, D], F32R)

        zeroed, ident_steps, w_loaded, x_loaded, gate_loaded = (
            sem("zeroed"), sem("ident_steps"), sem("w_loaded"), [sem(f"x_loaded{i}") for i in range(GROUPS)], sem("gate_loaded"))
        wt_done, wt_ready, gate_steps, stats0 = sem("wt_done"), sem("wt_ready"), sem("gate_steps"), sem("stats0")
        ctx_loaded = [sem("ctx_loaded0"), sem("ctx_loaded1")]
        kop_written = [sem("kop_written0"), sem("kop_written1")]
        w0_raw, w0, w0_loaded, w0_hi, w0_lo = keep["w0_raw"], keep["w0"], keep["w0_loaded"], sem("w0_hi_ready"), sem("w0_lo_ready")
        xn_ready, qk_done, v_done, q_ready, k_ready, v_ready = (
            sem(n) for n in ("xn_ready", "qk_done", "v_done", "q_ready", "k_ready", "v_ready"))
        score_done, smax_ready, shift_ready, prob_ready, den_ready, rden_ready = (
            sem(n) for n in ("score_done", "smax_ready", "shift_ready", "prob_ready", "den_ready", "rden_ready"))
        pt_done, pt_ready, o_done, head_ready, mix_ready, proj_done, x_ready, st_ready = (
            sem(n) for n in ("pt_done", "pt_ready", "o_done", "head_ready", "mix_ready", "proj_done", "x_ready", "st_ready"))
        khi_ready, klo_ready, late_ready, v_odd_ready = sem("khi_ready"), sem("klo_ready"), sem("late_ready"), sem("v_odd_ready")

        def v_copies(s, h):
            r = slice(h * SEQ, (h + 1) * SEQ)
            src = v_ps[r].rearrange("p (b g h n) -> p b g h n", b=2, g=4, h=2)
            return [(v_m[r, s.slot, b, :, h], src[:, b, :, h]) for b in range(2)]

        block = ctx.enter_context(nc.Block())

        @block.sync
        def _(sp):
            def load_x(g):
                tiles = slice(g * GT, (g + 1) * GT)
                sp.dma_start(x_all[:, tiles], d["x"][tiles].rearrange("t p n -> p t n")).then_inc(x_loaded[g], 16)

            load_x(0)
            sp.wait_ge(zeroed, 1)
            for m, w in ((0, "wq"), (1, "wk"), (2, "wo")):
                for b in range(2):
                    r = slice(b * SEQ, (b + 1) * SEQ)
                    sp.dma_start(w_raw[r, m, r], d[w]).then_inc(w_loaded, 16)
            twice = d["wv"].rearrange("(o r) n -> o r n", o=1).to_broadcast([2, SEQ, SEQ])
            for b in range(2):
                sp.dma_start(w_raw[:, 3 + b, b * SEQ:(b + 1) * SEQ], twice).then_inc(w_loaded, 16)

            def step(s):
                if s.inside(TILES):
                    after(sp, qk_done, s.plus(-2))
                    after(sp, v_done, s.plus(-2))
                    after(sp, klo_ready, s.plus(-2))
                    sp.dma_start(ctx_t[:, s.slot], dram_at(d["ctx"], s.n)).then_inc(ctx_loaded[s.slot], 16)
                    if s.known and s.n == 0:
                        load_x(1)
                        for m, g in enumerate(("g_xattn", "g_ffn", "gamma")):
                            w = 2 if m < 2 else 1
                            sp.dma_start(gate_in[:, 2 * m:2 * m + w], d[g]).then_inc(gate_loaded, 16)
                        for g in range(2, GROUPS):
                            load_x(g)
                t = s.plus(-2)
                if t.inside(TILES):
                    after(sp, khi_ready, t)
                    after(sp, klo_ready, t)
                    rows = d["kop"].rearrange("t u r n -> t r u n")
                    rows = rows[t.n] if t.known else rows[bass.ds(t.n, 1)].rearrange("o r u n -> (o r) u n")
                    for part, src in enumerate((k_hi, k_lo, k_hi)):
                        dst = rows[part * D1:(part + 1) * D1].rearrange("r u n -> u r n")
                        sp.dma_start(dst, raw(src[:, t.slot])).then_inc(kop_written[t.slot], 16)
                if s.inside(TILES):
                    a = d["a"][("L0_ffn_w_gate", "L0_ffn_w_up")[s.slot]].rearrange("(c p) i -> p c i", p=P)
                    cols = columns(s.rnd, W0_COLS)
                    sp.dma_start(w0_raw[:, s.slot, :, cols], a[:, :, cols]).then_inc(w0_loaded[s.slot], 16)

            run_steps(sp, step, TILES, 2, 2)
            sp.dma_start(keep["wd0_raw"][:], d["a"]["L0_ffn_w_down"].rearrange("(c p j) n -> p c j n", p=P, j=4)).then_inc(keep["wd0_loaded"], 16)
            for slot in range(2):
                sp.wait_ge(kop_written[slot], 16 * 3 * TILES // 2)

        @block.gpsimd
        def _(pool):
            pool.memset(w_raw[:], 0.0).then_inc(zeroed, 1)
            pool.memset(ident[:], 0.0)
            pool.memset(sel_out[:], 0.0)
            pool.memset(sel_den[:], 0.0).then_inc(ident_steps, 1)
            pool.wait_ge(ident_steps, 1)
            pool.affine_select(out=ident[:], in_=ident[:], compare_op=ALU.not_equal, fill=1.0, base=0,
                               pattern=[[-1, P]], channel_multiplier=1).then_inc(ident_steps, 1)
            pool.memset(k_m[:], 0.0)
            pool.memset(v_m[:], 0.0).then_inc(zeroed, 1)
            v = sel_out[:].rearrange("p (u r) -> p u r", u=4)
            pool.affine_select(out=v, in_=v, compare_op=ALU.not_equal, fill=1.0, base=0,
                               pattern=[[-UROWS, 4], [-1, D1]], channel_multiplier=1)
            v = sel_den[:].rearrange("p (u r) -> p u r", u=4)
            pool.affine_select(out=v, in_=v, compare_op=ALU.not_equal, fill=1.0, base=-D1,
                               pattern=[[-UROWS, 4], [0, D1]], channel_multiplier=1).then_inc(ident_steps, 1)
            pool.memset(x_all[:, TILES:XT], 0.0)
            pool.memset(norm.stats[:, TILES:XT], 0.0)
            pool.memset(norm.eps[:], EPS).then_inc(ident_steps, 1)

            def step(s):
                if s.inside(TILES):
                    after_dma(pool, w0_loaded, s)
                    after(pool, khi_ready, s)
                    after_dma(pool, kop_written, s.plus(-2), 3)
                    pool.tensor_tensor(k_lo[:, s.slot], ctx_t[:, s.slot], raw(k_hi[:, s.slot]), ALU.subtract).then_inc(klo_ready, 1)
                if s.inside(TILES):
                    m, r, n = s.slot, columns(s.rnd, W0_COLS), columns(s.rnd, W0_COLS // 4)
                    src = w0_raw[:, m, :, r].rearrange("p c (g j) -> p c j g", j=4)
                    pool.tensor_copy(w0[0][:, m, :, :, n], src).then_inc(w0_hi, 1)
                    after(pool, w0_hi, s)
                    pool.tensor_tensor(w0[1][:, m, :, :, n], src, raw(w0[0][:, m, :, :, n]), ALU.subtract).then_inc(w0_lo, 1)
                t = s.plus(-1)
                if t.inside(TILES):
                    after(pool, late_ready, t)
                    after(pool, head_ready, t)
                    after(pool, proj_done, t.plus(-2))
                    pool.tensor_tensor(mix[:, t.slot], xn_late[:, t.slot], head[:, t.slot], ALU.subtract).then_inc(mix_ready, 1)

            run_steps(pool, step, TILES, 2, 2)
            pool.wait_ge(w0_lo, TILES)

        @block.scalar
        def _(act):
            act.wait_ge(ident_steps, 4)
            norm.scalar(act, slice(0, GT))
            act.wait_ge(norm.steps, norm.rooted)
            act.wait_ge(zeroed, 2)
            act.wait_ge(wt_done, 1)
            act.activation(w_t[:, 0:4].rearrange("p m n -> p (m n)"), banks[0][:], ACT.Copy)
            act.activation(w_t[:, 4], banks[1][:, 0:P], ACT.Copy).then_inc(wt_ready, 1)

            def step(s):
                t = s.plus(-1)
                if s.inside(TILES):
                    after(act, qk_done, s)
                    after(act, score_done, s.plus(-2))
                    act.activation(q_t[:, s.slot].rearrange("p c n -> p (c n)"), qk_ps[s.slot][:, 0:D], ACT.Copy).then_inc(q_ready, 1)
                    for h in range(4):
                        r = slice(h * N0, (h + 1) * N0)
                        src = qk_ps[s.slot][r, D:2 * D].rearrange("p (c b e) -> p c b e", c=DC, b=2)
                        op = act.activation(k_m[r, s.slot, :, :, h], src, ACT.Copy)
                    op.then_inc(k_ready, 1)
                if t.inside(TILES):
                    after(act, pt_done, t)
                    after(act, o_done, t.plus(-2))
                    act.activation(p_t[:, t.slot], pt_ps[:], ACT.Copy).then_inc(pt_ready, 1)
                    after(act, mix_ready, t.plus(-2))
                    act.activation(xn_late[:, t.slot], at(x_all, t.n), ACT.Identity, bias=column(norm.shift, t.n),
                                   scale=column(norm.rstd, t.n)).then_inc(late_ready, 1)
                if s.inside(TILES):
                    after(act, v_done, s)
                    after(act, o_done, s.plus(-2))
                    for out, src in v_copies(s, 1):
                        op = act.activation(out, src, ACT.Copy)
                    op.then_inc(v_odd_ready, 1)
                if s.inside(TILES):
                    after_dma(act, ctx_loaded, s)
                    after_dma(act, kop_written, s.plus(-2), 3)
                    act.activation(k_hi[:, s.slot], ctx_t[:, s.slot], ACT.Copy).then_inc(khi_ready, 1)
                    after(act, shift_ready, s)
                    after(act, pt_done, s.plus(-2))
                    after(act, den_ready, s.plus(-2))
                    act.activation(prob[:, s.slot], shifted[:, s.slot], ACT.Exp, scale=SCALE0).then_inc(prob_ready, 1)
                    if s.known and s.n == 0:
                        act.wait_ge(gate_loaded, 48)
                        act.activation(gates[:], gate_in[:, 0:4], ACT.Tanh).then_inc(gate_steps, 1)
                    if s.known and s.n == 2:
                        norm.scalar(act, slice(GT, XT))

            run_steps(act, step, TILES, 2, 2, 2)
            norm.scalar(act, EARLY)

        @block.tensor
        def _(pe):
            pe.wait_ge(w_loaded, 16 * 8)
            pe.wait_ge(ident_steps, 2)
            for m in range(4):
                pe.transpose(banks[0][:, m * P:(m + 1) * P], w_raw[:, m], ident[:])
            pe.transpose(banks[1][:, 0:P], w_raw[:, 4], ident[:]).then_inc(wt_done, 1)
            pe.wait_ge(wt_ready, 1)

            def step(s):
                t, u = s.plus(-1), s.plus(-2)
                if s.inside(TILES):
                    after(pe, xn_ready, s)
                    after_dma(pe, ctx_loaded, s)
                    after(pe, q_ready, s.plus(-2))
                    after(pe, k_ready, s.plus(-2))
                    for m, src in ((0, xn), (1, ctx_t)):
                        for c in range(DC):
                            o = (2 * m + c) * P
                            mm = pe.matmul(qk_ps[s.slot][:, o:o + P], lhsT=src[:, s.slot, c * P:(c + 1) * P], rhs=w_t[:, m],
                                           start=True, stop=True)
                    mm.then_inc(qk_done, 1)
                    after(pe, v_ready, s.plus(-1))
                    after(pe, v_odd_ready, s.plus(-1))
                    for b in range(2):
                        mm = pe.matmul(v_ps[:, b * D:(b + 1) * D], lhsT=w_t[:, 3 + b], rhs=ctx_t[:, s.slot], start=True, stop=True)
                    mm.then_inc(v_done, 1)
                if t.inside(TILES):
                    after(pe, prob_ready, t)
                    after(pe, pt_ready, t.plus(-1))
                    for hp in range(4):
                        mm = pe.transpose(pt_ps[:, hp * P:(hp + 1) * P], prob[:, t.slot, hp * P:(hp + 1) * P], ident[:])
                    mm.then_inc(pt_done, 1)
                if s.inside(TILES):
                    after(pe, q_ready, s)
                    after(pe, k_ready, s)
                    after(pe, shift_ready, s.plus(-2))
                    for c in range(DC):
                        for b in range(2):
                            mm = pe.matmul(s_ps[s.slot][b * SEQ:(b + 1) * SEQ, c * D:(c + 1) * D],
                                           lhsT=q_t[:, s.slot, c, b * SEQ:(b + 1) * SEQ],
                                           rhs=k_m[:, s.slot, c, b].rearrange("p h e -> p (h e)"),
                                           start=True, stop=True, tile_position=(0, b * SEQ))
                    mm.then_inc(score_done, 1)
                if t.inside(TILES):
                    after(pe, pt_ready, t)
                    after(pe, v_ready, t)
                    after(pe, v_odd_ready, t)
                    after(pe, head_ready, t.plus(-1))
                    for hp in range(4):
                        for b in range(2):
                            mm = pe.matmul(o_ps[b * SEQ:(b + 1) * SEQ, hp * SEQ:(hp + 1) * SEQ],
                                           lhsT=p_t[:, t.slot, hp * P + b * SEQ:hp * P + (b + 1) * SEQ],
                                           rhs=v_m[:, t.slot, b, hp].rearrange("p h n -> p (h n)"),
                                           start=True, stop=True, tile_position=(0, b * SEQ))
                    mm.then_inc(o_done, 1)
                if u.inside(TILES):
                    after(pe, mix_ready, u)
                    after(pe, x_ready, u.plus(-1))
                    pe.matmul(proj_ps[:, 0:D], lhsT=w_t[:, 2], rhs=mix[:, u.slot], start=True, stop=True).then_inc(proj_done, 1)

            run_steps(pe, step, TILES, 2, 2)

        @block.vector
        def _(dve):
            def statistics(g):
                dve.wait_ge(x_loaded[g], 16)
                for t in range(g * GT, (g + 1) * GT):
                    dve.bn_stats(norm.stats[:, t], x_all[:, t]).then_inc(stats0, 1)

            dve.wait_ge(ident_steps, 4)
            statistics(0)
            dve.wait_ge(stats0, GT)
            norm.vector(dve, slice(0, GT))
            dve.wait_ge(zeroed, 2)

            def normalise(n):
                after(dve, qk_done, n.plus(-2))
                norm.apply(dve, xn[:, n.slot], x_all, n.n).then_inc(xn_ready, 1)

            def step(s):
                t, u, n = s.plus(-1), s.plus(-2), s.plus(1)
                if t.inside(TILES):
                    after(dve, prob_ready, t)
                    dve.tensor_reduce(den[:, t.slot], prob[:, t.slot].rearrange("p (h e) -> p h e", h=H0), AX_X, ALU.add).then_inc(den_ready, 1)
                    after(dve, den_ready, t)
                    dve.reciprocal(rden[:, t.slot], den[:, t.slot]).then_inc(rden_ready, 1)
                if s.inside(TILES):
                    after(dve, v_done, s)
                    after(dve, o_done, s.plus(-2))
                    for out, src in v_copies(s, 0):
                        op = dve.tensor_copy(out, src)
                    op.then_inc(v_ready, 1)
                if s.inside(TILES):
                    normalise(n)
                    after(dve, score_done, s)
                    dve.tensor_reduce(smax[:, s.slot], s_ps[s.slot][:].rearrange("p (h e) -> p h e", h=H0), AX_X, ALU.max).then_inc(smax_ready, 1)
                    after(dve, smax_ready, s)
                    after(dve, prob_ready, s.plus(-2))
                    dve.tensor_tensor(shifted[:, s.slot].rearrange("p (h e) -> p h e", h=H0),
                                      s_ps[s.slot][:].rearrange("p (h e) -> p h e", h=H0),
                                      smax[:, s.slot].unsqueeze(2).to_broadcast([P, H0, SEQ]), ALU.subtract).then_inc(shift_ready, 1)
                if s.known and s.n == 2:
                    dve.wait_ge(stats0, TILES)
                    norm.vector(dve, slice(GT, XT), lambda: finished(t, u))
                elif s.known and s.n == TILES:
                    dve.wait_ge(st_ready, EARLY.stop)
                    norm.vector(dve, EARLY, lambda: finished(t, u))
                    normalised(dve, norm, keep["f0_xn"], x_all, Step(0, 0, 1), keep["f0_xn_ready"])
                else:
                    finished(t, u)
                if s.known and s.n < 2:
                    statistics(2 + s.n)
                if s.known and s.n == 1:
                    dve.wait_ge(gate_steps, 1)
                    dve.tensor_tensor(gates[:, 1:2], gates[:, 1:2], gate_in[:, 4:5], ALU.mult).then_inc(gate_steps, 1)
                    dve.wait_ge(gate_steps, 2)

            def finished(t, u):
                if t.inside(TILES):
                    after(dve, mix_ready, t.plus(-2))
                    after(dve, o_done, t)
                    after(dve, rden_ready, t)
                    dve.tensor_tensor(head[:, t.slot].rearrange("p (h n) -> p h n", h=H0),
                                      o_ps[:, 0:D].rearrange("p (h n) -> p h n", h=H0),
                                      rden[:, t.slot].unsqueeze(2).to_broadcast([P, H0, N0]), ALU.mult).then_inc(head_ready, 1)
                if u.inside(TILES):
                    after(dve, proj_done, u)
                    dve.scalar_tensor_tensor(at(x_all, u.n), proj_ps[:, 0:D], gates[:, 0:1], at(x_all, u.n), ALU.mult, ALU.add).then_inc(x_ready, 1)
                    after(dve, x_ready, u)
                    dve.bn_stats(at(norm.stats, u.n), at(x_all, u.n)).then_inc(st_ready, 1)

            normalise(Step(0, 0, 2))
            statistics(1)
            run_steps(dve, step, TILES, 2, 2, 2)
            dve.wait_ge(st_ready, TILES)


def normalised(dve, norm, xn, x_all, g, ready):
    for k in range(GT):
        op = norm.apply(dve, xn[:, k], x_all, g.n * GT + k)
    op.then_inc(ready, 1)


def feed_forward0(nc, sem, keep, d):
    x_all, norm, ident, gates = keep["x_all"], keep["norm"], keep["ident"], keep["gates"]
    w, wd_raw, queries, operands = keep["w0"], keep["wd0_raw"], keep["q"], keep["operands"]
    with ExitStack() as ctx:
        def sb(name, shape, dt):
            return ctx.enter_context(nc.sbuf_tensor(name, shape, dt))

        def pair(name, shape):
            return sb(name + "_hi", shape, F32R), sb(name + "_lo", shape, F32R)

        banks = [ctx.enter_context(nc.psum_tensor(f"f0_bank{i}", [P, 512], F32)) for i in range(8)]
        g_ps, u_ps, down_ps, xt_ps = banks[0:2], banks[2:4], banks[4:6], banks[6:8]

        wd = pair("wd0", [P, QUAD0, 4, D])
        xn, xn_ready = keep["f0_xn"], keep["f0_xn_ready"]
        xt = pair("f0_xt", [P, DC, GN])
        sg = sb("f0_sg", [P, 2, GN], F32)
        hid = keep["w0_raw"][:].rearrange("p m c i -> p (m c i)").rearrange("p (c j n) -> p c j n", c=2, j=4)
        mag = sb("f0_mag", [P, 4, GN], F32)
        beat_a, beat_b, beat_c = (sb(f"f0_beat_{n}", [P, 2, GN], BF16) for n in "abc")
        wins = sb("f0_wins", [P, 4, GN], BF16)
        sums = sb("f0_sums", [P, 4, GN], BF16)
        kept = sb("f0_kept", [P, 4, GN], F32)
        hs = pair("f0_hs", [P, 4, GN])

        whi_ready, w_ready = sem("f0_whi_ready"), sem("f0_w_ready")
        xt_done, xhi_ready, xt_ready = sem("f0_xt_done"), sem("f0_xhi_ready"), sem("f0_xt_ready")
        gate_done, up_done, silu_ready, hid_ready, mag_ready = (
            sem("f0_" + n) for n in ("gate_done", "up_done", "silu_ready", "hid_ready", "mag_ready"))
        beat_ready, wins_ready, sums_ready, kept_ready, hshi_ready, hs_ready = (
            sem("f0_" + n) for n in ("beat_ready", "wins_ready", "sums_ready", "kept_ready", "hshi_ready", "hs_ready"))
        down_done, x_ready, st_ready = sem("f0_down_done"), sem("f0_x_ready"), sem("f0_st_ready")

        block = ctx.enter_context(nc.Block())

        @block.tensor
        def _(pe):
            def transposes(g):
                after(pe, xn_ready, g)
                after(pe, xt_ready, g.plus(-1), DC)
                for dc in range(DC):
                    for k in range(GT):
                        mm = pe.transpose(xt_ps[dc][:, k * P:(k + 1) * P], xn[:, k, dc * P:(dc + 1) * P], ident[:])
                    mm.then_inc(xt_done, 1)

            def hidden(g, c):
                for j in range(4):
                    n = g.n * 8 + c * 4 + j
                    slot = j % 2
                    for m, ps, free, done in ((0, g_ps, silu_ready, gate_done), (1, u_ps, hid_ready, up_done)):
                        if not (g.known and n < 2):
                            pe.wait_ge(free, n - 1)
                        for dc in range(DC):
                            if c == 0 and j == 0 and m == 0:
                                after(pe, xt_ready, g, DC, dc + 1)
                            mm = product3(pe, ps[slot][:], [part[:, m, dc, j, c * P:(c + 1) * P] for part in w],
                                          (xt[0][:, dc], xt[1][:, dc]), dc == 0, dc == DC - 1)
                        mm.then_inc(done, 1)

            def down(g, c):
                if g.known and g.n < 0:
                    return
                if c == 0:
                    after(pe, x_ready, g.plus(-1), GT)
                if g.known and g.n == 0:
                    pe.wait_ge(w_ready, 4 * (c + 1))
                for i, j in enumerate(MEMBERS):
                    pe.wait_ge(hs_ready, g.n * 8 + c * 4 + i + 1)
                    for k in range(GT):
                        cols = slice(k * P, (k + 1) * P)
                        mm = product3(pe, down_ps[k // 2][:, (k % 2) * D:(k % 2 + 1) * D],
                                      (hs[0][:, j, cols], hs[1][:, j, cols]), (wd[0][:, c, j], wd[1][:, c, j]),
                                      c == 0 and i == 0 and k % 2 == 0, c == QUAD0 - 1 and i == 3, skip_group_check=True)
                mm.then_inc(down_done, 1)

            def group(g):
                hidden(g, 0)
                down(g.plus(-1), 1)
                if g is not LAST:
                    transposes(g.plus(1))
                hidden(g, 1)
                down(g, 0)

            transposes(Step(0, 0, 1))
            group(Step(0, 0, 1))
            with pe.Fori(1, GROUPS - 1) as r:
                group(Step(r, 0, 1))
            group(LAST)
            down(Step(GROUPS - 1, 0, 1), 1)

        @block.scalar
        def _(act):
            def xt_high(g):
                after(act, up_done, g.plus(-1), 8)
                for dc in range(DC):
                    after(act, xt_done, g, DC, dc + 1)
                    act.activation(xt[0][:, dc], xt_ps[dc][:], ACT.Copy).then_inc(xhi_ready, 1)

            def hidden_high(s, i):
                n, j = s * 4 + i, MEMBERS[i]
                act.wait_ge(kept_ready, n + 1)
                if not (isinstance(s, int) and s < 1):
                    act.wait_ge(down_done, s)
                act.activation(hs[0][:, j], kept[:, j], ACT.Copy).then_inc(hshi_ready, 1)

            def group(g):
                for c in range(2):
                    s = g.n * 2 + c
                    for j in range(4):
                        n = s * 4 + j
                        first = g.known and g.n == 0 and c == 0
                        if j >= 2 and not first:
                            for i in ((0, 1, 2), (3,))[j - 2]:
                                hidden_high(s - 1, i)
                        act.wait_ge(gate_done, n + 1)
                        if not (first and j < 2):
                            act.wait_ge(hid_ready, n - 1)
                        act.activation(sg[:, j % 2], g_ps[j % 2][:], ACT.Silu).then_inc(silu_ready, 1)
                        act.wait_ge(hid_ready, n + 1)
                        if not first:
                            act.wait_ge(beat_ready, s)
                        act.activation(mag[:, j], hid[:, c, j], ACT.Abs).then_inc(mag_ready, 1)
                if g is not LAST:
                    xt_high(g.plus(1))

            xt_high(Step(0, 0, 1))
            norm.scalar(act, LATE)
            group(Step(0, 0, 1))
            with act.Fori(1, GROUPS - 1) as r:
                group(Step(r, 0, 1))
            group(LAST)
            norm.scalar(act, EARLY)
            act.wait_ge(norm.steps, norm.rooted)
            for tile in range(2):
                queries.high(act, norm, x_all, Step(0, tile, 2))
            for i in range(4):
                hidden_high(2 * GROUPS - 1, i)

        @block.gpsimd
        def _(pool):
            pool.wait_ge(keep["wd0_loaded"], 16)
            for c in range(QUAD0):
                for j in range(4):
                    pool.tensor_copy(wd[0][:, c, j], wd_raw[:, c, j]).then_inc(whi_ready, 1)
                for j in range(4):
                    pool.wait_ge(whi_ready, 4 * c + j + 1)
                    pool.tensor_tensor(wd[1][:, c, j], wd_raw[:, c, j], raw(wd[0][:, c, j]), ALU.subtract).then_inc(w_ready, 1)

            def hidden_low(s):
                for i, j in enumerate(MEMBERS):
                    pool.wait_ge(hshi_ready, s * 4 + (i + 1))
                    pool.tensor_tensor(hs[1][:, j], kept[:, j], raw(hs[0][:, j]), ALU.subtract).then_inc(hs_ready, 1)

            with pool.Fori(0, 2 * GROUPS - 2) as s:
                hidden_low(s)
            operands.clear(pool, 0)
            hidden_low(2 * GROUPS - 2)
            for tile in range(2):
                queries.low(pool, Step(0, tile, 2))
            hidden_low(2 * GROUPS - 1)

        @block.sync
        def _(sp):
            tiles = [Step(0, tile, 2) for tile in range(2)]
            sp.wait_ge(operands.cleared, 1)
            for h in range(2):
                operands.load_k(sp, d, tiles[0], h)
            for t in tiles:
                after(sp, queries.lo_ready, t)
                queries.store(sp, d, t)
            queries.after_store(sp, tiles[0])
            for h in range(2):
                operands.load_q(sp, d, tiles[0], h)

        @block.vector
        def _(dve):

            def xt_low(g):
                for dc in range(DC):
                    after(dve, xhi_ready, g, DC, dc + 1)
                    dve.tensor_tensor(xt[1][:, dc], xt_ps[dc][:], raw(xt[0][:, dc]), ALU.subtract).then_inc(xt_ready, 1)

            def hidden(g, c, j):
                n = g.n * 8 + c * 4 + j
                dve.wait_ge(silu_ready, n + 1)
                dve.wait_ge(up_done, n + 1)
                if not (g.known and g.n == 0):
                    dve.wait_ge(mag_ready, n - 7)
                dve.tensor_tensor(hid[:, c, j], sg[:, j % 2], u_ps[j % 2][:], ALU.mult).then_inc(hid_ready, 1)

            def compare(s, meanwhile):
                dve.wait_ge(mag_ready, s * 4 + 4)
                if not (isinstance(s, int) and s < 1):
                    dve.wait_ge(sums_ready, s * 2)
                dve.tensor_tensor(beat_a[:], mag[:, 0:2], mag[:, 2:4], ALU.is_ge)
                meanwhile()
                dve.tensor_tensor(beat_b[:, 0], mag[:, 0], mag[:, 3], ALU.is_ge)
                dve.tensor_tensor(beat_b[:, 1], mag[:, 1], mag[:, 2], ALU.is_ge)
                dve.tensor_tensor(beat_c[:], mag[:, 0:4:2], mag[:, 1:4:2], ALU.is_ge).then_inc(beat_ready, 1)

            def count(s, between=None):
                def last_win():
                    dve.tensor_tensor(wins[:, 2], beat_a[:, 0], beat_b[:, 1], ALU.add).then_inc(wins_ready, 1)

                dve.wait_ge(beat_ready, s + 1)
                dve.tensor_tensor(wins[:, 0:2], beat_a[:], beat_b[:], ALU.add)
                dve.tensor_tensor(wins[:, 3], beat_a[:, 1], beat_b[:, 0], ALU.add).then_inc(wins_ready, 1)
                if not between:
                    last_win()
                dve.wait_ge(wins_ready, s * 2 + 1)
                if not (isinstance(s, int) and s < 1):
                    dve.wait_ge(kept_ready, s * 4)
                dve.tensor_tensor(sums[:, 0:4:3], wins[:, 0:4:3], beat_c[:], ALU.add).then_inc(sums_ready, 1)
                if between:
                    between()
                    last_win()
                dve.wait_ge(wins_ready, s * 2 + 2)
                dve.tensor_tensor(sums[:, 1:3], wins[:, 1:3], beat_c[:], ALU.subtract).then_inc(sums_ready, 1)

            def keep_two(s, c, members):
                for i in members:
                    j = MEMBERS[i]
                    dve.wait_ge(sums_ready, s * 2 + (1 if i < 2 else 2))
                    op, bound = ((ALU.is_ge, 2.0), (ALU.is_ge, 1.0), (ALU.is_le, 0.0), (ALU.is_le, 1.0))[j]
                    if not (isinstance(s, int) and s < 1):
                        dve.wait_ge(hs_ready, s * 4 + (i - 3))
                    dve.scalar_tensor_tensor(kept[:, j], sums[:, j], bound, hid[:, c, j], op, ALU.mult).then_inc(kept_ready, 1)

            def residual(g):
                after(dve, down_done, g, 2)
                for k in range(GT):
                    t = g.n * GT + k
                    dve.scalar_tensor_tensor(at(x_all, t), down_ps[k // 2][:, (k % 2) * D:(k % 2 + 1) * D], gates[:, 2:3],
                                             at(x_all, t), ALU.mult, ALU.add).then_inc(x_ready, 1)

            def statistics(g):
                for k in range(GT):
                    t = g.n * GT + k
                    dve.wait_ge(x_ready, t + 1)
                    dve.bn_stats(at(norm.stats, t), at(x_all, t)).then_inc(st_ready, 1)

            def group(g):
                first = g.known and g.n == 0
                for c in range(2):
                    s = g.n * 2 + c
                    lagged = not (first and c == 0)
                    hidden(g, c, 0)
                    if lagged:
                        keep_two(s - 1, 1 - c, (0, 1, 2))
                    hidden(g, c, 1)
                    if lagged:
                        keep_two(s - 1, 1 - c, (3,))
                    if c == 0 and g is not LAST:
                        after(dve, xt_done, g, DC)
                        normalised(dve, norm, xn, x_all, g.plus(1), xn_ready)
                    if c == 1 and not first:
                        residual(g.plus(-1))
                    hidden(g, c, 2)
                    if c == 1 and not first:
                        statistics(g.plus(-1))
                    hidden(g, c, 3)
                    if g is LAST and c == 1:
                        dve.wait_ge(st_ready, EARLY.stop)
                        norm.vector(dve, EARLY, lambda: compare(s, lambda: None))
                    else:
                        compare(s, (lambda: xt_low(g.plus(1))) if c == 1 else (lambda: None))
                    count(s, (lambda: keep_two(s, c, (0, 1))) if g is LAST and c == 1 else None)

            xt_low(Step(0, 0, 1))
            norm.vector(dve, LATE)
            group(Step(0, 0, 1))
            with dve.Fori(1, GROUPS - 1) as r:
                group(Step(r, 0, 1))
            group(LAST)
            keep_two(2 * GROUPS - 1, 1, (2, 3))
            residual(Step(GROUPS - 1, 0, 1))
            dve.wait_ge(x_ready, TILES)


def attention1(nc, sem, keep, d):
    x_all, norm, ident, gates = keep["x_all"], keep["norm"], keep["ident"], keep["gates"]
    sel_out, sel_den = keep["sel_out"], keep["sel_den"]
    w, wd, a, queries, operands = keep["w1"], keep["wd1"], d["a"], keep["q"], keep["operands"]
    qop, kop, op_loaded = operands.q, operands.k, operands.loaded
    turned = keep["turned"]
    PAIRS = UNITS // 2
    FULL = DS // P
    with ExitStack() as ctx:
        def sb(name, shape, dt):
            return ctx.enter_context(nc.sbuf_tensor(name, shape, dt))

        s_ps = [ctx.enter_context(nc.psum_tensor(f"a1_s{i}", [P, 2, 512], F32)) for i in range(2)]
        st_ps = [ctx.enter_context(nc.psum_tensor(f"a1_st{i}", [P, 512], F32)) for i in range(2)]
        pv_ps = ctx.enter_context(nc.psum_tensor("a1_pv", [P, 512], F32))
        misc = ctx.enter_context(nc.psum_tensor("a1_misc", [P, 512], F32))

        operands.add_slot(sb)
        ctx_t = sb("a1_ctx", [P, 2, D], F32)
        vt = sb("a1_vt", [P, 2, DC, UNITS, 32], F32)
        smax = sb("a1_smax", [P, 2, UNITS, 2], F32)
        neg = sb("a1_neg", [P, 2, 2, HALF], F32R)
        neg_t = sb("a1_neg_t", [HALF, 2, D], F32)
        prob = sb("a1_prob", [P, 8, 2 * D], F32)
        pv = sb("a1_pv_sb", [P, 2, QUADS, D], F32)
        back = sb("a1_back", [P, 2, D], F32)
        rden = sb("a1_rden", [P, D], F32)
        att = sb("a1_att", [P, D], F32)

        vt_cleared, last_stats = sem("a1_vt_cleared"), sem("a1_last_stats")
        max_loaded = [[sem(f"a1_max_loaded{i}{h}") for i in range(2)] for h in range(2)]
        ctx_loaded = [sem(f"a1_ctx_loaded{i}") for i in range(2)]
        s_done, smax_ready, neg_ready, neg_done, neg_t_ready = (
            sem("a1_" + n) for n in ("s_done", "smax_ready", "neg_ready", "neg_done", "neg_t_ready"))
        st_done, prob_ready, pv_done, pv_ready = (sem("a1_" + n) for n in ("st_done", "prob_ready", "pv_done", "pv_ready"))
        vt_done, vt_ready, sel_done, back_ready, rden_ready, att_ready, x_ready, st_ready = (
            sem("a1_" + n) for n in ("vt_done", "vt_ready", "sel_done", "back_ready", "rden_ready", "att_ready", "x_ready", "st_ready"))
        BORROWED = 5
        ws_raw = prob[:, BORROWED:].rearrange("p u n -> p (u n)")[:, 0:2 * DC * DS].rearrange("p (m c i) -> p m c i", m=2, c=DC)
        wsd_raw = turned.plain[:].rearrange("p c n -> p (c n)")[:, 0:(CH1 - CHR) * D].rearrange("p (c n) -> p c n", n=D)
        we_raw = sb("we_raw", [P, 2, DC, DE], F32)
        wed_raw = sb("wed_raw", [P, 2, D], F32)
        ws_loaded, shared_hi, shared_lo = sem("ws_loaded"), sem("shared_hi"), sem("shared_lo")
        we_loaded, wed_loaded = [sem("we_loaded0"), sem("we_loaded1")], [sem("wed_loaded0"), sem("wed_loaded1")]
        split_hi, split_lo = sem("a1_split_hi"), sem("a1_split_lo")

        block = ctx.enter_context(nc.Block())
        LAG = 3
        FIRST = Step(0, 0, 1)
        first_xn = vt[:, (TILES - 2) % 2].rearrange("p c u n -> p (c u n)").rearrange("p (k n) -> p k n", k=GT)

        shared = [(ws_raw, w[0][:, :, :, E * DE:I1], w[1][:, :, :, E * DE:I1]),
                  (wsd_raw[:, 0:FULL], wd[0][:, CHR:CHR + FULL], wd[1][:, CHR:CHR + FULL]),
                  (wsd_raw[0:LASTM, FULL], wd[0][0:LASTM, CH1 - 1], wd[1][0:LASTM, CH1 - 1])]

        def last_chunk(n):
            return n.rnd - 1 + n.slot * (CHR - TILES // 2 + 1)

        def prepared_here(m):
            return not m.known or 2 <= m.n < TILES

        def has_chunk(n):
            return not n.known or n.rnd >= 1

        def pieces(n):
            cols = columns(n.rnd, DE)
            out = [(we_raw[:, n.slot], w[0][:, n.slot, :, cols], w[1][:, n.slot, :, cols])]
            if has_chunk(n):
                out.append((wed_raw[:, n.slot], at(wd[0], last_chunk(n)), at(wd[1], last_chunk(n))))
            return out

        @block.sync
        def _(sp):
            def load_shared():
                for m, name in enumerate(("L1_ffn_Ws_gate", "L1_ffn_Ws_up")):
                    sp.dma_start(ws_raw[:, m], a[name].rearrange("(c p) j -> p c j", p=P)).then_inc(ws_loaded, 16)
                down = a["L1_ffn_Ws_down"]
                sp.dma_start(wsd_raw[:, 0:FULL], down[0:FULL * P].rearrange("(c p) n -> p c n", p=P)).then_inc(ws_loaded, 16)
                sp.dma_start(wsd_raw[0:LASTM, FULL], down[FULL * P:DS]).then_inc(ws_loaded, 16)

            def load_pieces(n):
                after(sp, split_lo, n.plus(-2))
                src = a[("L1_ffn_We_gate", "L1_ffn_We_up")[n.slot]].rearrange("e (c p) j -> p e c j", p=P)
                src = src[:, n.rnd] if n.known else src[:, bass.ds(n.rnd, 1)].rearrange("p o c j -> p (o c) j")
                sp.dma_start(we_raw[:, n.slot], src).then_inc(we_loaded[n.slot], 16)
                if has_chunk(n):
                    src = a["L1_ffn_We_down"].rearrange("e j n -> (e j) n").rearrange("(c p) n -> c p n", p=P)
                    sp.dma_start(wed_raw[:, n.slot], dram_at(src, last_chunk(n))).then_inc(wed_loaded[n.slot], 16)
            def maxima(t, h):
                if not t.inside(TILES):
                    return
                after(sp, neg_t_ready, t, 2, h + 1)
                sp.dma_start(raw(qop[t.slot][MROW:P, 2 * h:2 * h + 2]), neg_t[:, h]).then_inc(max_loaded[h][t.slot], 16)

            def load_operands(t, h):
                if not t.inside(TILES) or (t.known and t.n == 0):
                    return
                after(sp, st_done, t.plus(-2), UNITS, 8 * (h + 1))
                if t.known and t.n == 1:
                    sp.wait_ge(operands.cleared, 2)
                operands.load_k(sp, d, t, h)
                queries.after_store(sp, t)
                operands.load_q(sp, d, t, h)

            def step(s):
                maxima(s.plus(-2), 1)
                v = s.plus(-1)
                if v.inside(TILES):
                    after(sp, vt_done, v.plus(-2))
                    sp.dma_start(ctx_t[:, v.slot], dram_at(d["ctx"], v.n)).then_inc(ctx_loaded[v.slot], 16)
                load_operands(s, 0)
                maxima(s.plus(-1), 0)
                if s.inside(TILES) and not (s.known and s.n == 0):
                    load_pieces(s)
                load_operands(s, 1)
                if s.known and s.n == 0:
                    load_pieces(s)
                    load_shared()

            run_steps(sp, step, TILES, LAG, 2)

        @block.gpsimd
        def _(pool):
            operands.clear(pool, 1)
            pool.memset(vt[:], 0.0).then_inc(vt_cleared, 1)
            pool.wait_ge(vt_cleared, 1)
            pool.memset(vt[:, :, :, :, D1:D1 + 1], 1.0).then_inc(vt_cleared, 1)

            def step(s):
                n, l, o = s.plus(-1), s.plus(-2), s.plus(-3)
                m = s.plus(1)
                if prepared_here(m):
                    queries.low(pool, m)
                    after(pool, queries.lo_ready, m)
                    for h in range(2):
                        after_dma(pool, op_loaded[h], m.plus(-2), 8)
                if n.inside(TILES):
                    after_dma(pool, we_loaded, n)
                    if has_chunk(n):
                        after_dma(pool, wed_loaded, n.plus(-2))
                if l.inside(TILES):
                    after(pool, split_hi, l)
                    for src, hi, lo in pieces(l):
                        op = pool.tensor_tensor(lo, src, raw(hi), ALU.subtract)
                    op.then_inc(split_lo, 1)
                if prepared_here(m):
                    queries.store(pool, d, m)
                if n.inside(TILES):
                    for src, hi, lo in pieces(n):
                        op = pool.tensor_copy(hi, src)
                    op.then_inc(split_hi, 1)
                if s.known and s.n in (1, 2):
                    for k in ((0,), (1, 2))[s.n - 1]:
                        src, hi, lo = shared[k]
                        pool.wait_ge(shared_hi, k + 1)
                        pool.tensor_tensor(lo, src, raw(hi), ALU.subtract).then_inc(shared_lo, 1)
                if o.inside(TILES):
                    after(pool, rden_ready, o, 2)
                    after(pool, x_ready, o.plus(-1))
                    pool.tensor_tensor(att[:], back[:, 0], rden[:], ALU.mult).then_inc(att_ready, 1)
                    after(pool, att_ready, o)
                    pool.tensor_tensor(at(x_all, o.n), at(x_all, o.n), att[:], ALU.add).then_inc(x_ready, 1)

            run_steps(pool, step, TILES, LAG, 2)
            pool.wait_ge(split_lo, TILES)
            pool.wait_ge(shared_lo, len(shared))
            for slot in range(2):
                pool.wait_ge(queries.written[slot], 16 * 3 * (TILES // 2 - (slot == 1)))

        @block.scalar
        def _(act):
            norm.scalar(act, LATE)
            act.wait_ge(norm.steps, norm.rooted)

            def step(s):
                v, t, o = s.plus(-1), s.plus(-2), s.plus(-3)
                def maxima_copied(w_, h):
                    if w_.inside(TILES):
                        after(act, neg_done, w_, 2, h + 1)
                        after_dma(act, max_loaded[h], w_.plus(-1))
                        act.activation(neg_t[:, h], misc[0:HALF, 0:D], ACT.Copy).then_inc(neg_t_ready, 1)

                def weighted(w_, q):
                    if w_.inside(TILES):
                        after(act, pv_done, w_, QUADS, q + 1)
                        after(act, sel_done, w_.plus(-2))
                        act.activation(pv[:, w_.slot, q], pv_ps[:, 0:D], ACT.Copy).then_inc(pv_ready, 1)

                if s.known and s.n == TILES + LAG - 1:
                    norm.scalar(act, EARLY)
                for u in range(UNITS):
                    j = u // 2
                    if t.inside(TILES):
                        after(act, st_done, t, UNITS, u + 1)
                        quad = (u - 8) // 4
                        if quad >= 0:
                            after(act, pv_done, t, QUADS, quad + 1)
                        else:
                            after(act, pv_done, t.plus(-1), QUADS, quad + QUADS + 1)
                        if t.known and t.n == 0 and u == BORROWED:
                            act.wait_ge(shared_lo, 1)
                        act.activation(prob[:, u % 8], st_ps[u % 2][:], ACT.Exp, scale=SCALE1).then_inc(prob_ready, 1)
                    if u == 2:
                        maxima_copied(t, 1)
                    if u == 5 and prepared_here(s.plus(1)):
                        queries.high(act, norm, x_all, s.plus(1))
                    if u == 6 and s.known and s.n == 1:
                        act.wait_ge(ws_loaded, 64)
                        for src, hi, lo in shared:
                            act.activation(hi, src, ACT.Copy).then_inc(shared_hi, 1)
                    if u == 3:
                        weighted(o, 3)
                    if u == 9 and o.inside(TILES):
                        after(act, sel_done, o)
                        after(act, att_ready, o.plus(-1))
                        act.activation(back[:].rearrange("p m n -> p (m n)"), misc[:], ACT.Copy).then_inc(back_ready, 1)
                    if u == 11:
                        maxima_copied(v, 0)
                    if u == 14 and v.inside(TILES):
                        after(act, vt_done, v)
                        act.activation(vt[:, v.slot, :, :, 0:D1], misc[:, 0:D].rearrange("p (c u r) -> p c u r", c=DC, r=D1),
                                       ACT.Identity, scale=gates[:, 1:2]).then_inc(vt_ready, 1)
                    if u in (7, 11, 15):
                        weighted(t, (u - 7) // 4)

            run_steps(act, step, TILES, LAG, 2)
            act.wait_ge(shared_lo, len(shared))
            for dc in range(DC):
                turned.copy(act, FIRST, dc, s_ps[0][:, dc])
            turned.high(act, FIRST)

        @block.tensor
        def _(pe):
            def step(s):
                v, t, o = s.plus(-1), s.plus(-2), s.plus(-3)

                def turn(w_, h, before):
                    if w_.inside(TILES):
                        after(pe, neg_ready, w_, 2, h + 1)
                        before()
                        for q in range(2):
                            mm = pe.transpose(misc[0:HALF, q * P:(q + 1) * P], raw(neg[:, h, q]), ident[:])
                        mm.then_inc(neg_done, 1)

                def products(w_, q, c):
                    if not w_.inside(TILES):
                        return
                    if c == 0:
                        after(pe, prob_ready, w_, UNITS, 4 * q + 4)
                        after(pe, vt_ready, w_)
                        if q:
                            after(pe, pv_ready, w_, QUADS, q)
                        else:
                            after(pe, pv_ready, w_.plus(-1), QUADS)
                    for v4 in range(4):
                        u = 4 * q + v4
                        mm = pe.matmul(pv_ps[v4 * 32:(v4 + 1) * 32, 0:D], lhsT=vt[:, w_.slot, c, u],
                                       rhs=prob[:, u % 8, c * D:(c + 1) * D], start=(c == 0), stop=(c == DC - 1),
                                       tile_position=(0, v4 * 32))
                    if c == DC - 1:
                        mm.then_inc(pv_done, 1)

                def selected(w_, m):
                    if not w_.inside(TILES):
                        return
                    if m == 0:
                        after(pe, pv_ready, w_, QUADS)
                        if t.inside(TILES):
                            after(pe, neg_t_ready, t, 2)
                    for q in range(QUADS):
                        mm = pe.matmul(misc[q * 32:(q + 1) * 32, m * D:(m + 1) * D], lhsT=(sel_out, sel_den)[m][:],
                                       rhs=pv[:, w_.slot, q], start=True, stop=True, tile_position=(0, q * 32))
                    if m == 1:
                        mm.then_inc(sel_done, 1)

                for u in range(UNITS):
                    j, k = divmod(u, 2)
                    if t.inside(TILES):
                        if u % HALF == 0:
                            after_dma(pe, max_loaded[u // HALF], t)
                        if u >= 2:
                            after(pe, prob_ready, t, UNITS, u - 1)
                        else:
                            after(pe, prob_ready, t.plus(-1), UNITS, UNITS - 1 + u)
                        for c in range(DC):
                            mm = pe.matmul(st_ps[u % 2][:, c * D:(c + 1) * D], lhsT=kop[t.slot][:, u // 4, c * P:(c + 1) * P],
                                           rhs=qop[t.slot][:, u // 4, u % 4], start=True, stop=True)
                        mm.then_inc(st_done, 1)
                    if v.inside(TILES):
                        if u % HALF == 0:
                            after_dma(pe, op_loaded[u // HALF], v, 8)
                        if k == 0 and j >= 2:
                            after(pe, smax_ready, v, PAIRS, j - 1)
                        elif k == 0:
                            after(pe, smax_ready, v.plus(-1), PAIRS, PAIRS - 1 + j)
                        for q in range(2):
                            mm = pe.matmul(s_ps[j % 2][:, k, q * D:(q + 1) * D], lhsT=qop[v.slot][0:MROW, u // 4, u % 4, q * P:(q + 1) * P],
                                           rhs=kop[v.slot][0:MROW, u // 4], start=True, stop=True)
                        if k == 1:
                            mm.then_inc(s_done, 1)
                    if u == 2:
                        turn(t, 1, lambda: after(pe, vt_ready, t))
                    if u in (1, 3):
                        products(o, 3, u // 2)
                    if u % 2 and u > 3:
                        products(t, u // 4 - 1, u % 4 // 2)
                    if u in (6, 8):
                        selected(o, u // 2 - 3)
                    if u == 11:
                        def before():
                            after(pe, neg_t_ready, t, 2)
                            after(pe, back_ready, o)
                        turn(v, 0, before)
                    if u == 14 and v.inside(TILES):
                        after_dma(pe, ctx_loaded, v)
                        after(pe, neg_t_ready, v, 2, 1)
                        if v.known and v.n == 0:
                            pe.wait_ge(vt_cleared, 2)
                        for c in range(DC):
                            mm = pe.transpose(misc[:, c * P:(c + 1) * P], ctx_t[:, v.slot, c * P:(c + 1) * P], ident[:])
                        mm.then_inc(vt_done, 1)

            run_steps(pe, step, TILES, LAG, 2)
            pe.wait_ge(turned.xn_ready, 1)
            pe.wait_ge(smax_ready, TILES * PAIRS)
            for dc in range(DC):
                turned.transpose(pe, first_xn, dc, s_ps[0][:, dc], ident)

        @block.vector
        def _(dve):
            for t in range(TILES - GT, TILES):
                dve.bn_stats(norm.stats[:, t], x_all[:, t]).then_inc(last_stats, 1)
            dve.wait_ge(last_stats, GT)
            norm.vector(dve, LATE)

            def step(s):
                v, t, o, p = s.plus(-1), s.plus(-2), s.plus(-3), s.plus(-4)

                def negated(w_, h):
                    if not w_.inside(TILES):
                        return
                    src = smax[:, w_.slot, 8 * h:8 * h + 8].rearrange("p u q -> p q u")
                    after(dve, smax_ready, w_, PAIRS, 4 * h + 4)
                    after(dve, neg_done, w_.plus(-1), 2, h + 1)
                    dve.tensor_scalar(neg[:, h], src, -1.0, None, ALU.mult).then_inc(neg_ready, 1)

                negated(t, 1)
                if s.known and s.n == TILES + LAG - 1:
                    dve.wait_ge(st_ready, EARLY.stop)
                    norm.vector(dve, EARLY)
                    dve.wait_ge(pv_done, (TILES - 1) * QUADS)
                    for k in range(GT):
                        op = norm.apply(dve, first_xn[:, k], x_all, k)
                    op.then_inc(turned.xn_ready, 1)
                for j in range(PAIRS):
                    if j == 4:
                        negated(v, 0)
                    if v.inside(TILES):
                        after(dve, s_done, v, PAIRS, j + 1)
                        dve.tensor_reduce(smax[:, v.slot, 2 * j:2 * j + 2].rearrange("p u q -> p (u q)"),
                                          s_ps[j % 2][:].rearrange("p u (q n) -> p (u q) n", q=2), AX_X, ALU.max).then_inc(smax_ready, 1)
                    if j in (5, 6) and o.inside(TILES):
                        cols = slice((j - 5) * P, (j - 4) * P)
                        after(dve, back_ready, o)
                        after(dve, att_ready, o.plus(-1))
                        dve.reciprocal(rden[:, cols], back[:, 1, cols]).then_inc(rden_ready, 1)
                    if j == 1 and s.known and s.n == TILES + LAG:
                        turned.low(dve, FIRST)
                    if j == 1 and p.inside(TILES):
                        after(dve, x_ready, p)
                        dve.bn_stats(at(norm.stats, p.n), at(x_all, p.n)).then_inc(st_ready, 1)

            run_steps(dve, step, TILES, LAG + 1, 2)
            dve.wait_ge(st_ready, TILES)


def feed_forward1(nc, sem, keep, d):
    x_all, norm, ident, gates = keep["x_all"], keep["norm"], keep["ident"], keep["gates"]
    wgu, wd = keep["w1"], keep["wd1"]
    a, turned = d["a"], keep["turned"]
    xt, xt32 = turned.parts, turned.plain
    with ExitStack() as ctx:
        def sb(name, shape, dt):
            return ctx.enter_context(nc.sbuf_tensor(name, shape, dt))

        def pair(name, shape):
            return sb(name + "_hi", shape, F32R), sb(name + "_lo", shape, F32R)

        banks = [ctx.enter_context(nc.psum_tensor(f"f1_bank{i}", [P, 512], F32)) for i in range(8)]
        g_ps, u_ps, down_ps, mix_ps, misc = banks[0:2], banks[2:4], banks[4:6], banks[6], banks[7]

        wr = sb("f1_wr", [P, DC, E], F32)
        xn = sb("f1_xn", [P, GT, D], F32)
        sg = sb("f1_sg", [P, 2, GN], F32)
        prod = sb("f1_prod", [P, 2, GN], F32)
        hid = sb("f1_hid", [P, 2, GN], F32)
        hs = pair("f1_hs", [P, 2, GN])
        logit = sb("f1_logit", [P, GT, E], F32)
        lmax = sb("f1_lmax", [P, GT], F32)
        expo = sb("f1_expo", [P, GT, E], F32)
        esum = sb("f1_esum", [P, GT], F32)
        score = sb("f1_score", [P, GT, E], F32)
        above = sb("f1_above", [P, GT, E, E], F32)
        same = sb("f1_same", [P, GT, E, E], F32)
        rank = sb("f1_rank", [P, GT, E], F32)
        weight = sb("f1_weight", [P, GT, E], F32)
        parts = sb("f1_parts", [P, GT, 2, E], F32R)
        parts_t = sb("f1_parts_t", [2 * E, GN], F32R)
        earlier = sb("f1_earlier", [P, E, E], F32)
        sel_e = sb("f1_sel_e", [2 * E, CHR, P], F32R)
        sel_a = sb("f1_sel_a", [2 * E, 2, CHR * P], F32)

        wr_loaded, consts = sem("f1_wr_loaded"), sem("f1_consts")
        gate_done, up_done, silu_ready, prod_ready, mix_done, hid_ready, hshi_ready, hs_ready, chunk_done = (
            sem("f1_" + n) for n in ("gate_done", "up_done", "silu_ready", "prod_ready", "mix_done", "hid_ready", "hshi_ready",
                                     "hs_ready", "chunk_done"))
        logit_done, r_steps, exp_ready, parts_ready, parts_done, parts_t_ready = (
            sem("f1_" + n) for n in ("logit_done", "r_steps", "exp_ready", "parts_ready", "parts_done", "parts_t_ready"))
        x_ready, stored, half_done = sem("f1_x_ready"), sem("stored"), sem("f1_half_done")
        R_STEPS = 11

        SHARED = CH1 - CHR

        def chunk_of(i):
            return (i + CHR) % CH1

        def rows(i):
            return P if chunk_of(i) < CH1 - 1 else LASTM

        def multiplied(eng, g, i):
            q, i = divmod(i, CH1)
            if g.known and g.n + q < 0:
                return
            if i >= SHARED:
                eng.wait_ge(prod_ready, (g.n + q) * CHR + (i - SHARED + 1))
            else:
                eng.wait_ge(hid_ready, (g.n + q) * CH1 + (i + 1))

        block = ctx.enter_context(nc.Block())

        @block.sync
        def _(sp):
            sp.dma_start(wr[:], a["L1_ffn_W_router"].rearrange("(c p) e -> p c e", p=P)).then_inc(wr_loaded, 16)
            done = [(g + 1) * GT for g in range(GROUPS - 1)] + list(range(TILES - GT + 1, TILES + 1))
            for first, end in zip([0] + done, done):
                sp.wait_ge(x_ready, end)
                sp.dma_start(d["out"][first:end].rearrange("t p n -> p t n"), x_all[:, first:end]).then_inc(stored, 16)
            sp.wait_ge(stored, 16 * len(done))

        @block.tensor
        def _(pe):
            def transposes(g, dc):
                if dc == 0:
                    after(pe, turned.xn_ready, g)
                    after(pe, parts_t_ready, g.plus(-1))
                else:
                    after(pe, turned.plain_ready, g, 2, 1)
                turned.transpose(pe, xn, dc, misc, ident)

            def router(g):
                after(pe, turned.plain_ready, g, 2)
                for k in range(GT):
                    for dc in range(DC):
                        mm = pe.matmul(misc[:, k * E:(k + 1) * E], lhsT=xt32[:, dc, k * P:(k + 1) * P], rhs=wr[:, dc],
                                       start=(dc == 0), stop=(dc == DC - 1))
                mm.then_inc(logit_done, 1)

            def weights(g):
                after(pe, parts_ready, g, 2)
                for k in range(GT):
                    mm = pe.transpose(misc[0:2 * E, k * P:(k + 1) * P], raw(parts[:, k].rearrange("p a e -> p (a e)")), ident[:])
                mm.then_inc(parts_done, 1)

            def hidden(g, c):
                n, slot = g.n * CH1 + c, c % 2
                r, i = rows(c), chunk_of(c) * P
                for m, ps, done in ((0, g_ps, gate_done), (1, u_ps, up_done)):
                    if m == 1:
                        multiplied(pe, g, c - 2)
                    elif not (g.known and n < 2):
                        pe.wait_ge(silu_ready, n - 1)
                    for dc in range(DC):
                        if c == 0 and m == 0:
                            after(pe, turned.ready, g, DC, dc + 1)
                        lhs = [t[:, m, dc, i:i + r] for t in wgu]
                        mm = product3(pe, ps[slot][0:r], lhs, (xt[0][:, dc], xt[1][:, dc]), dc == 0, dc == DC - 1)
                    mm.then_inc(done, 1)
                if c >= SHARED:
                    if c == SHARED:
                        if g.known and g.n == 0:
                            pe.wait_ge(consts, 5)
                        after(pe, parts_t_ready, g)
                        after(pe, hid_ready, g.plus(-1), CH1)
                    else:
                        pe.wait_ge(hid_ready, n)
                    pe.matmul(mix_ps[:], lhsT=sel_e[:, chunk_of(c)], rhs=parts_t[:], start=True, stop=True).then_inc(mix_done, 1)

            def down(g, c, last=False):
                if g.known and g.n < 0:
                    return
                n, r = g.n * CH1 + c, rows(c)
                if c == 0:
                    after(pe, x_ready, g.plus(-1), GT)
                pe.wait_ge(hs_ready, n + 1)
                for k in range(GT):
                    cols = slice(k * P, (k + 1) * P)
                    mm = product3(pe, down_ps[k // 2][:, (k % 2) * D:(k % 2 + 1) * D],
                                  [t[0:r, c % 2, cols] for t in hs], [t[0:r, chunk_of(c)] for t in wd],
                                  c == 0 and k % 2 == 0, c == CH1 - 1, skip_group_check=True)
                    if last and k == 1:
                        mm.then_inc(half_done, 1)
                mm.then_inc(chunk_done, 1)

            def group(g):
                for c in range(CH1):
                    hidden(g, c)
                    if c == 0:
                        down(g.plus(-1), CH1 - 1)
                    elif c > 1:
                        down(g, c - 2)
                    if c == CH1 - 1:
                        down(g, CH1 - 2)
                    if g.known and g.n == 0 and c == 0:
                        pe.wait_ge(wr_loaded, 16)
                        router(g)
                    if g.known and g.n == 0 and c == 2:
                        weights(g)
                    if g is LAST:
                        continue
                    if c == 3:
                        transposes(g.plus(1), 0)
                    if c == 5:
                        transposes(g.plus(1), 1)
                    if c == 7:
                        router(g.plus(1))
                    if c == 11:
                        weights(g.plus(1))

            first = Step(0, 0, 1)
            group(first)
            with pe.Fori(1, GROUPS - 1) as r:
                group(Step(r, 0, 1))
            group(LAST)
            down(LAST, CH1 - 1, last=True)

        @block.scalar
        def _(act):
            norm.scalar(act, LATE)

            def transposed(g, dc):
                after(act, turned.ready, g.plus(-1), DC)
                after(act, logit_done, g.plus(-1))
                turned.copy(act, g, dc, misc[:])

            def high(g):
                after(act, up_done, g.plus(-1), CH1)
                turned.high(act, g)

            def exponentials(g):
                after(act, r_steps, g, R_STEPS, 3)
                act.activation(expo[:], logit[:], ACT.Exp).then_inc(exp_ready, 1)

            def hidden_high(n, c, start):
                act.wait_ge(hid_ready, n + 1)
                if not start:
                    act.wait_ge(chunk_done, n - 1)
                act.activation(hs[0][0:rows(c), c % 2], hid[0:rows(c), c % 2], ACT.Copy).then_inc(hshi_ready, 1)

            def group(g):
                for c in range(CH1):
                    n, r = g.n * CH1 + c, rows(c)
                    zero = g.known and g.n == 0
                    if not (zero and c == 0):
                        hidden_high(n - 1, (c - 1) % CH1, zero and c < 3)
                    act.wait_ge(gate_done, n + 1)
                    multiplied(act, g, c - 2)
                    act.activation(sg[0:r, c % 2], g_ps[c % 2][0:r], ACT.Silu).then_inc(silu_ready, 1)
                    if zero and c == 0:
                        exponentials(g)
                    if g is LAST:
                        continue
                    if c == 4:
                        transposed(g.plus(1), 0)
                    if c == 6:
                        transposed(g.plus(1), 1)
                    if c == 9:
                        exponentials(g.plus(1))
                if g is not LAST:
                    high(g.plus(1))

            first = Step(0, 0, 1)
            group(first)
            with act.Fori(1, GROUPS - 1) as r:
                group(Step(r, 0, 1))
            group(LAST)
            hidden_high(GROUPS * CH1 - 1, CH1 - 1, False)

        @block.gpsimd
        def _(pool):
            pool.memset(earlier[:], 1.0)
            pool.memset(sel_a[:], 1.0).then_inc(consts, 1)
            pool.wait_ge(consts, 1)
            pool.affine_select(out=earlier[:], in_=earlier[:], compare_op=ALU.is_gt, fill=0.0, base=0,
                               pattern=[[1, E], [-1, E]], channel_multiplier=0).then_inc(consts, 1)
            for m in range(2):
                v = sel_a[:, m]
                op = pool.affine_select(out=v, in_=v, compare_op=ALU.is_ge, fill=0.0, base=DE * E * m,
                                        pattern=[[1, CHR * P]], channel_multiplier=-DE)
            op.then_inc(consts, 1)
            pool.wait_ge(consts, 3)
            for m in range(2):
                v = sel_a[:, m]
                op = pool.affine_select(out=v, in_=v, compare_op=ALU.is_ge, fill=0.0, base=DE - 1 - DE * E * m,
                                        pattern=[[-1, CHR * P]], channel_multiplier=DE)
            op.then_inc(consts, 1)
            def group(g):
                for c in range(CH1):
                    r = rows(c)
                    pool.wait_ge(hshi_ready, g.n * CH1 + (c + 1))
                    pool.tensor_tensor(hs[1][0:r, c % 2], hid[0:r, c % 2], raw(hs[0][0:r, c % 2]), ALU.subtract).then_inc(hs_ready, 1)

            with pool.Fori(0, GROUPS) as r:
                group(Step(r, 0, 1))

        @block.vector
        def _(dve):
            norm.vector(dve, LATE)

            def stage(g, k, op):
                op.then_inc(r_steps, 1)
                after(dve, r_steps, g, R_STEPS, k)

            def softmax_start(g):
                after(dve, logit_done, g)
                after(dve, exp_ready, g.plus(-1))
                stage(g, 1, dve.tensor_copy(logit[:].rearrange("p k e -> p (k e)"), misc[:, 0:GT * E]))
                stage(g, 2, dve.tensor_reduce(lmax[:], logit[:], AX_X, ALU.max))
                stage(g, 3, dve.tensor_tensor(logit[:], logit[:], lmax[:].unsqueeze(2).to_broadcast([P, GT, E]), ALU.subtract))

            def top2(g):
                after(dve, exp_ready, g)
                stage(g, 4, dve.tensor_reduce(esum[:], expo[:], AX_X, ALU.add))
                stage(g, 5, dve.reciprocal(lmax[:], esum[:]))
                stage(g, 6, dve.tensor_tensor(score[:], expo[:], lmax[:].unsqueeze(2).to_broadcast([P, GT, E]), ALU.mult))
                for k in range(GT):
                    other = score[:, k].unsqueeze(1).to_broadcast([P, E, E])
                    own = score[:, k].unsqueeze(2).to_broadcast([P, E, E])
                    dve.tensor_tensor(above[:, k], other, own, ALU.is_gt)
                    op = dve.tensor_tensor(same[:, k], other, own, ALU.is_equal)
                stage(g, 7, op)
                for k in range(GT):
                    op = dve.tensor_tensor(same[:, k], same[:, k], earlier[:], ALU.mult)
                stage(g, 8, op)
                flat = "p k a b -> p (k a b)"
                stage(g, 9, dve.tensor_tensor(above[:].rearrange(flat), above[:].rearrange(flat), same[:].rearrange(flat), ALU.add))
                stage(g, 10, dve.tensor_reduce(rank[:].rearrange("p k e -> p (k e)"), above[:].rearrange("p k a b -> p (k a) b"), AX_X, ALU.add))
                stage(g, 11, dve.scalar_tensor_tensor(weight[:], rank[:], 2.0, score[:], ALU.is_lt, ALU.mult))
                after(dve, parts_done, g.plus(-1))
                dve.tensor_copy(parts[:, :, 0], weight[:]).then_inc(parts_ready, 1)
                after(dve, parts_ready, g, 2, 1)
                dve.tensor_tensor(parts[:, :, 1], weight[:], raw(parts[:, :, 0]), ALU.subtract).then_inc(parts_ready, 1)

            def parts_turned(g):
                after(dve, parts_done, g)
                after(dve, mix_done, g.plus(-1), CHR)
                dve.tensor_copy(parts_t[:], misc[0:2 * E, :]).then_inc(parts_t_ready, 1)

            def chunk(g, c):
                n, r, slot = g.n * CH1 + c, rows(c), c % 2
                zero = g.known and g.n == 0 and c < 2
                routed = c >= SHARED
                dve.wait_ge(silu_ready, n + 1)
                dve.wait_ge(up_done, n + 1)
                if not zero:
                    dve.wait_ge(hs_ready, n - 1)
                out = prod if routed else hid
                done = prod_ready if routed else hid_ready
                dve.tensor_tensor(out[0:r, slot], sg[0:r, slot], u_ps[slot][0:r], ALU.mult).then_inc(done, 1)
                if routed:
                    multiplied(dve, g, c)
                    dve.wait_ge(mix_done, g.n * CHR + (c - SHARED + 1))
                    dve.tensor_tensor(hid[:, slot], prod[:, slot], mix_ps[:], ALU.mult).then_inc(hid_ready, 1)

            def residual(g, last=False):
                if not last:
                    after(dve, chunk_done, g, CH1)
                for k in range(GT):
                    t = g.n * GT + k
                    if last and k == 0:
                        dve.wait_ge(half_done, 1)
                    if last and k == 2:
                        after(dve, chunk_done, g, CH1)
                    dve.scalar_tensor_tensor(at(x_all, t), down_ps[k // 2][:, (k % 2) * D:(k % 2 + 1) * D], gates[:, 3:4],
                                             at(x_all, t), ALU.mult, ALU.add).then_inc(x_ready, 1)

            def group(g):
                for c in range(CH1):
                    if c == CH1 - 1 and g is not LAST:
                        turned.low(dve, g.plus(1))
                    chunk(g, c)
                    if g.known and g.n == 0 and c == 0:
                        dve.wait_ge(consts, 2)
                        top2(g)
                    if g.known and g.n == 0 and c == 1:
                        dve.wait_ge(consts, 4)
                        dve.tensor_tensor(sel_e[:].rearrange("k c p -> k (c p)"), sel_a[:, 0], sel_a[:, 1], ALU.add).then_inc(consts, 1)
                    if g.known and g.n == 0 and c == 2:
                        parts_turned(g)
                    if c == 1:
                        if not (g.known and g.n == 0):
                            residual(g.plus(-1))
                    if g is LAST:
                        continue
                    if c == 1:
                        after(dve, turned.done, g, 2)
                        normalised(dve, norm, xn, x_all, g.plus(1), turned.xn_ready)
                    if c == 8:
                        softmax_start(g.plus(1))
                    if c == 10:
                        top2(g.plus(1))
                if g is not LAST:
                    parts_turned(g.plus(1))

            first = Step(0, 0, 1)
            softmax_start(first)
            group(first)
            with dve.Fori(1, GROUPS - 1) as r:
                group(Step(r, 0, 1))
            group(LAST)
            residual(LAST, last=True)
            dve.wait_ge(x_ready, TILES)


def flamingo(nc, a, out):
    d = {
        "x": a["x"].rearrange("(t b) s n -> t (b s) n", b=2),
        "ctx": a["ctx_2048"].rearrange("(t b) s n -> t (b s) n", b=2),
        "wq": a["L0_xattn_W_q"], "wk": a["L0_xattn_W_k"], "wv": a["L0_xattn_W_v"], "wo": a["L0_xattn_W_o"],
        "g_xattn": a["g_xattn"].partition_broadcast(P), "g_ffn": a["g_ffn"].partition_broadcast(P),
        "gamma": a["L1_xattn_gamma"].partition_broadcast(P),
        "kop": nc.dram_tensor("kop_rows", (TILES, UNITS, QROWS, D), F32).ap(),
        "qop": nc.dram_tensor("qop_rows", (2, UNITS, QROWS, D), F32).ap(),
        "out": out.rearrange("(t b) s n -> t (b s) n", b=2),
        "a": a,
    }
    with ExitStack() as ctx:
        def sb(name, shape, dt):
            return ctx.enter_context(nc.sbuf_tensor(name, shape, dt))

        def sem(name):
            return ctx.enter_context(nc.semaphore(name))

        keep = {
            "x_all": sb("x_all", [P, XT, D], F32),
            "norm": Norm(sb, sem),
            "ident": sb("ident", [P, P], F32),
            "gates": sb("gates", [P, 4], F32),
            "sel_out": sb("sel_out", [P, 32], F32),
            "sel_den": sb("sel_den", [P, 32], F32),
        }
        keep["q"] = QueryParts(sb, sem)
        keep["operands"] = Operands(sb, sem)
        with ExitStack() as early:
            keep["w0_raw"] = early.enter_context(nc.sbuf_tensor("w0_raw", [P, 2, DC, I0], F32))
            keep["wd0_raw"] = early.enter_context(nc.sbuf_tensor("wd0_raw", [P, QUAD0, 4, D], F32))
            keep["w0"] = [early.enter_context(nc.sbuf_tensor(n, [P, 2, DC, 4, I0 // 4], F32R)) for n in ("w0_hi", "w0_lo")]
            keep["w0_loaded"] = [sem("w0_loaded0"), sem("w0_loaded1")]
            keep["wd0_loaded"] = sem("wd0_loaded")
            keep["f0_xn"] = early.enter_context(nc.sbuf_tensor("f0_xn", [P, GT, D], F32))
            keep["f0_xn_ready"] = sem("f0_xn_ready")
            attention0(nc, sem, keep, d)
            feed_forward0(nc, sem, keep, d)
        keep["w1"] = [sb(n, [P, 2, DC, I1], F32R) for n in ("w1_hi", "w1_lo")]
        keep["turned"] = Turned(sb, sem)
        keep["wd1"] = [sb(n, [P, CH1, D], F32R) for n in ("wd1_hi", "wd1_lo")]
        attention1(nc, sem, keep, d)
        feed_forward1(nc, sem, keep, d)


_INS = ['x', 'ctx_2048', 'g_xattn', 'g_ffn', 'L0_xattn_W_q', 'L0_xattn_W_k', 'L0_xattn_W_v', 'L0_xattn_W_o',
        'L0_ffn_w_gate', 'L0_ffn_w_up', 'L0_ffn_w_down', 'L1_xattn_gamma', 'L1_ffn_W_router', 'L1_ffn_We_gate',
        'L1_ffn_We_up', 'L1_ffn_We_down', 'L1_ffn_Ws_gate', 'L1_ffn_Ws_up', 'L1_ffn_Ws_down']


def kernel(**inputs):
    import numpy as _np
    import concourse.bacc as _bacc
    from concourse import mybir as _mybir
    from concourse.bass_utils import run_bass_kernel_spmd as _run

    nc = _bacc.Bacc("TRN2", target_bir_lowering=False, num_devices=1)
    arrays, args = {}, {}
    for name in _INS:
        a = _np.ascontiguousarray(inputs[name])
        if a.ndim == 0:
            a = a.reshape(1)
        arrays[f"in_{name}"] = a
        args[name] = nc.dram_tensor(f"in_{name}", a.shape, _mybir.dt.from_np(a.dtype), kind="ExternalInput").ap()
    out = nc.dram_tensor("out_x", (BATCH, SEQ, D), F32, kind="ExternalOutput").ap()
    flamingo(nc, args, out)
    r = _run(nc, [arrays], core_ids=[0])
    return r.results[0]["out_x"]
```
